# Optimizing a Trainium2 kernel written in Bass

```python
import numpy as np
import jax
import jax.numpy as jnp

def _softmax(x, axis=-1):
    return jax.nn.softmax(x, axis=axis)

def _gelu(x):
    return jax.nn.gelu(x, approximate=True)

def _silu(x):
    return jax.nn.silu(x)

def _sigmoid(x):
    return jax.nn.sigmoid(x)

def _layernorm(x, axis=-1, eps=1e-05):
    m = jnp.mean(x, axis=axis, keepdims=True)
    v = jnp.var(x, axis=axis, keepdims=True)
    return (x - m) / jnp.sqrt(v + eps)

def _scatter_add(tgt, idx, src, axis=0):
    return tgt.at[idx].add(src)

def _segment_sum(src, seg, n):
    return jax.ops.segment_sum(src, seg, n)
kernel_name = 'mk_conv_seq_d2_conv_nchw192_r4_d9a05a'

def setup_inputs(seed: int=0):
    np.random.seed(seed)
    _w = jnp.asarray

    def _rec_inputs():
        import jax
        import jax.numpy as jnp
        _gk = jax.random.key(seed)
        x = -1.8e-05 + 0.9999 * jax.random.normal(jax.random.fold_in(_gk, 1), (8, 48, 48, 48), jnp.float32)
        return x
    x = _rec_inputs()

    def _L0_conv_setup():
        import jax, jax.numpy as jnp
        import numpy as np
        from jax import lax
        WH = WW = 8
        HEADS = 4

        def _rel_index(Wh, Ww):
            coords = np.stack(np.meshgrid(np.arange(Wh), np.arange(Ww), indexing='ij')).reshape(2, -1)
            rel = coords[:, :, None] - coords[:, None, :]
            rel[0] += Wh - 1
            rel[1] += Ww - 1
            return jnp.asarray(rel[0] * (2 * Ww - 1) + rel[1], dtype=jnp.int32)
        REL_IDX = _rel_index(WH, WW)

        def _rep_pad1_detach(x):
            xp = jnp.pad(lax.stop_gradient(x), ((0, 0), (0, 0), (1, 1), (1, 1)), mode='edge')
            return xp.at[:, :, 1:-1, 1:-1].set(x)
        key = jax.random.key(seed)
        ks = jax.random.split(key, 6)
        B, C, H, W = (8, 48, 48, 48)
        mid = 2 * C
        s = 0.05
        return {'x': jax.random.normal(ks[0], (B, C, H, W), jnp.float32), 'qkv_w': jax.random.normal(ks[1], (3 * C, C), jnp.float32) * s, 'qkv_b': jnp.zeros((3 * C,), jnp.float32), 'proj_w': jax.random.normal(ks[2], (C, C), jnp.float32) * s, 'proj_b': jnp.zeros((C,), jnp.float32), 'bias_table': jax.random.normal(ks[3], ((2 * WH - 1) * (2 * WW - 1),), jnp.float32) * s, 'w1_w': jax.random.normal(ks[4], (mid, C), jnp.float32) * s, 'w1_b': jnp.zeros((mid,), jnp.float32), 'w2_w': jax.random.normal(ks[5], (C, mid // 2, 3, 3), jnp.float32) * s, 'w2_b': jnp.zeros((C,), jnp.float32)}
    _L0_conv_all = _L0_conv_setup()
    _L0_conv_in = {k: v for k, v in _L0_conv_all.items() if k in ('qkv_w', 'qkv_b', 'proj_w', 'proj_b', 'bias_table', 'w1_w', 'w1_b', 'w2_w', 'w2_b')}
    del _L0_conv_all

    def _L1_conv_setup():
        import jax, jax.numpy as jnp
        import numpy as np
        DIM = 48
        HEADS = 6
        H = 16
        W = 16
        B = 16
        HID = int(DIM * 4.0)

        def make_rope(Hh, Ww, c):
            k_max = c // 4
            theta = 1.0 / 10000.0 ** (np.arange(k_max) / k_max)
            hi = np.arange(Hh)[:, None, None] * theta
            wi = np.arange(Ww)[None, :, None] * theta
            angles = np.concatenate([np.broadcast_to(hi, (Hh, Ww, k_max)), np.broadcast_to(wi, (Hh, Ww, k_max))], axis=-1)
            return (jnp.asarray(np.cos(angles), jnp.float32), jnp.asarray(np.sin(angles), jnp.float32))

        def rope_apply(x, cos, sin):
            b, Hh, Ww, c = x.shape
            xr = x.reshape(b, Hh, Ww, c // 2, 2)
            re, im = (xr[..., 0], xr[..., 1])
            out = jnp.stack([re * cos - im * sin, re * sin + im * cos], axis=-1)
            return out.reshape(b, Hh, Ww, c)

        def dwconv(x, w, b):
            C = x.shape[1]
            y = jax.lax.conv_general_dilated(x, w, (1, 1), 'SAME', dimension_numbers=('NCHW', 'OIHW', 'NCHW'), feature_group_count=C)
            return y + b[None, :, None, None]

        def conv1x1(x, w, b):
            return jnp.einsum('bchw,oc->bohw', x, w) + b[None, :, None, None]

        def ln2d(x, w, b):
            mu = x.mean(axis=1, keepdims=True)
            var = x.var(axis=1, keepdims=True)
            xn = (x - mu) / jnp.sqrt(var + 1e-05)
            return xn * w[None, :, None, None] + b[None, :, None, None]
        key = jax.random.key(seed)
        ks = jax.random.split(key, 32)
        s = 0.02

        def p(i, shape):
            return jax.random.normal(ks[i], shape, jnp.float32) * s
        return {'x': jax.random.normal(ks[0], (B, DIM, H, W), jnp.float32), 'cpe1_w': p(1, (DIM, 1, 3, 3)), 'cpe1_b': p(2, (DIM,)), 'norm1_w': jnp.ones((DIM,), jnp.float32), 'norm1_b': jnp.zeros((DIM,), jnp.float32), 'act_proj_w': p(3, (DIM, DIM)), 'act_proj_b': p(4, (DIM,)), 'in_proj_w': p(5, (DIM, DIM)), 'in_proj_b': p(6, (DIM,)), 'dwc_w': p(7, (DIM, 1, 3, 3)), 'dwc_b': p(8, (DIM,)), 'qk_w': p(9, (2 * DIM, DIM)), 'qk_b': p(10, (2 * DIM,)), 'lepe_w': p(11, (DIM, 1, 3, 3)), 'lepe_b': p(12, (DIM,)), 'out_proj_w': p(13, (DIM, DIM)), 'out_proj_b': p(14, (DIM,)), 'cpe2_w': p(15, (DIM, 1, 3, 3)), 'cpe2_b': p(16, (DIM,)), 'norm2_w': jnp.ones((DIM,), jnp.float32), 'norm2_b': jnp.zeros((DIM,), jnp.float32), 'fc1_w': p(17, (HID, DIM)), 'fc1_b': p(18, (HID,)), 'fc2_w': p(19, (DIM, HID)), 'fc2_b': p(20, (DIM,))}
    _L1_conv_all = _L1_conv_setup()
    _L1_conv_in = {k: v for k, v in _L1_conv_all.items() if k in ('cpe1_w', 'cpe1_b', 'norm1_w', 'norm1_b', 'act_proj_w', 'act_proj_b', 'in_proj_w', 'in_proj_b', 'dwc_w', 'dwc_b', 'qk_w', 'qk_b', 'lepe_w', 'lepe_b', 'out_proj_w', 'out_proj_b', 'cpe2_w', 'cpe2_b', 'norm2_w', 'norm2_b', 'fc1_w', 'fc1_b', 'fc2_w', 'fc2_b')}
    del _L1_conv_all
    return {'x': x, 'L0_conv_qkv_w': _L0_conv_in['qkv_w'], 'L0_conv_qkv_b': _L0_conv_in['qkv_b'], 'L0_conv_proj_w': _L0_conv_in['proj_w'], 'L0_conv_proj_b': _L0_conv_in['proj_b'], 'L0_conv_bias_table': _L0_conv_in['bias_table'], 'L0_conv_w1_w': _L0_conv_in['w1_w'], 'L0_conv_w1_b': _L0_conv_in['w1_b'], 'L0_conv_w2_w': _L0_conv_in['w2_w'], 'L0_conv_w2_b': _L0_conv_in['w2_b'], 'L1_conv_cpe1_w': _L1_conv_in['cpe1_w'], 'L1_conv_cpe1_b': _L1_conv_in['cpe1_b'], 'L1_conv_norm1_w': _L1_conv_in['norm1_w'], 'L1_conv_norm1_b': _L1_conv_in['norm1_b'], 'L1_conv_act_proj_w': _L1_conv_in['act_proj_w'], 'L1_conv_act_proj_b': _L1_conv_in['act_proj_b'], 'L1_conv_in_proj_w': _L1_conv_in['in_proj_w'], 'L1_conv_in_proj_b': _L1_conv_in['in_proj_b'], 'L1_conv_dwc_w': _L1_conv_in['dwc_w'], 'L1_conv_dwc_b': _L1_conv_in['dwc_b'], 'L1_conv_qk_w': _L1_conv_in['qk_w'], 'L1_conv_qk_b': _L1_conv_in['qk_b'], 'L1_conv_lepe_w': _L1_conv_in['lepe_w'], 'L1_conv_lepe_b': _L1_conv_in['lepe_b'], 'L1_conv_out_proj_w': _L1_conv_in['out_proj_w'], 'L1_conv_out_proj_b': _L1_conv_in['out_proj_b'], 'L1_conv_cpe2_w': _L1_conv_in['cpe2_w'], 'L1_conv_cpe2_b': _L1_conv_in['cpe2_b'], 'L1_conv_norm2_w': _L1_conv_in['norm2_w'], 'L1_conv_norm2_b': _L1_conv_in['norm2_b'], 'L1_conv_fc1_w': _L1_conv_in['fc1_w'], 'L1_conv_fc1_b': _L1_conv_in['fc1_b'], 'L1_conv_fc2_w': _L1_conv_in['fc2_w'], 'L1_conv_fc2_b': _L1_conv_in['fc2_b']}

def reference(x, L0_conv_qkv_w, L0_conv_qkv_b, L0_conv_proj_w, L0_conv_proj_b, L0_conv_bias_table, L0_conv_w1_w, L0_conv_w1_b, L0_conv_w2_w, L0_conv_w2_b, L1_conv_cpe1_w, L1_conv_cpe1_b, L1_conv_norm1_w, L1_conv_norm1_b, L1_conv_act_proj_w, L1_conv_act_proj_b, L1_conv_in_proj_w, L1_conv_in_proj_b, L1_conv_dwc_w, L1_conv_dwc_b, L1_conv_qk_w, L1_conv_qk_b, L1_conv_lepe_w, L1_conv_lepe_b, L1_conv_out_proj_w, L1_conv_out_proj_b, L1_conv_cpe2_w, L1_conv_cpe2_b, L1_conv_norm2_w, L1_conv_norm2_b, L1_conv_fc1_w, L1_conv_fc1_b, L1_conv_fc2_w, L1_conv_fc2_b):
    import jax
    import jax.numpy as jnp

    def _L0_conv_ref(x, qkv_w, qkv_b, proj_w, proj_b, bias_table, w1_w, w1_b, w2_w, w2_b):
        import jax, jax.numpy as jnp
        import numpy as np
        from jax import lax
        WH = WW = 8
        HEADS = 4

        def _rel_index(Wh, Ww):
            coords = np.stack(np.meshgrid(np.arange(Wh), np.arange(Ww), indexing='ij')).reshape(2, -1)
            rel = coords[:, :, None] - coords[:, None, :]
            rel[0] += Wh - 1
            rel[1] += Ww - 1
            return jnp.asarray(rel[0] * (2 * Ww - 1) + rel[1], dtype=jnp.int32)
        REL_IDX = _rel_index(WH, WW)

        def _rep_pad1_detach(x):
            xp = jnp.pad(lax.stop_gradient(x), ((0, 0), (0, 0), (1, 1), (1, 1)), mode='edge')
            return xp.at[:, :, 1:-1, 1:-1].set(x)
        B, C, H, W = x.shape
        nh, nw = (H // WH, W // WW)
        N = WH * WW
        d = C // HEADS
        xw = x.reshape(B, C, nh, WH, nw, WW).transpose(0, 2, 4, 3, 5, 1).reshape(-1, N, C)
        qkv = xw @ qkv_w.T + qkv_b
        qkv = qkv.reshape(-1, N, 3, HEADS, d).transpose(2, 0, 3, 1, 4)
        q, k, v = (qkv[0], qkv[1], qkv[2])
        bias = bias_table[REL_IDX]
        scores = jnp.einsum('bhnd,bhmd->bhnm', q, k) / jnp.sqrt(jnp.asarray(d, x.dtype))
        attn = jax.nn.softmax(scores + bias, axis=-1)
        out = jnp.einsum('bhnm,bhmd->bhnd', attn, v)
        out = out.transpose(0, 2, 1, 3).reshape(-1, N, C) @ proj_w.T + proj_b
        x1 = out.reshape(B, nh, nw, WH, WW, C).transpose(0, 5, 1, 3, 2, 4).reshape(B, C, H, W)
        x = x + x1
        h = jnp.einsum('bchw,oc->bohw', x, w1_w) + w1_b[:, None, None]
        a, b = jnp.split(h, 2, axis=1)
        g = a * jax.nn.sigmoid(b)
        g = _rep_pad1_detach(g)
        y = lax.conv_general_dilated(g, w2_w, (1, 1), 'VALID', dimension_numbers=('NCHW', 'OIHW', 'NCHW'))
        y = y + w2_b[:, None, None]
        y = jnp.where(y >= 0, y, 0.2 * y)
        return x + y

    def _L1_conv_ref(x, cpe1_w, cpe1_b, norm1_w, norm1_b, act_proj_w, act_proj_b, in_proj_w, in_proj_b, dwc_w, dwc_b, qk_w, qk_b, lepe_w, lepe_b, out_proj_w, out_proj_b, cpe2_w, cpe2_b, norm2_w, norm2_b, fc1_w, fc1_b, fc2_w, fc2_b):
        import jax, jax.numpy as jnp
        import numpy as np
        DIM = 48
        HEADS = 6
        H = 16
        W = 16
        B = 16
        HID = int(DIM * 4.0)

        def make_rope(Hh, Ww, c):
            k_max = c // 4
            theta = 1.0 / 10000.0 ** (np.arange(k_max) / k_max)
            hi = np.arange(Hh)[:, None, None] * theta
            wi = np.arange(Ww)[None, :, None] * theta
            angles = np.concatenate([np.broadcast_to(hi, (Hh, Ww, k_max)), np.broadcast_to(wi, (Hh, Ww, k_max))], axis=-1)
            return (jnp.asarray(np.cos(angles), jnp.float32), jnp.asarray(np.sin(angles), jnp.float32))

        def rope_apply(x, cos, sin):
            b, Hh, Ww, c = x.shape
            xr = x.reshape(b, Hh, Ww, c // 2, 2)
            re, im = (xr[..., 0], xr[..., 1])
            out = jnp.stack([re * cos - im * sin, re * sin + im * cos], axis=-1)
            return out.reshape(b, Hh, Ww, c)

        def dwconv(x, w, b):
            C = x.shape[1]
            y = jax.lax.conv_general_dilated(x, w, (1, 1), 'SAME', dimension_numbers=('NCHW', 'OIHW', 'NCHW'), feature_group_count=C)
            return y + b[None, :, None, None]

        def conv1x1(x, w, b):
            return jnp.einsum('bchw,oc->bohw', x, w) + b[None, :, None, None]

        def ln2d(x, w, b):
            mu = x.mean(axis=1, keepdims=True)
            var = x.var(axis=1, keepdims=True)
            xn = (x - mu) / jnp.sqrt(var + 1e-05)
            return xn * w[None, :, None, None] + b[None, :, None, None]
        b, c, Hh, Ww = x.shape
        n = Hh * Ww
        d = c // HEADS
        cos, sin = make_rope(Hh, Ww, c)
        x = x + dwconv(x, cpe1_w, cpe1_b)
        y = ln2d(x, norm1_w, norm1_b)
        act_res = jax.nn.silu(conv1x1(y, act_proj_w, act_proj_b))
        y = conv1x1(y, in_proj_w, in_proj_b)
        t = jax.nn.silu(dwconv(y, dwc_w, dwc_b)).transpose(0, 2, 3, 1).reshape(b, n, c)
        qk = t @ qk_w.T + qk_b
        q = jax.nn.elu(qk[..., :c]) + 1.0
        k = jax.nn.elu(qk[..., c:]) + 1.0
        v = t
        q_rope = rope_apply(q.reshape(b, Hh, Ww, c), cos, sin).reshape(b, n, HEADS, d).transpose(0, 2, 1, 3)
        k_rope = rope_apply(k.reshape(b, Hh, Ww, c), cos, sin).reshape(b, n, HEADS, d).transpose(0, 2, 1, 3)
        qh = q.reshape(b, n, HEADS, d).transpose(0, 2, 1, 3)
        kh = k.reshape(b, n, HEADS, d).transpose(0, 2, 1, 3)
        vh = v.reshape(b, n, HEADS, d).transpose(0, 2, 1, 3)
        kmean = kh.mean(axis=2, keepdims=True)
        z = 1.0 / (jnp.einsum('bhnd,bhmd->bhnm', qh, kmean) + 1e-06)
        scale = n ** (-0.5)
        kv = jnp.einsum('bhnd,bhne->bhde', k_rope * scale, vh * scale)
        attn = jnp.einsum('bhnd,bhde->bhne', q_rope, kv) * z
        attn = attn.transpose(0, 2, 1, 3).reshape(b, n, c)
        v_img = vh.transpose(0, 2, 1, 3).reshape(b, Hh, Ww, c).transpose(0, 3, 1, 2)
        lepe = dwconv(v_img, lepe_w, lepe_b).transpose(0, 2, 3, 1).reshape(b, n, c)
        attn = attn + lepe
        y = attn.transpose(0, 2, 1).reshape(b, c, Hh, Ww)
        y = conv1x1(y * act_res, out_proj_w, out_proj_b)
        x = x + y
        x = x + dwconv(x, cpe2_w, cpe2_b)
        y = ln2d(x, norm2_w, norm2_b)
        y = conv1x1(y, fc1_w, fc1_b)
        y = jax.nn.gelu(y, approximate=False)
        y = conv1x1(y, fc2_w, fc2_b)
        return x + y

    def _gn(v, G=32, eps=1e-05):
        B_, C_, H_, W_ = v.shape
        g = v.reshape(B_, G, C_ // G, H_, W_)
        m = jnp.mean(g, axis=(2, 3, 4), keepdims=True)
        s = jnp.var(g, axis=(2, 3, 4), keepdims=True)
        return ((g - m) / jnp.sqrt(s + eps)).reshape(v.shape)

    def _ln_c(v, eps=1e-06):
        m = jnp.mean(v, axis=1, keepdims=True)
        s = jnp.var(v, axis=1, keepdims=True)
        return (v - m) / jnp.sqrt(s + eps)

    def _ln_t(v, eps=1e-05):
        m = jnp.mean(v, axis=-1, keepdims=True)
        s = jnp.var(v, axis=-1, keepdims=True)
        return (v - m) / jnp.sqrt(s + eps)

    def _to_tokens(v):
        B_, C_, H_, W_ = v.shape
        return v.reshape(B_, C_, H_ * W_).transpose(0, 2, 1)

    def _from_tokens(t, like):
        B_, C_, H_, W_ = like.shape
        return t.transpose(0, 2, 1).reshape(B_, C_, H_, W_)
    x = _L0_conv_ref(x, L0_conv_qkv_w, L0_conv_qkv_b, L0_conv_proj_w, L0_conv_proj_b, L0_conv_bias_table, L0_conv_w1_w, L0_conv_w1_b, L0_conv_w2_w, L0_conv_w2_b)
    x = _L1_conv_ref(x, L1_conv_cpe1_w, L1_conv_cpe1_b, L1_conv_norm1_w, L1_conv_norm1_b, L1_conv_act_proj_w, L1_conv_act_proj_b, L1_conv_in_proj_w, L1_conv_in_proj_b, L1_conv_dwc_w, L1_conv_dwc_b, L1_conv_qk_w, L1_conv_qk_b, L1_conv_lepe_w, L1_conv_lepe_b, L1_conv_out_proj_w, L1_conv_out_proj_b, L1_conv_cpe2_w, L1_conv_cpe2_b, L1_conv_norm2_w, L1_conv_norm2_b, L1_conv_fc1_w, L1_conv_fc1_b, L1_conv_fc2_w, L1_conv_fc2_b)
    return x

_drawn_inputs = setup_inputs


def setup_inputs(seed=0):
    import zlib

    import numpy as np

    out = dict(_drawn_inputs(seed))
    spreads = {'L0_conv_qkv_b': (0.0, 0.1),
     'L0_conv_proj_b': (0.0, 0.1),
     'L0_conv_w1_b': (0.0, 0.1),
     'L0_conv_w2_b': (0.0, 0.1),
     'L1_conv_norm1_w': (1.0, 0.6),
     'L1_conv_norm1_b': (0.0, 0.8),
     'L1_conv_norm2_w': (1.0, 0.6),
     'L1_conv_norm2_b': (0.0, 0.8)}
    factors = {'L0_conv_qkv_w': 3.637,
     'L0_conv_bias_table': 8.0,
     'L1_conv_cpe1_b': 3.36,
     'L1_conv_act_proj_w': 8.0,
     'L1_conv_act_proj_b': 8.0,
     'L1_conv_in_proj_w': 8.0,
     'L1_conv_in_proj_b': 8.0,
     'L1_conv_dwc_w': 8.0,
     'L1_conv_dwc_b': 8.0,
     'L1_conv_qk_w': 26.566,
     'L1_conv_qk_b': 64.0,
     'L1_conv_lepe_w': 8.0,
     'L1_conv_lepe_b': 8.0,
     'L1_conv_out_proj_w': 8.0,
     'L1_conv_out_proj_b': 2.864,
     'L1_conv_fc1_w': 2.93,
     'L1_conv_fc1_b': 8.0,
     'L1_conv_fc2_w': 2.964,
     'L1_conv_fc2_b': 3.45,
     'L1_conv_cpe2_b': 3.126}
    for name, (base, spread) in spreads.items():
        noise = np.random.default_rng([zlib.crc32(name.encode()), seed]).standard_normal(out[name].shape)
        drawn = base * np.exp(spread * noise) if base else spread * noise
        out[name] = jnp.asarray(drawn.astype(out[name].dtype))
    for name, factor in factors.items():
        out[name] = (out[name] * factor).astype(out[name].dtype)
    return out
```

```python
from contextlib import ExitStack

import numpy as np

import concourse.bass as bass
from concourse import mybir

F32 = mybir.dt.float32
ALU = mybir.AluOpType
ACT = mybir.ActivationFunctionType
AX = mybir.AxisListType

B, C, H, W = 8, 48, 48, 48
PAIRS = B // 2
R = 2 * C
PX = H * W
WIN = 8
TOK = WIN * WIN
HEADS0, D0 = 4, C // 4
HEADS1, D1 = 6, C // 6
STRIPS = H // WIN
SPX = WIN * W
NW = W // WIN
CH = 3
CROWS = H // CH
CPX = CROWS * W
TT = 2 * W + 2
TILES = H // 2
CT_ = TILES // CH
HID = 4 * C
FG = HID // 64
PADW = W + 2
BANK = 512
NSLOT = 4
VCOL = D0 + 1

SQ = ["q", "k", "v", "w1a", "w1b", "act", "inp", "lq", "lk", "out"]
CN = ["center", "mean", "swap", "swapT", "headmask"]
VEC = (["bq", "bk", "bw1a", "bw1b", "bw2", "cpe1_b", "n1w", "n1b", "act_b", "inp_b", "dwc_b", "lq_b",
        "lepe_b", "out_b", "cpe2_b", "n2w", "n2b", "fc2_b", "proj_b", "bv"]
       + [f"{n}{t}" for n in ("cpe1_", "dwc_", "lepe_", "cpe2_") for t in range(9)])
VI = {n: j for j, n in enumerate(VEC)}
CONVS = ["cpe1_", "dwc_", "lepe_", "cpe2_"]
PE_CHUNKS = (1,)
DVE_CHUNKS = (0, 2)


def attention_schedule():
    order = []
    for t in range(-1, STRIPS + 2):
        for job, s in (("qk", t + 1), ("tr0", t), ("ot", t - 1), ("v", t + 1), ("tr1", t), ("sc0", t + 1),
                       ("pj", t - 1), ("av", t), ("sc1", t + 1), ("w1", t - 2)):
            if 0 <= s < STRIPS:
                order.append((job, s))
    return order


ATT = attention_schedule()


def job_order():
    jobs = list(ATT)
    jobs += [("cv", d) for d in range(CH)]
    jobs += [("cp1", d) for d in PE_CHUNKS]
    jobs += [("xc", d) for d in range(CH)] + [("va", d) for d in range(CH)]
    jobs += [(j, d) for d in range(CH) for j in ("ip", "ac")]
    jobs += [("dc", d) for d in PE_CHUNKS]
    jobs += [(j, d) for d in range(CH) for j in ("kt", "q", "vt")]
    jobs += [("ks", 0), ("kv", 0), ("kk", 0)]
    jobs += [("dn", d) for d in range(CH)] + [("le", d) for d in PE_CHUNKS]
    jobs += [("at", d) for d in range(CH)] + [("op", d) for d in range(CH)]
    jobs += [("cp2", d) for d in PE_CHUNKS]
    jobs += [("xc2", d) for d in range(CH)] + [("va2", d) for d in range(CH)]
    for d in range(CH):
        jobs += [(f"f1_{m}", d) for m in range(FG)] + [("f2", d)]
    return jobs


JOBS = job_order()
NTH = {j: n for n, j in enumerate(JOBS)}
USES = [len(range(k, len(JOBS), NSLOT)) for k in range(NSLOT)]
LOOP = True


def build(nc, x, wsq, wproj, w2, wfc1, wfc2, vec, fc1b, kbrow, bias, const, ident, masks, rope_c, rope_th,
          rope_tw, out):
    ctx = ExitStack()
    with ctx:
        def sb(name, shape):
            return ctx.enter_context(nc.sbuf_tensor(name, shape, F32))

        def sem(name):
            return ctx.enter_context(nc.semaphore(name))

        wsq_sb = sb("wsq_sb", [R, len(SQ) * R])
        wproj_sb = sb("wproj_sb", [R, 4 * R])
        w2_sb = sb("w2_sb", [R, 9 * R])
        wfc1_sb = sb("wfc1_sb", [R, FG * 128])
        wfc2_sb = sb("wfc2_sb", [128, FG * R])
        vec_sb = sb("vec_sb", [R, len(VEC)])
        fc1b_sb = sb("fc1b_sb", [128, FG])
        kbrow_sb = sb("kbrow_sb", [TT, R])
        bias_sb = sb("bias_sb", [128, TOK])
        const_sb = sb("const_sb", [R, len(CN) * R])
        ident_sb = sb("ident_sb", [128, 128])
        masks_sb = sb("masks_sb", [128, 2 + HEADS0 + 4])
        rope_c_sb = sb("rope_c_sb", [R, 2 * PX])
        rope_th_sb = sb("rope_th_sb", [TT, 2 * TILES * (C // 2)])
        rope_tw_sb = sb("rope_tw_sb", [TT, 2 * (C // 2)])
        diag = [sb(n + "diag", [R, 9 * R]) for n in CONVS]
        kbias = sb("kbias", [R, HEADS0])
        small = sb("small", [R, 8])
        fc1b2 = sb("fc1b2", [128, FG])

        def wq(n):
            j = SQ.index(n)
            return wsq_sb[:, j * R:(j + 1) * R]

        def cn(n):
            j = CN.index(n)
            return const_sb[:, j * R:(j + 1) * R]

        def v(n):
            return vec_sb[:, VI[n]:VI[n] + 1]

        img_mask = [masks_sb[0:R, j:j + 1] for j in range(2)]
        head_mask = [masks_sb[0:R, 2 + h:3 + h] for h in range(HEADS0)]
        ones2 = masks_sb[0:TT, 2 + HEADS0:4 + HEADS0]
        eps_ln = masks_sb[0:R, 4 + HEADS0:5 + HEADS0]
        eps_z = masks_sb[0:R, 5 + HEADS0:6 + HEADS0]
        half_bw1b, proj_b2, act_b2, inp_b2 = (small[:, j:j + 1] for j in range(4))

        XR = sb("XR", [R, PX])
        X1t = sb("X1", [128, PX])
        X1 = X1t[0:R, :]
        VT = X1t[0:TT, :].rearrange("p (t c) -> p t c", c=R)
        G = sb("G", [128, PADW * PADW])
        Gp = G[0:R, :].rearrange("p (y x) -> p y x", x=PADW)
        Q = G[0:R, 0:PX]
        HB = G[:, 0:FG * CPX].rearrange("p (m n) -> p m n", m=FG)
        ZP = sb("ZP", [R, PADW, PADW])
        TP = sb("TP", [R, PADW, PADW])
        X3 = sb("X3", [R, PX])
        XC = sb("XC", [R, PX])
        LVt = sb("LV", [128, PX])
        LV = LVt[0:R, :]
        AR = sb("AR", [R, PX])
        CT = [sb(f"CT{j}", [R, CPX]) for j in range(2)]
        YB = [XC[:, j * CPX:(j + 1) * CPX] for j in range(2)]
        QE = AZ = YB
        KM = [LVt[0:TT, j * CPX:(j + 1) * CPX] for j in range(2)]
        SG = [LV[:, j * SPX:(j + 1) * SPX] for j in range(2)]
        REG = sb("REG", [128, 13 * CPX])
        qbd = [REG[0:R, j * CPX:(j + 1) * CPX] for j in range(2)]
        kx = [REG[0:R, (2 + 2 * j) * CPX:(4 + 2 * j) * CPX] for j in range(2)]
        SC = [REG[:, (6 + j) * CPX:(7 + j) * CPX] for j in range(4)]
        PT = [REG[:, (10 + j) * CPX:(11 + j) * CPX] for j in range(2)]
        OT = [REG[0:R, 12 * CPX + j * SPX:12 * CPX + (j + 1) * SPX] for j in range(2)]
        KK, KC, KS = (REG[0:TT, j * PX:(j + 1) * PX] for j in range(3))
        QC, QS = KC[0:R, :], KS[0:R, :]
        XW = [sb(f"XW{j}", [R, CPX]) for j in range(2)]
        vx = [sb(f"vx{j}", [128, NW * 8 * VCOL]) for j in range(2)]
        OB = [sb(f"OB{j}", [128, NW * C]) for j in range(2)]
        mx = sb("mx", [128, 4 * 12])
        rs = sb("rs", [128, 2 * NW * HEADS0])
        kvs_sb = sb("kvs_sb", [R, R])
        kv_sb = sb("kv_sb", [R, R])
        kv2_sb = sb("kv2_sb", [R, R])
        km_sb = sb("km_sb", [R, R])

        PS = [ctx.enter_context(nc.psum_tensor(f"ps{k}", [128, 2 * BANK], F32)) for k in range(NSLOT)]

        loaded_a = sem("loaded_a")
        loaded_b = sem("loaded_b")
        setup_pe = sem("setup_pe")
        setup_dve = sem("setup_dve")
        zeroed = sem("zeroed")
        x_loaded = sem("x_loaded")
        out_stored = sem("out_stored")
        filled = [sem(f"filled{k}") for k in range(NSLOT)]
        freed = [sem(f"freed{k}") for k in range(NSLOT)]
        windows_ready = sem("windows_ready")
        max_ready = sem("max_ready")
        sub_ready = sem("sub_ready")
        exp_ready = sem("exp_ready")
        rs_ready = sem("rs_ready")
        tanh_ready = sem("tanh_ready")
        sig_ready = sem("sig_ready")
        g_padded = sem("g_padded")
        leaky_ready = sem("leaky_ready")
        x2_ready = sem("x2_ready")
        conv_step = sem("conv_step")
        sq_ready = sem("sq_ready")
        exp2_ready = sem("exp2_ready")
        yn_ready = sem("yn_ready")
        t_ready = sem("t_ready")
        q_ready = sem("q_ready")
        kexp_ready = sem("kexp_ready")
        k_ready = sem("k_ready")
        kcs_ready = sem("kcs_ready")
        kvs_copied = sem("kvs_copied")
        kv_summed = sem("kv_summed")
        qcs_ready = sem("qcs_ready")
        ytmp_ready = sem("ytmp_ready")
        ym_ready = sem("ym_ready")

        def slot(job):
            return PS[NTH[job] % NSLOT]

        def wait_slot(pe, i, job):
            k, n = NTH[job] % NSLOT, NTH[job] // NSLOT
            pe.wait_ge(freed[k], i * (2 * USES[k]) + 2 * n + 2)

        def wait_filled(eng, i, job):
            k, n = NTH[job] % NSLOT, NTH[job] // NSLOT
            eng.wait_ge(filled[k], i * USES[k] + n + 1)

        def wait_read(eng, i, job):
            k, n = NTH[job] % NSLOT, NTH[job] // NSLOT
            eng.wait_ge(freed[k], i * (2 * USES[k]) + 2 * n + 4)

        def wait_first(eng, i, job):
            k, n = NTH[job] % NSLOT, NTH[job] // NSLOT
            eng.wait_ge(freed[k], i * (2 * USES[k]) + 2 * n + 3)

        def fill(job):
            return filled[NTH[job] % NSLOT]

        def free(job):
            return freed[NTH[job] % NSLOT]

        def two(job, rows=R, n=SPX):
            return slot(job)[0:rows, :].rearrange("p (b n) -> p b n", b=2)[:, :, 0:n]

        def chunk(t, d):
            return t[:, d * CPX:(d + 1) * CPX]

        def pairs(ap):
            return ap.rearrange("p (b n) -> p b n", b=2)

        def rows16(ap):
            return ap.rearrange("p (y x) -> p y x", x=W)

        def shifted(t, y0, rows, tap):
            dy, dx = tap // 3, tap % 3
            return t[:, y0 + dy:y0 + dy + rows, dx:dx + W]

        def inner(t, d):
            return t[:, 1 + d * CROWS:1 + (d + 1) * CROWS, 1:1 + W]

        def inner2(t, d):
            return inner(t, d)

        def bc_mid(ap, n):
            return ap.unsqueeze(1).broadcast_to([ap.shape[0], n, ap.shape[1]])

        def bc_last(ap, n):
            return ap.unsqueeze(2).broadcast_to([ap.shape[0], ap.shape[1], n])

        def conv_at(i, conv, j, k):
            return i * (4 * len(DVE_CHUNKS) * 9) + (conv * len(DVE_CHUNKS) + j) * 9 + k + 1

        def halo_last(d):
            return min(d + 1, CH - 1)

        def wait_x3(eng, i, conv, d, job):
            if d in PE_CHUNKS:
                wait_read(eng, i, (job, d))
            else:
                eng.wait_ge(conv_step, conv_at(i, conv, DVE_CHUNKS.index(d), 8))

        def wait_t(eng, i, d):
            if d in PE_CHUNKS:
                wait_read(eng, i, ("dc", d))
            else:
                eng.wait_ge(t_ready, i * len(DVE_CHUNKS) + DVE_CHUNKS.index(d) + 1)

        xp = x.rearrange("(n b) c h w -> n (b c) (h w)", b=2)
        op = out.rearrange("(n b) c h w -> n (b c) (h w)", b=2)

        block = ctx.enter_context(nc.Block())

        @block.sync
        def _(sp):
            sp.sem_inc(out_stored, 16)
            sp.dma_start(XR[:, :], xp[0]).then_inc(x_loaded, 16)
            for dst, src in ((wsq_sb, wsq), (vec_sb, vec), (masks_sb, masks), (ident_sb, ident),
                             (wproj_sb, wproj), (bias_sb, bias)):
                sp.dma_start(dst[:, :], src).then_inc(loaded_a, 16)
            for dst, src in ((w2_sb, w2), (const_sb, const), (wfc1_sb, wfc1), (wfc2_sb, wfc2), (fc1b_sb, fc1b),
                             (kbrow_sb, kbrow), (rope_c_sb, rope_c), (rope_th_sb, rope_th), (rope_tw_sb, rope_tw)):
                sp.dma_start(dst[:, :], src).then_inc(loaded_b, 16)

            def body(i):
                for d in range(CH):
                    wait_read(sp, i, ("f2", d))
                    sp.dma_start(op[i][:, d * CPX:(d + 1) * CPX], chunk(X3, d)).then_inc(out_stored, 16)

            def prefetch(i):
                wait_read(sp, i, ("pj", STRIPS - 1))
                sp.dma_start(XR[:, :], xp[i + 1]).then_inc(x_loaded, 16)

            if LOOP:
                with sp.Fori(0, PAIRS - 1) as i:
                    prefetch(i)
                    body(i)
            else:
                for i in range(PAIRS - 1):
                    prefetch(i)
                    body(i)
            body(PAIRS - 1)
            sp.wait_ge(out_stored, 16 * CH * PAIRS + 16)

        @block.tensor
        def _(pe):
            pe.wait_ge(loaded_a, 6 * 16)
            for b in range(2):
                pe.matmul(PS[0][0:R, 0:1], wproj_sb[0:C, b * R:(b + 1) * R], v("bv")[0:C, :],
                          start=(b == 0), stop=(b == 1))
            pe.wait_ge(loaded_b, 9 * 16)
            pe.matmul(PS[0][0:R, BANK:BANK + 1], wq("act"), v("n1b"), start=True, stop=True)
            pe.matmul(PS[1][0:R, 0:1], wq("inp"), v("n1b"), start=True, stop=True)
            for m in range(FG):
                mm = pe.matmul(PS[1 + m][0:128, BANK:BANK + 1], wfc1_sb[:, m * 128:(m + 1) * 128], v("n2b"),
                               start=True, stop=True)
            mm.then_inc(setup_pe, 1)
            for k in range(NSLOT):
                pe.sem_inc(freed[k], 2)
            pe.wait_ge(setup_dve, 2)

            def product(i, job, lhsT, src, rows=R):
                wait_slot(pe, i, job)
                for b in range(2):
                    mm = pe.matmul(slot(job)[0:rows, b * BANK:b * BANK + SPX], lhsT,
                                   src[:, b * SPX:(b + 1) * SPX], start=True, stop=True)
                mm.then_inc(fill(job), 1)

            def conv(i, job, d, w, src):
                wait_slot(pe, i, job)
                for tap in range(9):
                    for b in range(2):
                        mm = pe.matmul(slot(job)[0:R, b * BANK:b * BANK + SPX], w[:, tap * R:(tap + 1) * R],
                                       shifted(src, d * CROWS + b * WIN, WIN, tap),
                                       start=(tap == 0), stop=(tap == 8))
                mm.then_inc(fill(job), 1)

            def two_rows(y):
                return TP[:, :, :].rearrange("p y x -> p (y x)")[:, y * PADW + 1:y * PADW + 1 + TT]

            def attention(i):
                pe.wait_ge(x_loaded, i * 16 + 16)
                for name, s in ATT:
                    job = (name, s)
                    xs = XR[:, s * SPX:(s + 1) * SPX]
                    ps = slot(job)
                    if name == "qk":
                        wait_slot(pe, i, job)
                        pe.matmul(ps[0:R, 0:SPX], wq("q"), xs, start=True, stop=True)
                        mm = pe.matmul(ps[0:R, BANK:BANK + SPX], wq("k"), xs, start=True, stop=True)
                    elif name == "v":
                        wait_slot(pe, i, job)
                        pe.wait_ge(windows_ready, i * (2 * STRIPS) + 2 * s + 2)
                        for w in range(NW):
                            mm = pe.matmul(ps[:, w * 128:w * 128 + R], XW[s % 2][:, w * 128:(w + 1) * 128],
                                           wq("v"), start=True, stop=True)
                    elif name in ("sc0", "sc1"):
                        h = int(name[2])
                        if h == 0:
                            wait_read(pe, i, ("qk", s))
                        wait_slot(pe, i, job)
                        for j in range(3):
                            w = 3 * h + j
                            mm = pe.matmul(ps[:, j * 256:(j + 1) * 256], qbd[s % 2][:, w * 128:(w + 1) * 128],
                                           kx[s % 2][:, w * 256:(w + 1) * 256], start=True, stop=True)
                    elif name in ("tr0", "tr1"):
                        h = int(name[2])
                        n = 2 * s + h
                        pe.wait_ge(exp_ready, i * (2 * STRIPS) + n + 1)
                        wait_slot(pe, i, job)
                        for j in range(6):
                            mm = pe.transpose(ps[:, j * 128:(j + 1) * 128], SC[n % 4][:, j * 128:(j + 1) * 128],
                                              ident_sb[:, :])
                    elif name == "av":
                        wait_read(pe, i, ("tr1", s))
                        wait_read(pe, i, ("tr0", s))
                        wait_read(pe, i, ("v", s))
                        wait_slot(pe, i, job)
                        for w in range(NW):
                            for hp in range(2):
                                j = 2 * (w % 3) + hp
                                o = ps[:, w * 128:w * 128 + 8 * VCOL].rearrange("p (b e) -> p b e", b=2)
                                vb = vx[s % 2][:, (2 * w + hp) * 4 * VCOL:(2 * w + hp + 1) * 4 * VCOL]
                                mm = pe.matmul(o[:, :, hp * 2 * VCOL:(hp + 1) * 2 * VCOL],
                                               PT[w // 3][:, j * 128:(j + 1) * 128],
                                               vb.rearrange("p (b e) -> p b e", b=2), start=True, stop=True)
                    elif name == "ot":
                        wait_read(pe, i, ("av", s))
                        wait_slot(pe, i, job)
                        for w in range(NW // 2):
                            mm = pe.transpose(ps[0:R, w * 128:(w + 1) * 128], OB[s % 2][:, w * R:(w + 1) * R],
                                              ident_sb[:, :])
                    elif name == "pj":
                        wait_read(pe, i, ("ot", s))
                        wait_slot(pe, i, job)
                        for e in range(2):
                            dst = ps[0:R, 0:SPX].rearrange("p (y w e x) -> p e y w x", y=WIN, e=2, x=WIN)[:, e]
                            for b in range(2):
                                o = OT[s % 2].rearrange("p (w b y x) -> p b y w x", b=2, y=WIN, x=WIN)[:, b]
                                mm = pe.matmul(dst, wproj_sb[:, (2 * e + b) * R:(2 * e + b + 1) * R], o,
                                               start=(e == 0 and b == 0), stop=(e == 1 and b == 1),
                                               skip_group_check=True)
                    else:
                        wait_read(pe, i, ("pj", s))
                        wait_slot(pe, i, job)
                        x1 = X1[:, s * SPX:(s + 1) * SPX]
                        pe.matmul(ps[0:R, 0:SPX], wq("w1a"), x1, start=True, stop=True)
                        mm = pe.matmul(ps[0:R, BANK:BANK + SPX], wq("w1b"), x1, start=True, stop=True)
                    mm.then_inc(fill(job), 1)

            def norm(i, xc, va, conv_no, job, which):
                for d in range(CH):
                    wait_x3(pe, i, conv_no, d, job)
                    product(i, (xc, d), cn("center"), chunk(X3, d))
                for d in range(CH):
                    pe.wait_ge(sq_ready, i * (2 * CH) + which * CH + d + 1)
                    product(i, (va, d), cn("mean"), chunk(LV, d))

            def body(i):
                attention(i)
                for d in range(CH):
                    pe.wait_ge(g_padded, i * (STRIPS + 1) + min(2 * d + 3, STRIPS) + (d == CH - 1))
                    if d == 0:
                        pe.wait_ge(g_padded, i * (STRIPS + 1) + STRIPS + 1)
                    conv(i, ("cv", d), d, w2_sb, Gp)
                for d in PE_CHUNKS:
                    pe.wait_ge(x2_ready, i * CH + halo_last(d) + 1)
                    conv(i, ("cp1", d), d, diag[0], ZP)
                norm(i, "xc", "va", 0, "cp1", 0)
                for d in range(CH):
                    pe.wait_ge(yn_ready, i * (2 * CH) + d + 1)
                    product(i, ("ip", d), wq("inp"), chunk(XC, d))
                    product(i, ("ac", d), wq("act"), chunk(XC, d))
                for d in PE_CHUNKS:
                    wait_read(pe, i, ("ip", halo_last(d)))
                    conv(i, ("dc", d), d, diag[1], ZP)
                for d in range(CH):
                    wait_t(pe, i, d)
                    wait_slot(pe, i, ("kt", d))
                    for j in range(CT_):
                        y = 1 + d * CROWS + 2 * j
                        mm = pe.matmul(slot(("kt", d))[0:TT, j * 128:j * 128 + R], two_rows(y),
                                       wq("lk"), start=True, stop=True)
                    mm.then_inc(fill(("kt", d)), 1)
                    wait_slot(pe, i, ("q", d))
                    for b in range(2):
                        y = 1 + d * CROWS + b * WIN
                        mm = pe.matmul(slot(("q", d))[0:R, b * BANK:b * BANK + SPX], wq("lq"),
                                       TP[:, y:y + WIN, 1:1 + W], start=True, stop=True)
                    mm.then_inc(fill(("q", d)), 1)
                    wait_slot(pe, i, ("vt", d))
                    for j in range(CT_):
                        y = 1 + d * CROWS + 2 * j
                        mm = pe.transpose(slot(("vt", d))[0:TT, j * 128:j * 128 + R], two_rows(y),
                                          ident_sb[0:R, 0:R])
                    mm.then_inc(fill(("vt", d)), 1)
                ks, kv, kk = ("ks", 0), ("kv", 0), ("kk", 0)
                wait_slot(pe, i, ks)
                for t in range(TILES):
                    if t % CT_ == 0:
                        pe.wait_ge(k_ready, i * CH + t // CT_ + 1)
                    mm = pe.matmul(slot(ks)[0:R, 0:2], KK[:, t * R:(t + 1) * R], ones2,
                                   start=(t == 0), stop=(t == TILES - 1))
                mm.then_inc(fill(ks), 1)
                wait_slot(pe, i, kv)
                for t in range(TILES):
                    if t % CT_ == 0:
                        wait_read(pe, i, ("vt", t // CT_))
                        pe.wait_ge(kcs_ready, i * (4 * CH) + 4 * (t // CT_) + 4)
                    pe.matmul(slot(kv)[0:R, 0:R], KC[:, t * R:(t + 1) * R], VT[:, t, :],
                              start=(t == 0), stop=(t == TILES - 1))
                    mm = pe.matmul(slot(kv)[0:R, BANK:BANK + R], KS[:, t * R:(t + 1) * R], VT[:, t, :],
                                   start=(t == 0), stop=(t == TILES - 1))
                mm.then_inc(fill(kv), 1)
                pe.wait_ge(kvs_copied, i * 2 + 2)
                pe.matmul(slot(kv)[0:R, R:2 * R], cn("swapT"), kvs_sb[:, :], start=True, stop=False)
                pe.matmul(slot(kv)[0:R, R:2 * R], ident_sb[0:R, 0:R], kv_sb[:, :],
                          start=False, stop=True).then_inc(kv_summed, 1)
                wait_slot(pe, i, kk)
                wait_read(pe, i, kv)
                pe.matmul(slot(kk)[0:R, 0:R], cn("swap"), kv_sb[:, :], start=True, stop=True).then_inc(fill(kk), 1)
                for d in range(CH):
                    if d == 0:
                        wait_read(pe, i, ks)
                    pe.wait_ge(q_ready, i * CH + d + 1)
                    product(i, ("dn", d), km_sb[:, :], chunk(Q, d))
                for d in PE_CHUNKS:
                    wait_t(pe, i, halo_last(d))
                    conv(i, ("le", d), d, diag[2], TP)
                for d in range(CH):
                    job = ("at", d)
                    wait_slot(pe, i, job)
                    if d == 0:
                        wait_read(pe, i, kk)
                    pe.wait_ge(qcs_ready, i * (2 * CH) + 2 * d + 2)
                    for b in range(2):
                        o = slot(job)[0:R, b * BANK:b * BANK + SPX]
                        px = slice(d * CPX + b * SPX, d * CPX + (b + 1) * SPX)
                        pe.matmul(o, kv_sb[:, :], QC[:, px], start=True, stop=False)
                        mm = pe.matmul(o, kv2_sb[:, :], QS[:, px], start=False, stop=True)
                    mm.then_inc(fill(job), 1)
                for d in range(CH):
                    pe.wait_ge(ym_ready, i * CH + d + 1)
                    product(i, ("op", d), wq("out"), CT[d % 2][:, :])
                for d in PE_CHUNKS:
                    wait_read(pe, i, ("op", halo_last(d)))
                    conv(i, ("cp2", d), d, diag[3], ZP)
                norm(i, "xc2", "va2", 3, "cp2", 1)
                for d in range(CH):
                    pe.wait_ge(yn_ready, i * (2 * CH) + CH + d + 1)
                    for m in range(FG):
                        product(i, (f"f1_{m}", d), wfc1_sb[:, m * 128:(m + 1) * 128], chunk(XC, d), 128)
                    job = ("f2", d)
                    wait_slot(pe, i, job)
                    for m in range(FG):
                        wait_read(pe, i, (f"f1_{m}", d))
                        for b in range(2):
                            mm = pe.matmul(slot(job)[0:R, b * BANK:b * BANK + SPX], wfc2_sb[:, m * R:(m + 1) * R],
                                           HB[:, m, b * SPX:(b + 1) * SPX], start=(m == 0), stop=(m == FG - 1))
                    mm.then_inc(fill(job), 1)

            if LOOP:
                with pe.Fori(0, PAIRS) as i:
                    body(i)
            else:
                for i in range(PAIRS):
                    body(i)

        @block.scalar
        def _(act):
            act.wait_ge(setup_dve, 2)

            def edges(i, s):
                wait_read(act, i, ("w1", s))
                gs = Gp[:, 1 + s * WIN:1 + (s + 1) * WIN, :]
                act.activation(gs[:, :, 0:PADW:PADW - 1], gs[:, :, 1:PADW - 1:W - 1], ACT.Copy)\
                   .then_inc(g_padded, 1)

            def attention(i):
                act.wait_ge(x_loaded, i * 16 + 16)
                for name, s in ATT:
                    job = (name, s)
                    ps = slot(job)
                    if name == "qk":
                        dst = XW[s % 2][:, :].rearrange("p (w b y x) -> p b y w x", w=NW, b=2, y=WIN)
                        src = XR[:, s * SPX:(s + 1) * SPX].rearrange("p (y w x) -> p y w x", y=WIN, w=NW)
                        if s >= 2:
                            wait_filled(act, i, ("v", s - 2))
                        for b in range(2):
                            act.activation(dst[:, b], src, ACT.Copy).then_inc(windows_ready, 1)
                        wait_filled(act, i, job)
                        src = ps[0:R, BANK:BANK + SPX].rearrange("p (y w x) -> p y w x", y=WIN, w=NW)
                        dst = kx[s % 2].rearrange("p (w h y x) -> p h y w x", w=NW, h=HEADS0, y=WIN)
                        for h in range(HEADS0):
                            op_ = act.activation(dst[:, h], src, ACT.Identity, bias=kbias[:, h:h + 1],
                                                 scale=head_mask[h])
                        op_.then_inc(free(job), 1)
                    elif name in ("sc0", "sc1"):
                        n = 2 * s + int(name[2])
                        act.wait_ge(sub_ready, i * (2 * STRIPS) + n + 1)
                        act.activation(SC[n % 4], SC[n % 4], ACT.Exp).then_inc(exp_ready, 1)
                    elif name in ("tr0", "tr1"):
                        wait_filled(act, i, job)
                        act.activation(PT[int(name[2])], ps[:, 0:CPX], ACT.Copy).then_inc(free(job), 2)
                    elif name == "ot":
                        wait_filled(act, i, job)
                        act.activation(OT[s % 2], ps[0:R, 0:SPX], ACT.Copy).then_inc(free(job), 2)
                    elif name == "w1":
                        if s >= 2:
                            wait_read(act, i, ("w1", s - 2))
                        wait_filled(act, i, job)
                        act.activation(SG[s % 2], ps[0:R, BANK:BANK + SPX], ACT.Tanh, bias=half_bw1b,
                                       scale=0.5).then_inc(free(job), 1)
                        if s >= 1:
                            edges(i, s - 1)
                edges(i, STRIPS - 1)
                act.wait_ge(g_padded, i * (STRIPS + 1) + STRIPS)
                act.activation(Gp[:, 0:PADW:PADW - 1, :], Gp[:, 1:PADW - 1:H - 1, :], ACT.Copy)\
                   .then_inc(g_padded, 1)

            def norm(i, va, which):
                for d in range(CH):
                    wait_filled(act, i, (va, d))
                    act.activation(pairs(chunk(LV, d)), two((va, d)), ACT.Ln, bias=eps_ln)\
                       .then_inc(free((va, d)), 2)
                for d in range(CH):
                    wait_read(act, i, (va, d))
                act.activation(LV[:, :], LV[:, :], ACT.Exp, scale=-0.5).then_inc(exp2_ready, 1)

            def body(i):
                attention(i)
                for d in range(CH):
                    job = ("cv", d)
                    wait_filled(act, i, job)
                    if d >= 2:
                        act.wait_ge(x2_ready, i * CH + d - 1)
                    act.activation(pairs(YB[d % 2]), two(job), ACT.Identity, bias=v("bw2")).then_inc(free(job), 2)
                for d in PE_CHUNKS:
                    job = ("cp1", d)
                    wait_filled(act, i, job)
                    act.wait_ge(out_stored, i * (16 * CH) + 16)
                    act.activation(pairs(chunk(X3, d)), two(job), ACT.Identity, bias=v("cpe1_b"))\
                       .then_inc(free(job), 2)
                norm(i, "va", 0)
                for d in range(CH):
                    job = ("ac", d)
                    wait_filled(act, i, job)
                    act.activation(pairs(chunk(AR, d)), two(job), ACT.Silu, bias=act_b2).then_inc(free(job), 2)
                for j, d in enumerate(DVE_CHUNKS[:1]):
                    act.wait_ge(conv_step, conv_at(i, 1, j, 8))
                    act.activation(inner(TP, d), rows16(CT[j][:, :]), ACT.Silu).then_inc(t_ready, 1)
                for d in PE_CHUNKS:
                    job = ("dc", d)
                    wait_filled(act, i, job)
                    for b in range(2):
                        y = 1 + d * CROWS + b * WIN
                        op_ = act.activation(TP[:, y:y + WIN, 1:1 + W],
                                             rows16(slot(job)[0:R, b * BANK:b * BANK + SPX]), ACT.Silu,
                                             bias=v("dwc_b"))
                        op_.then_inc(free(job), 1)
                for j, d in list(enumerate(DVE_CHUNKS))[1:]:
                    act.wait_ge(conv_step, conv_at(i, 1, j, 8))
                    act.activation(inner(TP, d), rows16(CT[j][:, :]), ACT.Silu).then_inc(t_ready, 1)
                for d in range(CH):
                    wait_read(act, i, ("kt", d))
                    if d >= 2:
                        act.wait_ge(k_ready, i * CH + d - 1)
                    act.activation(KM[d % 2], chunk(KK, d), ACT.Exp)
                    act.activation(chunk(KK, d), chunk(KK, d), ACT.Relu).then_inc(kexp_ready, 1)
                    job = ("q", d)
                    wait_filled(act, i, job)
                    wait_first(act, i, job)
                    if d >= 2:
                        act.wait_ge(q_ready, i * CH + d - 1)
                    act.activation(pairs(QE[d % 2]), two(job), ACT.Exp, bias=v("lq_b")).then_inc(free(job), 1)
                    job = ("vt", d)
                    wait_filled(act, i, job)
                    act.activation(VT[:, d * CT_:(d + 1) * CT_, :],
                                   slot(job)[0:TT, :].rearrange("p (t c) -> p t c", c=128)[:, :, 0:R],
                                   ACT.Copy).then_inc(free(job), 2)
                for d in range(CH):
                    job = ("dn", d)
                    wait_filled(act, i, job)
                    act.activation(pairs(chunk(LV, d)), two(job), ACT.Ln, bias=eps_z).then_inc(free(job), 2)
                for d in range(CH):
                    wait_read(act, i, ("dn", d))
                act.activation(LV[:, :], LV[:, :], ACT.Exp, scale=-1.0).then_inc(exp2_ready, 1)
                for d in PE_CHUNKS:
                    job = ("cp2", d)
                    wait_filled(act, i, job)
                    act.activation(pairs(chunk(X3, d)), two(job), ACT.Identity, bias=v("cpe2_b"))\
                       .then_inc(free(job), 2)
                norm(i, "va2", 1)
                for d in range(CH):
                    if d >= 1:
                        wait_filled(act, i, ("f2", d - 1))
                    for m in range(FG):
                        job = (f"f1_{m}", d)
                        wait_filled(act, i, job)
                        act.activation(pairs(HB[:, m, :]), two(job, 128), ACT.Gelu, bias=fc1b2[:, m:m + 1])\
                           .then_inc(free(job), 2)

            if LOOP:
                with act.Fori(0, PAIRS) as i:
                    body(i)
            else:
                for i in range(PAIRS):
                    body(i)

        @block.vector
        def _(dve):
            dve.wait_ge(loaded_a, 6 * 16)
            dve.wait_ge(loaded_b, 9 * 16)
            dve.tensor_scalar(kbias[:, :], masks_sb[0:R, 2:2 + HEADS0], v("bk"), None, ALU.mult)
            dve.tensor_scalar(half_bw1b, v("bw1b"), 0.5, None, ALU.mult)
            for n in ("cpe1_4", "cpe2_4"):
                op_ = dve.tensor_scalar(v(n), v(n), 1.0, None, ALU.add)
            op_.then_inc(setup_dve, 1)
            dve.wait_ge(setup_dve, 1)
            for j, n in enumerate(CONVS):
                w9 = vec_sb[:, VI[n + "0"]:VI[n + "0"] + 9]
                dve.tensor_tensor(diag[j][:, :].rearrange("p (t c) -> p t c", c=R), bc_last(w9, R),
                                  bc_mid(ident_sb[0:R, 0:R], 9), ALU.mult)
            dve.wait_ge(setup_pe, 1)
            dve.tensor_tensor(proj_b2, PS[0][0:R, 0:1], v("proj_b"), ALU.add)
            dve.tensor_tensor(act_b2, PS[0][0:R, BANK:BANK + 1], v("act_b"), ALU.add)
            dve.tensor_tensor(inp_b2, PS[1][0:R, 0:1], v("inp_b"), ALU.add)
            for m in range(FG):
                dve.tensor_tensor(fc1b2[:, m:m + 1], PS[1 + m][:, BANK:BANK + 1], fc1b_sb[:, m:m + 1], ALU.add)
            dve.tensor_scalar(wq("act"), wq("act"), v("n1w"), None, ALU.mult)
            dve.tensor_scalar(wq("inp"), wq("inp"), v("n1w"), None, ALU.mult)
            dve.tensor_scalar(wfc1_sb[:, :], wfc1_sb[:, :], v("n2w"), None, ALU.mult).then_inc(setup_dve, 1)
            dve.wait_ge(zeroed, 8)

            def attention(i):
                for name, s in ATT:
                    job = (name, s)
                    ps = slot(job)
                    if name == "qk":
                        wait_filled(dve, i, job)
                        src = ps[0:R, 0:SPX].rearrange("p (y w x) -> p y w x", y=WIN, w=NW)
                        dst = qbd[s % 2].rearrange("p (w b y x) -> p b y w x", w=NW, b=2, y=WIN)
                        for b in range(2):
                            op_ = dve.tensor_scalar(dst[:, b], src, v("bq"), img_mask[b], ALU.add, ALU.mult)
                        op_.then_inc(free(job), 1)
                    elif name == "v":
                        wait_filled(dve, i, job)
                        for hh in range(2):
                            p = slice(64 * hh, 64 * hh + 64)
                            dst = vx[s % 2][p, :].rearrange("p (w j u e) -> p w j u e", w=NW, j=4, u=2)
                            src = ps[p, 0:NW * 128].rearrange("p (w c) -> p w c", w=NW)[:, :, hh * C:(hh + 1) * C]
                            op_ = dve.tensor_copy(dst[:, :, :, hh, 0:D0],
                                                  src.rearrange("p w (j e) -> p w j e", j=4))
                        op_.then_inc(free(job), 2)
                    elif name in ("sc0", "sc1"):
                        n = 2 * s + int(name[2])
                        sc = SC[n % 4].rearrange("p (j m) -> p j m", m=TOK)
                        wait_filled(dve, i, job)
                        dve.tensor_tensor(sc, ps[:, 0:CPX].rearrange("p (j m) -> p j m", m=TOK),
                                          bc_mid(bias_sb[:, :], 12), ALU.add).then_inc(free(job), 2)
                        wait_read(dve, i, job)
                        dve.tensor_reduce(mx[:, (n % 4) * 12:(n % 4) * 12 + 12], sc, AX.X, ALU.max)\
                           .then_inc(max_ready, 1)
                    elif name == "av":
                        wait_filled(dve, i, job)
                        for b in range(2):
                            p = slice(64 * b, 64 * b + 64)
                            o = ps[p, 0:NW * 128].rearrange("p (w c) -> p w c", w=NW)
                            o = o[:, :, b * 4 * VCOL:(b + 1) * 4 * VCOL].rearrange("p w (h e) -> p w h e", e=VCOL)
                            r = rs[p, (s % 2) * 24:(s % 2) * 24 + 24].rearrange("p (w h) -> p w h", w=NW)
                            dve.reciprocal(r, o[:, :, :, D0]).then_inc(rs_ready, 1)
                        dve.wait_ge(rs_ready, i * (2 * STRIPS) + 2 * s + 2)
                        for b in range(2):
                            p = slice(64 * b, 64 * b + 64)
                            o = ps[p, 0:NW * 128].rearrange("p (w c) -> p w c", w=NW)
                            o = o[:, :, b * 4 * VCOL:(b + 1) * 4 * VCOL].rearrange("p w (h e) -> p w h e", e=VCOL)
                            r = rs[p, (s % 2) * 24:(s % 2) * 24 + 24].rearrange("p (w h) -> p w h", w=NW)
                            op_ = dve.tensor_tensor(OB[s % 2][p, :].rearrange("p (w h e) -> p w h e", w=NW, h=HEADS0),
                                                    o[:, :, :, 0:D0],
                                                    r.unsqueeze(3).broadcast_to([64, NW, HEADS0, D0]), ALU.mult)
                        op_.then_inc(free(job), 2)
                    elif name == "pj":
                        wait_filled(dve, i, job)
                        px = slice(s * SPX, (s + 1) * SPX)
                        if s == 0:
                            dve.wait_ge(x_loaded, i * 16 + 16)
                        dve.scalar_tensor_tensor(out=X1[:, px], in0=ps[0:R, 0:SPX], scalar=proj_b2, in1=XR[:, px],
                                                 op0=ALU.add, op1=ALU.add).then_inc(free(job), 2)
                    elif name == "w1":
                        wait_filled(dve, i, job)
                        wait_first(dve, i, job)
                        dve.tensor_scalar(SG[s % 2], SG[s % 2], 0.5, 0.5, ALU.mult, ALU.add).then_inc(sig_ready, 1)
                        dve.wait_ge(sig_ready, i * STRIPS + s + 1)
                        dve.scalar_tensor_tensor(out=Gp[:, 1 + s * WIN:1 + (s + 1) * WIN, 1:1 + W],
                                                 in0=rows16(ps[0:R, 0:SPX]), scalar=v("bw1a"),
                                                 in1=rows16(SG[s % 2]), op0=ALU.add, op1=ALU.mult)\
                           .then_inc(free(job), 1)

            def conv(i, no, j, src, dst, first):
                d = DVE_CHUNKS[j]
                name = CONVS[no]
                taps = [4] + [t for t in range(9) if t != 4]
                for k, tap in enumerate(taps):
                    win = shifted(src, d * CROWS, CROWS, tap)
                    wt = v(f"{name}{tap}")
                    if k == 0:
                        first(win, wt).then_inc(conv_step, 1)
                    else:
                        dve.wait_ge(conv_step, conv_at(i, no, j, k - 1))
                        dve.scalar_tensor_tensor(out=rows16(dst), in0=win, scalar=wt, in1=rows16(dst),
                                                 op0=ALU.mult, op1=ALU.add).then_inc(conv_step, 1)

            def with_bias(dst, b):
                return lambda win, wt: dve.tensor_scalar(rows16(dst), win, wt, v(b), ALU.mult, ALU.add)

            def norm(i, xc, which):
                for d in range(CH):
                    job = (xc, d)
                    wait_filled(dve, i, job)
                    dve.tensor_copy(pairs(chunk(XC, d)), two(job)).then_inc(free(job), 2)
                dve.wait_ge(exp2_ready, i * 3 + 2 * which + 1)
                for d in range(CH):
                    dve.tensor_tensor(chunk(XC, d), chunk(XC, d), chunk(LV, d), ALU.mult).then_inc(yn_ready, 1)

            def body(i):
                attention(i)
                for d in range(CH):
                    wait_read(dve, i, ("cv", d))
                    dve.scalar_tensor_tensor(out=YB[d % 2], in0=YB[d % 2], scalar=0.2, in1=YB[d % 2],
                                             op0=ALU.mult, op1=ALU.max).then_inc(leaky_ready, 1)
                dve.wait_ge(out_stored, i * (16 * CH) + 16)
                for j, d in enumerate(DVE_CHUNKS):
                    dve.wait_ge(x2_ready, i * CH + halo_last(d) + 1)
                    conv(i, 0, j, ZP, chunk(X3, d), with_bias(chunk(X3, d), "cpe1_b"))
                norm(i, "xc", 0)
                for d in range(CH):
                    job = ("ip", d)
                    wait_filled(dve, i, job)
                    if d == 0:
                        for c in PE_CHUNKS:
                            wait_filled(dve, i, ("cp1", c))
                    for b in range(2):
                        y = 1 + d * CROWS + b * WIN
                        dve.tensor_scalar(ZP[:, y:y + WIN, 1:1 + W],
                                          rows16(slot(job)[0:R, b * BANK:b * BANK + SPX]), inp_b2, None,
                                          ALU.add).then_inc(free(job), 1)
                for j, d in enumerate(DVE_CHUNKS):
                    wait_read(dve, i, ("ip", halo_last(d)))
                    conv(i, 1, j, ZP, CT[j][:, :], with_bias(CT[j][:, :], "dwc_b"))

                def k_relu_exp(d):
                    dve.wait_ge(kexp_ready, i * CH + d + 1)
                    dve.scalar_tensor_tensor(out=chunk(KK, d), in0=KM[d % 2], scalar=1.0, in1=chunk(KK, d),
                                             op0=ALU.min, op1=ALU.add).then_inc(k_ready, 1)

                for d in range(CH):
                    job = ("kt", d)
                    wait_filled(dve, i, job)
                    dve.tensor_tensor(chunk(KK, d).rearrange("p (t c) -> p t c", c=R),
                                      slot(job)[0:TT, :].rearrange("p (t c) -> p t c", c=128)[:, :, 0:R],
                                      bc_mid(kbrow_sb[:, :], CT_), ALU.add).then_inc(free(job), 2)
                    job = ("q", d)
                    wait_filled(dve, i, job)
                    dve.tensor_scalar(pairs(chunk(Q, d)), two(job), v("lq_b"), 0.0, ALU.add, ALU.max)\
                       .then_inc(free(job), 1)
                    wait_read(dve, i, job)
                    dve.scalar_tensor_tensor(out=chunk(Q, d), in0=QE[d % 2], scalar=1.0, in1=chunk(Q, d),
                                             op0=ALU.min, op1=ALU.add).then_inc(q_ready, 1)
                    k_relu_exp(d)
                ks, kv, kk = ("ks", 0), ("kv", 0), ("kk", 0)
                wait_filled(dve, i, ks)
                dve.tensor_scalar(km_sb[:, :], cn("headmask"), slot(ks)[0:R, 0:1], 1.0 / PX, ALU.mult, ALU.mult)\
                   .then_inc(free(ks), 2)
                wait_filled(dve, i, kv)
                dve.tensor_copy(kvs_sb[:, :], slot(kv)[0:R, BANK:BANK + R]).then_inc(kvs_copied, 1)
                dve.tensor_copy(kv_sb[:, :], slot(kv)[0:R, 0:R]).then_inc(kvs_copied, 1)
                dve.wait_ge(kv_summed, i + 1)
                dve.scalar_tensor_tensor(out=kv_sb[:, :], in0=slot(kv)[0:R, R:2 * R], scalar=1.0 / PX,
                                         in1=cn("headmask"), op0=ALU.mult, op1=ALU.mult).then_inc(free(kv), 2)
                wait_filled(dve, i, kk)
                dve.tensor_copy(kv2_sb[:, :], slot(kk)[0:R, 0:R]).then_inc(free(kk), 2)

                def x4(d):
                    job = ("op", d)
                    wait_filled(dve, i, job)
                    for b in range(2):
                        y = 1 + d * CROWS + b * WIN
                        px = slice(d * CPX + b * SPX, d * CPX + (b + 1) * SPX)
                        dve.scalar_tensor_tensor(out=ZP[:, y:y + WIN, 1:1 + W],
                                                 in0=rows16(slot(job)[0:R, b * BANK:b * BANK + SPX]),
                                                 scalar=v("out_b"), in1=rows16(X3[:, px]),
                                                 op0=ALU.add, op1=ALU.add).then_inc(free(job), 1)

                dve.wait_ge(exp2_ready, i * 3 + 2)
                for d in range(CH):
                    job = ("at", d)
                    wait_filled(dve, i, job)
                    dve.tensor_tensor(pairs(AZ[d % 2]), two(job), pairs(chunk(LV, d)), ALU.mult)\
                       .then_inc(free(job), 2)
                    wait_read(dve, i, job)
                    ct = CT[d % 2][:, :]
                    if d in PE_CHUNKS:
                        le = ("le", d)
                        wait_filled(dve, i, le)
                        dve.scalar_tensor_tensor(out=pairs(ct), in0=two(le), scalar=v("lepe_b"),
                                                 in1=pairs(AZ[d % 2]), op0=ALU.add, op1=ALU.add)\
                           .then_inc(free(le), 2)
                        wait_read(dve, i, le)
                        dve.tensor_tensor(ct, ct, chunk(AR, d), ALU.mult).then_inc(ym_ready, 1)
                    else:
                        az = AZ[d % 2]
                        j = DVE_CHUNKS.index(d)
                        wait_t(dve, i, d)
                        wait_t(dve, i, halo_last(d))
                        for c in PE_CHUNKS:
                            wait_t(dve, i, c)
                        conv(i, 2, j, TP, ct, lambda win, wt: dve.scalar_tensor_tensor(
                            out=rows16(ct), in0=win, scalar=wt, in1=rows16(az), op0=ALU.mult, op1=ALU.add))
                        dve.wait_ge(conv_step, conv_at(i, 2, j, 8))
                        dve.scalar_tensor_tensor(out=ct, in0=ct, scalar=v("lepe_b"), in1=chunk(AR, d),
                                                 op0=ALU.add, op1=ALU.mult).then_inc(ym_ready, 1)
                    if d >= 1:
                        x4(d - 1)
                x4(CH - 1)
                for j, d in enumerate(DVE_CHUNKS):
                    wait_read(dve, i, ("op", halo_last(d)))
                    conv(i, 3, j, ZP, chunk(X3, d), with_bias(chunk(X3, d), "cpe2_b"))
                norm(i, "xc2", 1)
                for d in range(CH):
                    job = ("f2", d)
                    wait_filled(dve, i, job)
                    dve.scalar_tensor_tensor(out=pairs(chunk(X3, d)), in0=two(job), scalar=v("fc2_b"),
                                             in1=pairs(chunk(X3, d)), op0=ALU.add, op1=ALU.add)\
                       .then_inc(free(job), 2)

            if LOOP:
                with dve.Fori(0, PAIRS) as i:
                    body(i)
            else:
                for i in range(PAIRS):
                    body(i)

        @block.gpsimd
        def _(pool):
            pool.memset(ZP[:, :, :], 0.0).then_inc(zeroed, 1)
            pool.memset(TP[:, :, :], 0.0).then_inc(zeroed, 1)
            for j in range(2):
                pool.memset(vx[j][:, :], 0.0).then_inc(zeroed, 1)
            pool.wait_ge(zeroed, 4)
            for j in range(2):
                for hh in range(2):
                    dst = vx[j][64 * hh:64 * hh + 64, :].rearrange("p (w u e) -> p w u e", u=2, e=VCOL)
                    pool.memset(dst[:, :, hh, D0:VCOL], 1.0).then_inc(zeroed, 1)
            pool.wait_ge(zeroed, 8)
            pool.wait_ge(loaded_b, 9 * 16)

            def attention(i):
                for name, s in ATT:
                    if name in ("sc0", "sc1"):
                        n = 2 * s + int(name[2])
                        sc = SC[n % 4].rearrange("p (j m) -> p j m", m=TOK)
                        pool.wait_ge(max_ready, i * (2 * STRIPS) + n + 1)
                        pool.tensor_tensor(sc, sc, bc_last(mx[:, (n % 4) * 12:(n % 4) * 12 + 12], TOK),
                                           ALU.subtract).then_inc(sub_ready, 1)

            def squares(i, xc, which):
                for d in range(CH):
                    wait_read(pool, i, (xc, d))
                    pool.tensor_tensor(chunk(LV, d), chunk(XC, d), chunk(XC, d), ALU.mult).then_inc(sq_ready, 1)

            def body(i):
                attention(i)
                for d in range(CH):
                    pool.wait_ge(leaky_ready, i * CH + d + 1)
                    pool.tensor_tensor(inner(ZP, d), rows16(chunk(X1, d)), rows16(YB[d % 2]), ALU.add)\
                        .then_inc(x2_ready, 1)
                squares(i, "xc", 0)

                def k_rope(d):
                    pool.wait_ge(k_ready, i * CH + d + 1)
                    half = C // 2
                    k4 = chunk(KK, d).rearrange("p (t b u c) -> p t b u c", t=CT_, b=2, u=2)
                    for n, dst in enumerate((KC, KS)):
                        o4 = chunk(dst, d).rearrange("p (t b u c) -> p t b u c", t=CT_, b=2, u=2)
                        th = rope_th_sb[:, n * TILES * half:(n + 1) * TILES * half]
                        th = th.rearrange("p (t c) -> p t c", c=half)[:, d * CT_:(d + 1) * CT_, :]
                        tw = rope_tw_sb[:, n * half:(n + 1) * half]
                        pool.tensor_tensor(o4[:, :, :, 0, :], k4[:, :, :, 0, :],
                                           th.unsqueeze(2).broadcast_to([TT, CT_, 2, half]), ALU.mult)\
                            .then_inc(kcs_ready, 1)
                        pool.tensor_tensor(o4[:, :, :, 1, :], k4[:, :, :, 1, :],
                                           tw.unsqueeze(1).unsqueeze(1).broadcast_to([TT, CT_, 2, half]), ALU.mult)\
                            .then_inc(kcs_ready, 1)

                for d in range(CH):
                    k_rope(d)
                wait_filled(pool, i, ("kv", 0))
                for d in range(CH):
                    pool.wait_ge(q_ready, i * CH + d + 1)
                    for n, dst in enumerate((QC, QS)):
                        pool.tensor_tensor(chunk(dst, d), chunk(Q, d),
                                           rope_c_sb[:, n * PX + d * CPX:n * PX + (d + 1) * CPX], ALU.mult)\
                            .then_inc(qcs_ready, 1)
                squares(i, "xc2", 1)

            if LOOP:
                with pool.Fori(0, PAIRS) as i:
                    body(i)
            else:
                for i in range(PAIRS):
                    body(i)


def _block_diagonal(np_, a, b):
    z = np_.zeros_like(a)
    return np_.concatenate([np_.concatenate([a, z], 1), np_.concatenate([z, b], 1)], 0)


def layout(p):
    f = np.float32
    bd = lambda w: _block_diagonal(np, w.T, w.T)
    qkv = p["L0_conv_qkv_w"]
    w1 = p["L0_conv_w1_w"]
    lqk = p["L1_conv_qk_w"]
    vcols = np.zeros((R, R), f)
    for hh in range(2):
        for hp in range(2):
            for b in range(2):
                h = 2 * hp + hh
                col = ((hh * 2 + hp) * 2 + b) * D0
                vcols[b * C:(b + 1) * C, col:col + D0] = qkv[2 * C + h * D0:2 * C + (h + 1) * D0].T
    sq = {"q": bd(qkv[0:C]), "k": bd(qkv[C:2 * C]), "v": vcols, "w1a": bd(w1[0:C]), "w1b": bd(w1[C:2 * C]),
          "act": bd(p["L1_conv_act_proj_w"]), "inp": bd(p["L1_conv_in_proj_w"]), "lq": bd(lqk[0:C]),
          "lk": bd(lqk[C:2 * C]), "out": bd(p["L1_conv_out_proj_w"])}
    wsq = np.concatenate([sq[n] for n in SQ], 1)
    pw = p["L0_conv_proj_w"].T
    z = np.zeros_like(pw)
    zz = np.concatenate([z, z], 1)
    wproj = np.concatenate([np.concatenate([pw, z, z, pw, zz, zz], 1), np.concatenate([zz, zz, pw, z, z, pw], 1)], 0)
    w2 = np.concatenate([bd(p["L0_conv_w2_w"][:, :, t // 3, t % 3]) for t in range(9)], 1)
    f1, f2 = p["L1_conv_fc1_w"], p["L1_conv_fc2_w"]
    g = lambda m: slice(64 * m, 64 * m + 64)
    wfc1 = np.concatenate([_block_diagonal(np, f1[g(m)].T, f1[g(m)].T) for m in range(FG)], 1)
    wfc2 = np.concatenate([_block_diagonal(np, f2[:, g(m)].T, f2[:, g(m)].T) for m in range(FG)], 1)
    b0 = p["L0_conv_qkv_b"]
    vecs = {"bq": b0[0:C], "bk": b0[C:2 * C], "bv": b0[2 * C:], "bw1a": p["L0_conv_w1_b"][0:C],
            "bw1b": p["L0_conv_w1_b"][C:], "bw2": p["L0_conv_w2_b"], "proj_b": p["L0_conv_proj_b"],
            "cpe1_b": p["L1_conv_cpe1_b"], "n1w": p["L1_conv_norm1_w"], "n1b": p["L1_conv_norm1_b"],
            "act_b": p["L1_conv_act_proj_b"], "inp_b": p["L1_conv_in_proj_b"], "dwc_b": p["L1_conv_dwc_b"],
            "lq_b": p["L1_conv_qk_b"][0:C], "lepe_b": p["L1_conv_lepe_b"], "out_b": p["L1_conv_out_proj_b"],
            "cpe2_b": p["L1_conv_cpe2_b"], "n2w": p["L1_conv_norm2_w"], "n2b": p["L1_conv_norm2_b"],
            "fc2_b": p["L1_conv_fc2_b"]}
    for n in CONVS:
        w = p[f"L1_conv_{n}w"].reshape(C, 9)
        for t in range(9):
            vecs[f"{n}{t}"] = w[:, t]
    vec = np.stack([np.concatenate([vecs[n], vecs[n]]) for n in VEC], 1)
    fb = p["L1_conv_fc1_b"]
    fc1b = np.stack([np.concatenate([fb[g(m)], fb[g(m)]]) for m in range(FG)], 1)
    kb = p["L1_conv_qk_b"][C:]
    kbrow = np.broadcast_to(np.concatenate([kb, kb])[None], (TT, R))
    yy, xx = np.meshgrid(np.arange(WIN), np.arange(WIN), indexing="ij")
    co = np.stack([yy.reshape(-1), xx.reshape(-1)])
    rel = co[:, :, None] - co[:, None, :] + WIN - 1
    bias = p["L0_conv_bias_table"][rel[0] * (2 * WIN - 1) + rel[1]]
    bias = np.concatenate([bias, bias], 0)
    return {"wsq": wsq, "wproj": wproj, "w2": w2, "wfc1": wfc1, "wfc2": wfc2, "vec": vec, "fc1b": fc1b,
            "kbrow": kbrow, "bias": bias}


def constants():
    f = np.float32
    blk = np.kron(np.eye(2), np.ones((C, C)))
    swap = np.zeros((R, R))
    for j in range(0, R, 2):
        swap[j, j + 1], swap[j + 1, j] = -1, 1
    cn = {"center": np.eye(R) - blk / C, "mean": blk / C, "swap": swap, "swapT": swap.T,
          "headmask": np.kron(np.eye(R // D1), np.ones((D1, D1)))}
    const = np.concatenate([cn[n] for n in CN], 1).astype(f)
    masks = np.zeros((128, 2 + HEADS0 + 4), f)
    for b in range(2):
        masks[b * C:(b + 1) * C, b] = 1.0 / np.sqrt(D0)
    for h in range(HEADS0):
        masks[0:R, 2 + h] = (np.arange(R) % C) // D0 == h
    masks[:, 2 + HEADS0:4 + HEADS0] = 1.0
    masks[W:W + 2, 2 + HEADS0:4 + HEADS0] = 0.0
    masks[:, 4 + HEADS0] = 1e-5
    masks[:, 5 + HEADS0] = 1e-6
    kmax = C // 4
    theta = 1.0 / 10000.0 ** (np.arange(kmax) / kmax)
    hi = np.broadcast_to(np.arange(H)[:, None, None] * theta, (H, W, kmax))
    wi = np.broadcast_to(np.arange(W)[None, :, None] * theta, (H, W, kmax))
    ang = np.repeat(np.concatenate([hi, wi], -1).reshape(PX, C // 2), 2, axis=1)
    cs = np.stack([np.cos(ang), np.sin(ang)]).astype(f)
    rope_c = np.concatenate([np.concatenate([t.T, t.T], 0) for t in cs], 1)
    gap = lambda a: np.concatenate([a[:, :, 0:W], np.zeros_like(a[:, :, 0:2]), a[:, :, W:]], 2)
    tok = gap(cs.reshape(2, TILES, 2 * W, C)).transpose(2, 0, 1, 3)
    th = tok[:, :, :, 0:C // 2].reshape(TT, -1)
    tw = tok[:, :, 0, C // 2:].reshape(TT, -1)
    return {"const": const, "ident": np.eye(128, dtype=f), "masks": masks, "rope_c": rope_c, "rope_th": th,
            "rope_tw": tw}


_INS = ["x", "wsq", "wproj", "w2", "wfc1", "wfc2", "vec", "fc1b", "kbrow", "bias", "const", "ident", "masks",
        "rope_c", "rope_th", "rope_tw"]


def kernel(**inputs):
    import numpy as _np
    import concourse.bacc as _bacc
    from concourse import mybir as _mybir
    from concourse.bass_utils import run_bass_kernel_spmd as _run

    data = {n: _np.asarray(a) for n, a in inputs.items()}
    placed = {"x": data["x"], **layout(data), **constants()}
    nc = _bacc.Bacc("TRN2", target_bir_lowering=False, num_devices=1)
    arrays, args = {}, []
    for name in _INS:
        a = _np.ascontiguousarray(placed[name])
        arrays[f"in_{name}_dram"] = a
        args.append(nc.dram_tensor(f"in_{name}_dram", a.shape, _mybir.dt.from_np(a.dtype), kind="ExternalInput").ap())
    out = nc.dram_tensor("out_0_dram", (B, C, H, W), _mybir.dt.float32, kind="ExternalOutput").ap()
    build(nc, *args, out)
    r = _run(nc, [arrays], core_ids=[0])
    return r.results[0]["out_0_dram"]
```

```python
from contextlib import ExitStack

import numpy as np

import concourse.bass as bass
from concourse import mybir

F32 = mybir.dt.float32
ALU = mybir.AluOpType
ACT = mybir.ActivationFunctionType
AX = mybir.AxisListType

B, C, H, W = 8, 48, 48, 48
PAIRS = B // 2
R = 2 * C
PX = H * W
WIN = 8
TOK = WIN * WIN
HEADS0, D0 = 4, C // 4
HEADS1, D1 = 6, C // 6
STRIPS = H // WIN
SPX = WIN * W
NW = W // WIN
CH = 3
CROWS = H // CH
CPX = CROWS * W
TT = 2 * W + 2
TILES = H // 2
CT_ = TILES // CH
HID = 4 * C
FG = HID // 64
PADW = W + 2
BANK = 512
NSLOT = 4
NSC = 3
N_LOADS_A, N_LOADS_B = 6, 10
VCOL = D0 + 1

SQ = ["q", "k", "v", "w1a", "w1b", "act", "inp", "lq", "lk", "out"]
CN = ["center", "mean", "swap", "swapT", "headmask"]
VEC = (["bq", "bk", "bw1a", "bw1b", "bw2", "cpe1_b", "n1w", "n1b", "act_b", "inp_b", "dwc_b", "lq_b",
        "lepe_b", "out_b", "cpe2_b", "n2w", "n2b", "fc2_b", "proj_b", "bv"]
       + [f"{n}{t}" for n in ("cpe1_", "dwc_", "lepe_", "cpe2_") for t in range(9)])
VI = {n: j for j, n in enumerate(VEC)}
CONVS = ["cpe1_", "dwc_", "lepe_", "cpe2_"]
TAPS = [4, 0, 1, 2, 3, 5, 6, 7, 8]
PARTS = 3


ORDER = """
    +qk.0 +qk.1 cva.0 +sc0.0 cvb.0 +sc1.0 cv.0 cva.1 cvb.1 +sc0.1 cv.1 cva.2 c0_0.0 c0_1.0 c0_2.0 cvb.2
    cv.2 +tr0.0 +sc1.1 c0_0.1 +v.0 xc.0 c0_1.1 +tr1.0 +v.1 c0_2.1 +qk.2 va.0 +av.0 c0_0.2 xc.1 yn.0 +ot.0
    +tr0.1 +tr1.1 +v.2 va.1 c0_1.2 c0_2.2 ip.0 yn.1 +qk.3 xc.2 ip.1 c1_0.0 va.2 c1_1.0 +sc0.2 +sc1.2
    +sc0.3 yn.2 +av.1 +pj.0 ac.0 +ot.1 c1_2.0 ip.2 c1_0.1 +tr0.2 ac.1 +tr1.2 ts.0 +sc1.3 +v.3 c1_1.1 ac.2
    +av.2 c1_2.1 ts.1 kt.0 c1_0.2 +pj.1 q.0 +tr0.3 kt.1 +tr1.3 vt.0 c1_1.2 +qk.4 c1_2.2 q.1 kv.0 c2_0.0
    ts.2 vt.1 +av.3 +ot.2 kt.2 c2_1.0 q.2 +ot.3 +w1.0 kv.1 vt.2 +qk.5 c2_2.0 kv.2 c2_0.1 kp.0 dn.0 +sc0.4
    kk.0 +sc1.4 c2_1.1 dn.1 at.0 am.0 +pj.2 +v.4 c2_2.1 +v.5 dn.2 op.0 c2_0.2 at.1 am.1 +w1.1 +tr0.4
    +tr1.4 c2_1.2 +sc0.5 c2_2.2 at.2 op.1 +sc1.5 c3_0.0 +av.4 am.2 c3_1.0 c3_2.0 op.2 c3_0.1 +ot.4 xc2.0
    +tr0.5 c3_1.1 +pj.3 va2.0 +tr1.5 c3_2.1 c3_0.2 yn2.0 xc2.1 +w1.2 f1_2.0 c3_1.2 c3_2.2 f1_1.0 +av.5
    va2.1 +pj.4 xc2.2 +ot.5 f1_0.0 +w1.3 +pj.5 yn2.1 va2.2 f2.0 f1_2.1 f1_0.1 +w1.4 yn2.2 +w1.5 f1_1.1
    f2.1 f1_2.2 f1_0.2 f1_1.2 +edge.0 f2.2
"""
MERGED = [(t[0] == "+", (t.strip("+").split(".")[0], int(t.split(".")[1]))) for t in ORDER.split()]
ATT = [step for of_next, step in MERGED if of_next]
MAIN = [step for of_next, step in MERGED if not of_next]
CV_PARTS = ["cva", "cvb", "cv"]
NOT_PSUM = {"edge", "yn", "yn2", "ts", "am", "cvb", "cv"} | {f"c{n}_{k}" for n in range(4) for k in range(PARTS)}
RINGS = [[("cv", j[1]) if j[0] == "cva" else j for j in steps if j[0] not in NOT_PSUM] for steps in (ATT, MAIN)]
SLOT = {j: (2 * r + n % 2, n // 2) for r, ring in enumerate(RINGS) for n, j in enumerate(ring)}
USES = [sum(1 for k, _ in SLOT.values() if k == slot) for slot in range(NSLOT)]


def build(nc, x, wsq, wproj, w2, wfc1, wfc2, vec, fc1b, kbrow, bias, const, ident, masks, rope_y, rope_x,
          rope_th, rope_tw, out):
    ctx = ExitStack()
    with ctx:
        def sb(name, shape):
            return ctx.enter_context(nc.sbuf_tensor(name, shape, F32))

        def sem(name):
            return ctx.enter_context(nc.semaphore(name))

        wsq_sb = sb("wsq_sb", [R, len(SQ) * R])
        wproj_sb = sb("wproj_sb", [R, 4 * R])
        w2_sb = sb("w2_sb", [R, 9 * R])
        wfc1_sb = sb("wfc1_sb", [R, FG * 128])
        wfc2_sb = sb("wfc2_sb", [128, FG * R])
        vec_sb = sb("vec_sb", [R, len(VEC)])
        fc1b_sb = sb("fc1b_sb", [128, FG])
        kbrow_sb = sb("kbrow_sb", [TT, R])
        bias_sb = sb("bias_sb", [128, TOK])
        const_sb = sb("const_sb", [R, len(CN) * R])
        ident_sb = sb("ident_sb", [128, 128])
        masks_sb = sb("masks_sb", [128, 2 + HEADS0 + 4])
        rope_y_sb = sb("rope_y_sb", [R, 2 * H])
        rope_x_sb = sb("rope_x_sb", [R, 2 * W])
        rope_th_sb = sb("rope_th_sb", [TT, 2 * TILES * (C // 2)])
        rope_tw_sb = sb("rope_tw_sb", [TT, 2 * (C // 2)])
        kbias = sb("kbias", [R, HEADS0])
        small = sb("small", [R, 8])
        fc1b2 = sb("fc1b2", [128, FG])

        def wq(n):
            j = SQ.index(n)
            return wsq_sb[:, j * R:(j + 1) * R]

        def cn(n):
            j = CN.index(n)
            return const_sb[:, j * R:(j + 1) * R]

        def v(n):
            return vec_sb[:, VI[n]:VI[n] + 1]

        img_mask = [masks_sb[0:R, j:j + 1] for j in range(2)]
        head_mask = [masks_sb[0:R, 2 + h:3 + h] for h in range(HEADS0)]
        ones2 = masks_sb[0:TT, 2 + HEADS0:4 + HEADS0]
        eps_ln = masks_sb[0:R, 4 + HEADS0:5 + HEADS0]
        eps_z = masks_sb[0:R, 5 + HEADS0:6 + HEADS0]
        half_bw1b, proj_b2, act_b2, inp_b2 = (small[:, j:j + 1] for j in range(4))

        XR = sb("XR", [R, PX])
        X1 = sb("X1", [R, PX])
        Gp = sb("G", [R, PADW, PADW])
        qbd = [sb(f"qbd{j}", [R, CPX])[:, :] for j in range(2)]
        kx = [sb(f"kx{j}", [R, 2 * CPX])[:, :] for j in range(2)]
        SC = [sb(f"SC{j}", [128, CPX])[:, :] for j in range(NSC)]
        PT = [sb(f"PT{j}", [128, CPX])[:, :] for j in range(2)]
        OT = [sb(f"OT{j}", [R, SPX])[:, :] for j in range(2)]
        SG = [sb(f"SG{j}", [R, SPX])[:, :] for j in range(2)]
        XW = [sb(f"XW{j}", [R, CPX]) for j in range(2)]
        vx = [sb(f"vx{j}", [128, NW * 8 * VCOL]) for j in range(2)]
        OB = [sb(f"OB{j}", [128, NW * C]) for j in range(2)]
        mx = sb("mx", [128, NSC * 12])
        rs = sb("rs", [128, 2 * NW * HEADS0])
        ZP = sb("ZP", [R, PADW, PADW])
        TP = sb("TP", [R, PADW, PADW])
        X3 = sb("X3", [R, PX])
        XC = sb("XC", [R, PX])
        LVt = sb("LV", [128, PX])
        LV = LVt[0:R, :]
        AR = sb("AR", [R, PX])
        CT = [sb(f"CT{j}", [R, CPX]) for j in range(2)]
        QH = sb("QH", [128, FG * CPX])
        Q = QH[0:R, 0:PX]
        HB = QH[:, :].rearrange("p (m n) -> p m n", m=FG)
        QS = sb("QS", [R, PX])
        T0 = [QS[:, d * CPX:(d + 1) * CPX] for d in range(CH)]
        KK, KC, KS, VT = ([sb(f"{n}{j}", [TT, CPX])[:, :] for j in range(2)] for n in ("KK", "KC", "KS", "VT"))
        YB = [XC[:, j * CPX:(j + 1) * CPX] for j in range(2)]
        QE = AZ = YB
        KM = [LVt[0:TT, j * CPX:(j + 1) * CPX] for j in range(2)]
        kv_sum = sb("kv_sum", [R, 2 * R + 2])
        kv_sb = sb("kv_sb", [R, R])
        kv2_sb = sb("kv2_sb", [R, R])
        km_sb = sb("km_sb", [R, R])

        PS = [ctx.enter_context(nc.psum_tensor(f"ps{k}", [128, 2 * BANK], F32)) for k in range(NSLOT)]

        loaded_a = sem("loaded_a")
        loaded_b = sem("loaded_b")
        setup_pe = sem("setup_pe")
        setup_dve = sem("setup_dve")
        zeroed = sem("zeroed")
        x_loaded = [sem(f"x_loaded{s}") for s in range(STRIPS)]
        out_stored = sem("out_stored")
        filled = [sem(f"filled{k}") for k in range(NSLOT)]
        freed = [sem(f"freed{k}") for k in range(NSLOT)]
        windows_ready = sem("windows_ready")
        max_ready = sem("max_ready")
        sub_ready = sem("sub_ready")
        exp_ready = sem("exp_ready")
        rs_ready = sem("rs_ready")
        tanh_ready = sem("tanh_ready")
        sig_ready = sem("sig_ready")
        g_padded = sem("g_padded")
        leaky_ready = sem("leaky_ready")
        x2_ready = sem("x2_ready")
        conv_step = sem("conv_step")
        sq_ready = sem("sq_ready")
        exp2_ready = sem("exp2_ready")
        yn_ready = sem("yn_ready")
        t_ready = sem("t_ready")
        q_ready = sem("q_ready")
        kexp_ready = sem("kexp_ready")
        k_ready = sem("k_ready")
        kcs_ready = sem("kcs_ready")
        km_ready = sem("km_ready")
        qhalf_ready = sem("qhalf_ready")
        qcs_ready = sem("qcs_ready")
        am_ready = sem("am_ready")
        ym_ready = sem("ym_ready")

        def slot(job):
            return PS[SLOT[job][0]]

        def wait_slot(pe, i, job):
            k, n = SLOT[job]
            pe.wait_ge(freed[k], i * (2 * USES[k]) + 2 * n + 2)

        def wait_filled(eng, i, job):
            k, n = SLOT[job]
            eng.wait_ge(filled[k], i * USES[k] + n + 1)

        def wait_read(eng, i, job):
            k, n = SLOT[job]
            eng.wait_ge(freed[k], i * (2 * USES[k]) + 2 * n + 4)

        def wait_reads(eng, i, jobs, job=None):
            need = {}
            for k, n in [(SLOT[j][0], 2 * SLOT[j][1] + 4) for j in jobs] \
                    + ([(SLOT[job][0], 2 * SLOT[job][1] + 2)] if job else []):
                need[k] = max(need.get(k, 0), n)
            for k, n in need.items():
                eng.wait_ge(freed[k], i * (2 * USES[k]) + n)

        def wait_first(eng, i, job):
            k, n = SLOT[job]
            eng.wait_ge(freed[k], i * (2 * USES[k]) + 2 * n + 3)

        def fill(job):
            return filled[SLOT[job][0]]

        def free(job):
            return freed[SLOT[job][0]]

        def two(job, rows=R, n=SPX):
            return slot(job)[0:rows, :].rearrange("p (b n) -> p b n", b=2)[:, :, 0:n]

        def chunk(t, d):
            return t[:, d * CPX:(d + 1) * CPX]

        def pairs(ap):
            return ap.rearrange("p (b n) -> p b n", b=2)

        def rows16(ap):
            return ap.rearrange("p (y x) -> p y x", x=W)

        def shifted(t, y0, rows, tap):
            dy, dx = tap // 3, tap % 3
            return t[:, y0 + dy:y0 + dy + rows, dx:dx + W]

        def inner(t, d):
            return t[:, 1 + d * CROWS:1 + (d + 1) * CROWS, 1:1 + W]

        def inner2(t, d):
            return inner(t, d)

        def bc_mid(ap, n):
            return ap.unsqueeze(1).broadcast_to([ap.shape[0], n, ap.shape[1]])

        def bc_last(ap, n):
            return ap.unsqueeze(2).broadcast_to([ap.shape[0], ap.shape[1], n])

        def conv_at(i, conv, d, k):
            return i * (4 * CH * 9) + (conv * CH + d) * 9 + k + 1

        def wait_conv(eng, i, conv, d):
            eng.wait_ge(conv_step, conv_at(i, conv, d, 8))

        def halo_last(d):
            return min(d + 1, CH - 1)

        xp = x.rearrange("(n b) c h w -> n (b c) (h w)", b=2)
        op = out.rearrange("(n b) c h w -> n (b c) (h w)", b=2)

        block = ctx.enter_context(nc.Block())

        @block.sync
        def _(sp):
            def load(pair, s):
                px = slice(s * SPX, (s + 1) * SPX)
                sp.dma_start(XR[:, px], xp[pair][:, px]).then_inc(x_loaded[s], 16)

            def store(i):
                for d in range(CH):
                    wait_read(sp, i, ("f2", d))
                    sp.dma_start(op[i][:, d * CPX:(d + 1) * CPX], chunk(X3, d)).then_inc(out_stored, 16)

            sp.sem_inc(out_stored, 16)
            load(0, 0)
            for dst, src in ((wsq_sb, wsq), (vec_sb, vec), (masks_sb, masks), (ident_sb, ident),
                             (wproj_sb, wproj), (bias_sb, bias)):
                sp.dma_start(dst[:, :], src).then_inc(loaded_a, 16)
            for s in range(1, STRIPS):
                load(0, s)
            for dst, src in ((w2_sb, w2), (const_sb, const), (wfc1_sb, wfc1), (wfc2_sb, wfc2), (fc1b_sb, fc1b),
                             (kbrow_sb, kbrow), (rope_y_sb, rope_y), (rope_x_sb, rope_x), (rope_th_sb, rope_th),
                             (rope_tw_sb, rope_tw)):
                sp.dma_start(dst[:, :], src).then_inc(loaded_b, 16)
            for s in range(STRIPS):
                wait_read(sp, 0, ("pj", s))
                load(1, s)
            with sp.Fori(0, PAIRS - 2) as i:
                for s in range(STRIPS):
                    wait_read(sp, i + 1, ("pj", s))
                    load(i + 2, s)
                store(i)
            store(PAIRS - 2)
            store(PAIRS - 1)
            sp.wait_ge(out_stored, 16 * CH * PAIRS + 16)

        @block.tensor
        def _(pe):
            pe.wait_ge(loaded_a, N_LOADS_A * 16)
            for b in range(2):
                pe.matmul(PS[0][0:R, 0:1], wproj_sb[0:C, b * R:(b + 1) * R], v("bv")[0:C, :],
                          start=(b == 0), stop=(b == 1))
            pe.wait_ge(loaded_b, N_LOADS_B * 16)
            pe.matmul(PS[0][0:R, BANK:BANK + 1], wq("act"), v("n1b"), start=True, stop=True)
            pe.matmul(PS[1][0:R, 0:1], wq("inp"), v("n1b"), start=True, stop=True)
            for m in range(FG):
                mm = pe.matmul(PS[1 + m][0:128, BANK:BANK + 1], wfc1_sb[:, m * 128:(m + 1) * 128], v("n2b"),
                               start=True, stop=True)
            mm.then_inc(setup_pe, 1)
            for k in range(NSLOT):
                pe.sem_inc(freed[k], 2)
            pe.wait_ge(setup_dve, 2)

            def product(i, job, lhsT, src, rows=R):
                wait_slot(pe, i, job)
                for b in range(2):
                    mm = pe.matmul(slot(job)[0:rows, b * BANK:b * BANK + SPX], lhsT,
                                   src[:, b * SPX:(b + 1) * SPX], start=True, stop=True)
                mm.then_inc(fill(job), 1)

            def two_rows(y):
                return TP[:, :, :].rearrange("p y x -> p (y x)")[:, y * PADW + 1:y * PADW + 1 + TT]

            def attention(i, name, s):
                if name == "edge":
                    return
                job = (name, s)
                xs = XR[:, s * SPX:(s + 1) * SPX]
                ps = slot(job)
                if name == "qk":
                    pe.wait_ge(x_loaded[s], i * 16 + 16)
                    wait_slot(pe, i, job)
                    pe.matmul(ps[0:R, 0:SPX], wq("q"), xs, start=True, stop=True)
                    mm = pe.matmul(ps[0:R, BANK:BANK + SPX], wq("k"), xs, start=True, stop=True)
                elif name == "v":
                    pe.wait_ge(windows_ready, i * (2 * STRIPS) + 2 * s + 2)
                    wait_slot(pe, i, job)
                    for w in range(NW):
                        mm = pe.matmul(ps[:, w * 128:w * 128 + R], XW[s % 2][:, w * 128:(w + 1) * 128],
                                       wq("v"), start=True, stop=True)
                elif name in ("sc0", "sc1"):
                    h = int(name[2])
                    wait_reads(pe, i, [("qk", s)], job)
                    for j in range(3):
                        w = 3 * h + j
                        mm = pe.matmul(ps[:, j * 256:(j + 1) * 256], qbd[s % 2][:, w * 128:(w + 1) * 128],
                                       kx[s % 2][:, w * 256:(w + 1) * 256], start=True, stop=True)
                elif name in ("tr0", "tr1"):
                    n = 2 * s + int(name[2])
                    pe.wait_ge(exp_ready, i * (2 * STRIPS) + n + 1)
                    wait_slot(pe, i, job)
                    for j in range(6):
                        mm = pe.transpose(ps[:, j * 128:(j + 1) * 128], SC[n % NSC][:, j * 128:(j + 1) * 128],
                                          ident_sb[:, :])
                elif name == "av":
                    wait_reads(pe, i, [("tr0", s), ("tr1", s), ("v", s)], job)
                    for w in range(NW):
                        for hp in range(2):
                            j = 2 * (w % 3) + hp
                            o = ps[:, w * 128:w * 128 + 8 * VCOL].rearrange("p (b e) -> p b e", b=2)
                            vb = vx[s % 2][:, (2 * w + hp) * 4 * VCOL:(2 * w + hp + 1) * 4 * VCOL]
                            mm = pe.matmul(o[:, :, hp * 2 * VCOL:(hp + 1) * 2 * VCOL],
                                           PT[w // 3][:, j * 128:(j + 1) * 128],
                                           vb.rearrange("p (b e) -> p b e", b=2), start=True, stop=True)
                elif name == "ot":
                    wait_reads(pe, i, [("av", s)], job)
                    for w in range(NW // 2):
                        mm = pe.transpose(ps[0:R, w * 128:(w + 1) * 128], OB[s % 2][:, w * R:(w + 1) * R],
                                          ident_sb[:, :])
                elif name == "pj":
                    wait_reads(pe, i, [("ot", s)], job)
                    for e in range(2):
                        dst = ps[0:R, 0:SPX].rearrange("p (y w e x) -> p e y w x", y=WIN, e=2, x=WIN)[:, e]
                        for b in range(2):
                            o = OT[s % 2].rearrange("p (w b y x) -> p b y w x", b=2, y=WIN, x=WIN)[:, b]
                            mm = pe.matmul(dst, wproj_sb[:, (2 * e + b) * R:(2 * e + b + 1) * R], o,
                                           start=(e == 0 and b == 0), stop=(e == 1 and b == 1),
                                           skip_group_check=True)
                else:
                    wait_reads(pe, i, [("pj", s)], job)
                    x1 = X1[:, s * SPX:(s + 1) * SPX]
                    pe.matmul(ps[0:R, 0:SPX], wq("w1a"), x1, start=True, stop=True)
                    mm = pe.matmul(ps[0:R, BANK:BANK + SPX], wq("w1b"), x1, start=True, stop=True)
                mm.then_inc(fill(job), 1)

            def main(i, name, d):
                job = (name, d)
                if name in CV_PARTS:
                    part, job = CV_PARTS.index(name), ("cv", d)
                    if part == 0:
                        if d == 0:
                            pe.wait_ge(g_padded, i * (STRIPS + 1) + STRIPS + 1)
                        wait_slot(pe, i, job)
                    for tap in range(3 * part, 3 * part + 3):
                        for b in range(2):
                            mm = pe.matmul(slot(job)[0:R, b * BANK:b * BANK + SPX], w2_sb[:, tap * R:(tap + 1) * R],
                                           shifted(Gp, d * CROWS + b * WIN, WIN, tap),
                                           start=(tap == 0), stop=(tap == 8))
                    if part == 2:
                        mm.then_inc(fill(job), 1)
                elif name in ("xc", "xc2"):
                    wait_conv(pe, i, 0 if name == "xc" else 3, d)
                    product(i, job, cn("center"), chunk(X3, d))
                elif name in ("va", "va2"):
                    pe.wait_ge(sq_ready, i * (2 * CH) + (name == "va2") * CH + d + 1)
                    product(i, job, cn("mean"), chunk(LV, d))
                elif name in ("ip", "ac"):
                    pe.wait_ge(yn_ready, i * (2 * CH) + d + 1)
                    product(i, job, wq("inp" if name == "ip" else "act"), chunk(XC, d))
                elif name == "kt":
                    pe.wait_ge(t_ready, i * CH + d + 1)
                    wait_slot(pe, i, job)
                    for j in range(CT_):
                        mm = pe.matmul(slot(job)[0:TT, j * 128:j * 128 + R], two_rows(1 + d * CROWS + 2 * j),
                                       wq("lk"), start=True, stop=True)
                    mm.then_inc(fill(job), 1)
                elif name == "q":
                    wait_slot(pe, i, job)
                    for b in range(2):
                        y = 1 + d * CROWS + b * WIN
                        mm = pe.matmul(slot(job)[0:R, b * BANK:b * BANK + SPX], wq("lq"),
                                       TP[:, y:y + WIN, 1:1 + W], start=True, stop=True)
                    mm.then_inc(fill(job), 1)
                elif name == "vt":
                    wait_slot(pe, i, job)
                    for j in range(CT_):
                        mm = pe.transpose(slot(job)[0:TT, j * 128:j * 128 + R], two_rows(1 + d * CROWS + 2 * j),
                                          ident_sb[0:R, 0:R])
                    mm.then_inc(fill(job), 1)
                elif name == "kv":
                    pe.wait_ge(k_ready, i * CH + d + 1)
                    wait_slot(pe, i, job)
                    for t in range(CT_):
                        pe.matmul(slot(job)[0:R, R:R + 2], KK[d % 2][:, t * R:(t + 1) * R], ones2,
                                  start=(t == 0), stop=(t == CT_ - 1))
                    wait_read(pe, i, ("vt", d))
                    pe.wait_ge(kcs_ready, i * (4 * CH) + 4 * d + 4)
                    for src, at in ((KC, 0), (KS, BANK)):
                        for t in range(CT_):
                            mm = pe.matmul(slot(job)[0:R, at:at + R], src[d % 2][:, t * R:(t + 1) * R],
                                           VT[d % 2][:, t * R:(t + 1) * R], start=(t == 0), stop=(t == CT_ - 1))
                    mm.then_inc(fill(job), 1)
                elif name == "kp":
                    wait_reads(pe, i, [("kv", c) for c in range(CH)], job)
                    pe.matmul(slot(job)[0:R, 0:R], cn("swapT"), kv_sum[:, R + 2:2 * R + 2], start=True, stop=False)
                    pe.matmul(slot(job)[0:R, 0:R], ident_sb[0:R, 0:R], kv_sum[:, 0:R],
                              start=False, stop=True).then_inc(fill(job), 1)
                elif name == "kk":
                    wait_reads(pe, i, [("kp", 0)], job)
                    pe.matmul(slot(job)[0:R, 0:R], cn("swap"), kv_sb[:, :], start=True, stop=True)\
                        .then_inc(fill(job), 1)
                elif name == "dn":
                    if d == 0:
                        pe.wait_ge(km_ready, i + 1)
                    pe.wait_ge(q_ready, i * CH + d + 1)
                    product(i, job, km_sb[:, :], chunk(Q, d))
                elif name == "at":
                    pe.wait_ge(qcs_ready, i * (2 * CH) + CH + d + 1)
                    wait_reads(pe, i, [("kk", 0)], job)
                    for b in range(2):
                        o = slot(job)[0:R, b * BANK:b * BANK + SPX]
                        px = slice(d * CPX + b * SPX, d * CPX + (b + 1) * SPX)
                        pe.matmul(o, kv_sb[:, :], Q[:, px], start=True, stop=False)
                        mm = pe.matmul(o, kv2_sb[:, :], QS[:, px], start=False, stop=True)
                    mm.then_inc(fill(job), 1)
                elif name == "op":
                    pe.wait_ge(ym_ready, i * CH + d + 1)
                    product(i, job, wq("out"), CT[d % 2][:, :])
                elif name[:2] == "f1":
                    m = int(name[3])
                    pe.wait_ge(yn_ready, i * (2 * CH) + CH + d + 1)
                    product(i, job, wfc1_sb[:, m * 128:(m + 1) * 128], chunk(XC, d), 128)
                elif name == "f2":
                    for m in range(FG):
                        wait_reads(pe, i, [(f"f1_{m}", d)], job)
                        for b in range(2):
                            mm = pe.matmul(slot(job)[0:R, b * BANK:b * BANK + SPX], wfc2_sb[:, m * R:(m + 1) * R],
                                           HB[:, m, b * SPX:(b + 1) * SPX], start=(m == 0), stop=(m == FG - 1))
                    mm.then_inc(fill(job), 1)

            for name, n in ATT:
                attention(0, name, n)
            with pe.Fori(0, PAIRS - 1) as i:
                for of_next, (name, n) in MERGED:
                    attention(i + 1, name, n) if of_next else main(i, name, n)
            for name, n in MAIN:
                main(PAIRS - 1, name, n)

        @block.scalar
        def _(act):
            act.wait_ge(setup_dve, 2)

            def edges(i, s):
                wait_read(act, i, ("w1", s))
                gs = Gp[:, 1 + s * WIN:1 + (s + 1) * WIN, :]
                act.activation(gs[:, :, 0:PADW:PADW - 1], gs[:, :, 1:PADW - 1:W - 1], ACT.Copy)\
                   .then_inc(g_padded, 1)

            def attention(i, name, s):
                if name == "edge":
                    edges(i, STRIPS - 1)
                    act.wait_ge(g_padded, i * (STRIPS + 1) + STRIPS)
                    act.activation(Gp[:, 0:PADW:PADW - 1, :], Gp[:, 1:PADW - 1:H - 1, :], ACT.Copy)\
                       .then_inc(g_padded, 1)
                    return
                job = (name, s)
                ps = slot(job)
                if name == "qk":
                    dst = XW[s % 2][:, :].rearrange("p (w b y x) -> p b y w x", w=NW, b=2, y=WIN)
                    src = XR[:, s * SPX:(s + 1) * SPX].rearrange("p (y w x) -> p y w x", y=WIN, w=NW)
                    act.wait_ge(x_loaded[s], i * 16 + 16)
                    if s >= 2:
                        wait_filled(act, i, ("v", s - 2))
                    for b in range(2):
                        act.activation(dst[:, b], src, ACT.Copy).then_inc(windows_ready, 1)
                    wait_filled(act, i, job)
                    src = ps[0:R, BANK:BANK + SPX].rearrange("p (y w x) -> p y w x", y=WIN, w=NW)
                    dst = kx[s % 2].rearrange("p (w h y x) -> p h y w x", w=NW, h=HEADS0, y=WIN)
                    for h in range(HEADS0):
                        op_ = act.activation(dst[:, h], src, ACT.Identity, bias=kbias[:, h:h + 1],
                                             scale=head_mask[h])
                    op_.then_inc(free(job), 1)
                elif name in ("sc0", "sc1"):
                    n = 2 * s + int(name[2])
                    act.wait_ge(sub_ready, i * (2 * STRIPS) + n + 1)
                    act.activation(SC[n % NSC], SC[n % NSC], ACT.Exp).then_inc(exp_ready, 1)
                elif name in ("tr0", "tr1"):
                    wait_filled(act, i, job)
                    act.activation(PT[int(name[2])], ps[:, 0:CPX], ACT.Copy).then_inc(free(job), 2)
                elif name == "ot":
                    wait_filled(act, i, job)
                    act.activation(OT[s % 2], ps[0:R, 0:SPX], ACT.Copy).then_inc(free(job), 2)
                elif name == "w1":
                    if s >= 2:
                        wait_read(act, i, ("w1", s - 2))
                    wait_filled(act, i, job)
                    act.activation(SG[s % 2], ps[0:R, BANK:BANK + SPX], ACT.Tanh, bias=half_bw1b,
                                   scale=0.5).then_inc(free(job), 1)
                    if s >= 1:
                        edges(i, s - 1)

            def main(i, name, d):
                job = (name, d)
                if name == "cv":
                    wait_filled(act, i, job)
                    if d >= 2:
                        act.wait_ge(x2_ready, i * CH + d - 1)
                    act.activation(pairs(YB[d % 2]), two(job), ACT.Identity, bias=v("bw2")).then_inc(free(job), 2)
                elif name in ("va", "va2"):
                    wait_filled(act, i, job)
                    act.activation(pairs(chunk(LV, d)), two(job), ACT.Ln, bias=eps_ln).then_inc(free(job), 2)
                    wait_read(act, i, job)
                    act.activation(chunk(LV, d), chunk(LV, d), ACT.Exp, scale=-0.5).then_inc(exp2_ready, 1)
                elif name == "ac":
                    wait_filled(act, i, job)
                    act.activation(pairs(chunk(AR, d)), two(job), ACT.Silu, bias=act_b2).then_inc(free(job), 2)
                elif name == "ts":
                    wait_conv(act, i, 1, d)
                    act.activation(inner(TP, d), rows16(T0[d]), ACT.Silu).then_inc(t_ready, 1)
                elif name == "kt":
                    wait_read(act, i, job)
                    if d >= 2:
                        act.wait_ge(k_ready, i * CH + d - 1)
                    act.activation(KM[d % 2], KK[d % 2], ACT.Exp)
                    act.activation(KK[d % 2], KK[d % 2], ACT.Relu).then_inc(kexp_ready, 1)
                elif name == "q":
                    wait_filled(act, i, job)
                    wait_first(act, i, job)
                    if d >= 2:
                        act.wait_ge(q_ready, i * CH + d - 1)
                    act.activation(pairs(QE[d % 2]), two(job), ACT.Exp, bias=v("lq_b")).then_inc(free(job), 1)
                elif name == "vt":
                    wait_filled(act, i, job)
                    act.activation(VT[d % 2].rearrange("p (t c) -> p t c", c=R),
                                   slot(job)[0:TT, :].rearrange("p (t c) -> p t c", c=128)[:, :, 0:R],
                                   ACT.Copy).then_inc(free(job), 2)
                elif name == "dn":
                    wait_filled(act, i, job)
                    act.activation(pairs(chunk(LV, d)), two(job), ACT.Ln, bias=eps_z).then_inc(free(job), 2)
                    wait_read(act, i, job)
                    act.activation(chunk(LV, d), chunk(LV, d), ACT.Exp, scale=-1.0).then_inc(exp2_ready, 1)
                elif name[:2] == "f1":
                    m = int(name[3])
                    wait_filled(act, i, job)
                    act.activation(pairs(HB[:, m, :]), two(job, 128), ACT.Gelu, bias=fc1b2[:, m:m + 1])\
                       .then_inc(free(job), 2)

            for name, n in ATT:
                attention(0, name, n)
            with act.Fori(0, PAIRS - 1) as i:
                for of_next, (name, n) in MERGED:
                    attention(i + 1, name, n) if of_next else main(i, name, n)
            for name, n in MAIN:
                main(PAIRS - 1, name, n)

        @block.vector
        def _(dve):
            dve.wait_ge(loaded_a, N_LOADS_A * 16)
            dve.wait_ge(loaded_b, N_LOADS_B * 16)
            dve.tensor_scalar(kbias[:, :], masks_sb[0:R, 2:2 + HEADS0], v("bk"), None, ALU.mult)
            dve.tensor_scalar(half_bw1b, v("bw1b"), 0.5, None, ALU.mult)
            for n in ("cpe1_4", "cpe2_4"):
                op_ = dve.tensor_scalar(v(n), v(n), 1.0, None, ALU.add)
            op_.then_inc(setup_dve, 1)
            dve.wait_ge(setup_pe, 1)
            dve.tensor_tensor(proj_b2, PS[0][0:R, 0:1], v("proj_b"), ALU.add)
            dve.tensor_tensor(act_b2, PS[0][0:R, BANK:BANK + 1], v("act_b"), ALU.add)
            dve.tensor_tensor(inp_b2, PS[1][0:R, 0:1], v("inp_b"), ALU.add)
            for m in range(FG):
                dve.tensor_tensor(fc1b2[:, m:m + 1], PS[1 + m][:, BANK:BANK + 1], fc1b_sb[:, m:m + 1], ALU.add)
            dve.tensor_scalar(wq("act"), wq("act"), v("n1w"), None, ALU.mult)
            dve.tensor_scalar(wq("inp"), wq("inp"), v("n1w"), None, ALU.mult)
            dve.tensor_scalar(wfc1_sb[:, :], wfc1_sb[:, :], v("n2w"), None, ALU.mult).then_inc(setup_dve, 1)
            dve.wait_ge(setup_dve, 2)
            dve.wait_ge(zeroed, 8)

            def attention(i, name, s):
                if name == "edge":
                    return
                job = (name, s)
                ps = slot(job)
                if name == "qk":
                    wait_filled(dve, i, job)
                    src = ps[0:R, 0:SPX].rearrange("p (y w x) -> p y w x", y=WIN, w=NW)
                    dst = qbd[s % 2].rearrange("p (w b y x) -> p b y w x", w=NW, b=2, y=WIN)
                    for b in range(2):
                        op_ = dve.tensor_scalar(dst[:, b], src, v("bq"), img_mask[b], ALU.add, ALU.mult)
                    op_.then_inc(free(job), 1)
                elif name == "v":
                    wait_filled(dve, i, job)
                    for hh in range(2):
                        p = slice(64 * hh, 64 * hh + 64)
                        dst = vx[s % 2][p, :].rearrange("p (w j u e) -> p w j u e", w=NW, j=4, u=2)
                        src = ps[p, 0:NW * 128].rearrange("p (w c) -> p w c", w=NW)[:, :, hh * C:(hh + 1) * C]
                        op_ = dve.tensor_copy(dst[:, :, :, hh, 0:D0],
                                              src.rearrange("p w (j e) -> p w j e", j=4))
                    op_.then_inc(free(job), 2)
                elif name in ("sc0", "sc1"):
                    n = 2 * s + int(name[2])
                    sc = SC[n % NSC].rearrange("p (j m) -> p j m", m=TOK)
                    wait_filled(dve, i, job)
                    dve.tensor_tensor(sc, ps[:, 0:CPX].rearrange("p (j m) -> p j m", m=TOK),
                                      bc_mid(bias_sb[:, :], 12), ALU.add).then_inc(free(job), 2)
                    wait_read(dve, i, job)
                    dve.tensor_reduce(mx[:, (n % NSC) * 12:(n % NSC) * 12 + 12], sc, AX.X, ALU.max)\
                       .then_inc(max_ready, 1)
                elif name == "av":
                    wait_filled(dve, i, job)
                    for b in range(2):
                        p = slice(64 * b, 64 * b + 64)
                        o = ps[p, 0:NW * 128].rearrange("p (w c) -> p w c", w=NW)
                        o = o[:, :, b * 4 * VCOL:(b + 1) * 4 * VCOL].rearrange("p w (h e) -> p w h e", e=VCOL)
                        r = rs[p, (s % 2) * 24:(s % 2) * 24 + 24].rearrange("p (w h) -> p w h", w=NW)
                        dve.reciprocal(r, o[:, :, :, D0]).then_inc(rs_ready, 1)
                    dve.wait_ge(rs_ready, i * (2 * STRIPS) + 2 * s + 2)
                    for b in range(2):
                        p = slice(64 * b, 64 * b + 64)
                        o = ps[p, 0:NW * 128].rearrange("p (w c) -> p w c", w=NW)
                        o = o[:, :, b * 4 * VCOL:(b + 1) * 4 * VCOL].rearrange("p w (h e) -> p w h e", e=VCOL)
                        r = rs[p, (s % 2) * 24:(s % 2) * 24 + 24].rearrange("p (w h) -> p w h", w=NW)
                        op_ = dve.tensor_tensor(OB[s % 2][p, :].rearrange("p (w h e) -> p w h e", w=NW, h=HEADS0),
                                                o[:, :, :, 0:D0],
                                                r.unsqueeze(3).broadcast_to([64, NW, HEADS0, D0]), ALU.mult)
                    op_.then_inc(free(job), 2)
                elif name == "pj":
                    wait_filled(dve, i, job)
                    px = slice(s * SPX, (s + 1) * SPX)
                    dve.scalar_tensor_tensor(out=X1[:, px], in0=ps[0:R, 0:SPX], scalar=proj_b2, in1=XR[:, px],
                                             op0=ALU.add, op1=ALU.add).then_inc(free(job), 2)
                elif name == "w1":
                    wait_filled(dve, i, job)
                    wait_first(dve, i, job)
                    dve.tensor_scalar(SG[s % 2], SG[s % 2], 0.5, 0.5, ALU.mult, ALU.add).then_inc(sig_ready, 1)
                    dve.wait_ge(sig_ready, i * STRIPS + s + 1)
                    dve.scalar_tensor_tensor(out=Gp[:, 1 + s * WIN:1 + (s + 1) * WIN, 1:1 + W],
                                             in0=rows16(ps[0:R, 0:SPX]), scalar=v("bw1a"),
                                             in1=rows16(SG[s % 2]), op0=ALU.add, op1=ALU.mult)\
                       .then_inc(free(job), 1)

            def conv_part(i, no, d, part, src, dst, first):
                for k in range(3 * part, 3 * part + 3):
                    tap = TAPS[k]
                    win = shifted(src, d * CROWS, CROWS, tap)
                    wt = v(f"{CONVS[no]}{tap}")
                    if k == 0:
                        first(win, wt).then_inc(conv_step, 1)
                    else:
                        dve.wait_ge(conv_step, conv_at(i, no, d, k - 1))
                        dve.scalar_tensor_tensor(out=rows16(dst), in0=win, scalar=wt, in1=rows16(dst),
                                                 op0=ALU.mult, op1=ALU.add).then_inc(conv_step, 1)

            def with_bias(dst, b):
                return lambda win, wt: dve.tensor_scalar(rows16(dst), win, wt, v(b), ALU.mult, ALU.add)

            def main(i, name, d):
                job = (name, d)
                if name == "cv":
                    wait_read(dve, i, job)
                    dve.scalar_tensor_tensor(out=YB[d % 2], in0=YB[d % 2], scalar=0.2, in1=YB[d % 2],
                                             op0=ALU.mult, op1=ALU.max).then_inc(leaky_ready, 1)
                elif name[:2] == "c0":
                    part = int(name[3])
                    if part == 0:
                        if d == 0:
                            dve.wait_ge(out_stored, i * (16 * CH) + 16)
                        dve.wait_ge(x2_ready, i * CH + halo_last(d) + 1)
                    conv_part(i, 0, d, part, ZP, chunk(X3, d), with_bias(chunk(X3, d), "cpe1_b"))
                elif name in ("xc", "xc2"):
                    wait_filled(dve, i, job)
                    dve.tensor_copy(pairs(chunk(XC, d)), two(job)).then_inc(free(job), 2)
                elif name in ("yn", "yn2"):
                    dve.wait_ge(exp2_ready, i * (3 * CH) + (2 * CH if name == "yn2" else 0) + d + 1)
                    dve.tensor_tensor(chunk(XC, d), chunk(XC, d), chunk(LV, d), ALU.mult).then_inc(yn_ready, 1)
                elif name == "ip":
                    wait_filled(dve, i, job)
                    wait_conv(dve, i, 0, halo_last(d))
                    for b in range(2):
                        y = 1 + d * CROWS + b * WIN
                        dve.tensor_scalar(ZP[:, y:y + WIN, 1:1 + W],
                                          rows16(slot(job)[0:R, b * BANK:b * BANK + SPX]), inp_b2, None,
                                          ALU.add).then_inc(free(job), 1)
                elif name[:2] == "c1":
                    part = int(name[3])
                    if part == 0:
                        wait_read(dve, i, ("ip", halo_last(d)))
                    conv_part(i, 1, d, part, ZP, T0[d], with_bias(T0[d], "dwc_b"))
                elif name == "kt":
                    wait_filled(dve, i, job)
                    dve.tensor_tensor(KK[d % 2].rearrange("p (t c) -> p t c", c=R),
                                      slot(job)[0:TT, :].rearrange("p (t c) -> p t c", c=128)[:, :, 0:R],
                                      bc_mid(kbrow_sb[:, :], CT_), ALU.add).then_inc(free(job), 2)
                elif name == "q":
                    wait_filled(dve, i, job)
                    dve.tensor_scalar(pairs(chunk(Q, d)), two(job), v("lq_b"), 0.0, ALU.add, ALU.max)\
                       .then_inc(free(job), 1)
                    dve.wait_ge(kexp_ready, i * CH + d + 1)
                    dve.scalar_tensor_tensor(out=KK[d % 2], in0=KM[d % 2], scalar=1.0, in1=KK[d % 2],
                                             op0=ALU.min, op1=ALU.add).then_inc(k_ready, 1)
                    wait_read(dve, i, job)
                    dve.scalar_tensor_tensor(out=chunk(Q, d), in0=QE[d % 2], scalar=1.0, in1=chunk(Q, d),
                                             op0=ALU.min, op1=ALU.add).then_inc(q_ready, 1)
                elif name == "kv":
                    wait_filled(dve, i, job)
                    halves = ((kv_sum[:, 0:R + 2], slot(job)[0:R, 0:R + 2]),
                              (kv_sum[:, R + 2:2 * R + 2], slot(job)[0:R, BANK:BANK + R]))
                    if d > 0:
                        wait_read(dve, i, ("kv", d - 1))
                    for dst, src in halves:
                        if d == 0:
                            dve.tensor_copy(dst, src).then_inc(free(job), 1)
                        else:
                            dve.tensor_tensor(dst, src, dst, ALU.add).then_inc(free(job), 1)
                    if d == CH - 1:
                        wait_read(dve, i, job)
                        dve.tensor_scalar(km_sb[:, :], cn("headmask"), kv_sum[:, R:R + 1], 1.0 / PX,
                                          ALU.mult, ALU.mult).then_inc(km_ready, 1)
                elif name == "kp":
                    wait_filled(dve, i, job)
                    dve.scalar_tensor_tensor(out=kv_sb[:, :], in0=slot(job)[0:R, 0:R], scalar=1.0 / PX,
                                             in1=cn("headmask"), op0=ALU.mult, op1=ALU.mult).then_inc(free(job), 2)
                elif name == "kk":
                    wait_filled(dve, i, job)
                    dve.tensor_copy(kv2_sb[:, :], slot(job)[0:R, 0:R]).then_inc(free(job), 2)
                elif name == "at":
                    dve.wait_ge(exp2_ready, i * (3 * CH) + CH + d + 1)
                    wait_filled(dve, i, job)
                    dve.tensor_tensor(pairs(AZ[d % 2]), two(job), pairs(chunk(LV, d)), ALU.mult)\
                       .then_inc(free(job), 2)
                elif name == "am":
                    wait_read(dve, i, ("at", d))
                    wait_conv(dve, i, 2, d)
                    dve.tensor_tensor(CT[d % 2][:, :], CT[d % 2][:, :], AZ[d % 2], ALU.add).then_inc(am_ready, 1)
                elif name[:2] == "c2":
                    part = int(name[3])
                    ct = CT[d % 2][:, :]
                    if part == 0:
                        dve.wait_ge(t_ready, i * CH + halo_last(d) + 1)
                    conv_part(i, 2, d, part, TP, ct, with_bias(ct, "lepe_b"))
                elif name == "op":
                    wait_filled(dve, i, job)
                    for b in range(2):
                        y = 1 + d * CROWS + b * WIN
                        px = slice(d * CPX + b * SPX, d * CPX + (b + 1) * SPX)
                        dve.scalar_tensor_tensor(out=ZP[:, y:y + WIN, 1:1 + W],
                                                 in0=rows16(slot(job)[0:R, b * BANK:b * BANK + SPX]),
                                                 scalar=v("out_b"), in1=rows16(X3[:, px]),
                                                 op0=ALU.add, op1=ALU.add).then_inc(free(job), 1)
                elif name[:2] == "c3":
                    part = int(name[3])
                    if part == 0:
                        wait_read(dve, i, ("op", halo_last(d)))
                    conv_part(i, 3, d, part, ZP, chunk(X3, d), with_bias(chunk(X3, d), "cpe2_b"))
                elif name == "f2":
                    wait_filled(dve, i, job)
                    dve.scalar_tensor_tensor(out=pairs(chunk(X3, d)), in0=two(job), scalar=v("fc2_b"),
                                             in1=pairs(chunk(X3, d)), op0=ALU.add, op1=ALU.add)\
                       .then_inc(free(job), 2)

            for name, n in ATT:
                attention(0, name, n)
            with dve.Fori(0, PAIRS - 1) as i:
                for of_next, (name, n) in MERGED:
                    attention(i + 1, name, n) if of_next else main(i, name, n)
            for name, n in MAIN:
                main(PAIRS - 1, name, n)

        @block.gpsimd
        def _(pool):
            pool.memset(ZP[:, :, :], 0.0).then_inc(zeroed, 1)
            pool.memset(TP[:, :, :], 0.0).then_inc(zeroed, 1)
            for j in range(2):
                pool.memset(vx[j][:, :], 0.0).then_inc(zeroed, 1)
            pool.wait_ge(zeroed, 4)
            for j in range(2):
                for hh in range(2):
                    dst = vx[j][64 * hh:64 * hh + 64, :].rearrange("p (w u e) -> p w u e", u=2, e=VCOL)
                    pool.memset(dst[:, :, hh, D0:VCOL], 1.0).then_inc(zeroed, 1)
            pool.wait_ge(zeroed, 8)
            pool.wait_ge(loaded_b, N_LOADS_B * 16)

            def attention(i, name, s):
                if name in ("sc0", "sc1"):
                    n = 2 * s + int(name[2])
                    sc = SC[n % NSC].rearrange("p (j m) -> p j m", m=TOK)
                    pool.wait_ge(max_ready, i * (2 * STRIPS) + n + 1)
                    pool.tensor_tensor(sc, sc, bc_last(mx[:, (n % NSC) * 12:(n % NSC) * 12 + 12], TOK),
                                       ALU.subtract).then_inc(sub_ready, 1)

            def k_rope(i, d):
                pool.wait_ge(k_ready, i * CH + d + 1)
                half = C // 2
                k4 = KK[d % 2].rearrange("p (t b u c) -> p t b u c", t=CT_, b=2, u=2)
                for n, dst in enumerate((KC, KS)):
                    o4 = dst[d % 2].rearrange("p (t b u c) -> p t b u c", t=CT_, b=2, u=2)
                    th = rope_th_sb[:, n * TILES * half:(n + 1) * TILES * half]
                    th = th.rearrange("p (t c) -> p t c", c=half)[:, d * CT_:(d + 1) * CT_, :]
                    tw = rope_tw_sb[:, n * half:(n + 1) * half]
                    pool.tensor_tensor(o4[:, :, :, 0, :], k4[:, :, :, 0, :],
                                       th.unsqueeze(2).broadcast_to([TT, CT_, 2, half]), ALU.mult)\
                        .then_inc(kcs_ready, 1)
                    pool.tensor_tensor(o4[:, :, :, 1, :], k4[:, :, :, 1, :],
                                       tw.unsqueeze(1).unsqueeze(1).broadcast_to([TT, CT_, 2, half]), ALU.mult)\
                        .then_inc(kcs_ready, 1)

            def q_rope(i, d, n):
                rows = rows16(chunk(Q, d))
                dst = rows16(chunk(QS, d)) if n == 1 else rows
                ty = rope_y_sb[:, n * H + d * CROWS:n * H + (d + 1) * CROWS]
                tx = rope_x_sb[:, n * W:(n + 1) * W]
                pool.tensor_tensor(dst, rows, bc_last(ty, W), ALU.mult).then_inc(qhalf_ready, 1)
                pool.wait_ge(qhalf_ready, i * (2 * CH) + (1 - n) * CH + d + 1)
                pool.tensor_tensor(dst, dst, bc_mid(tx, CROWS), ALU.mult).then_inc(qcs_ready, 1)

            def main(i, name, d):
                if name == "cv":
                    pool.wait_ge(leaky_ready, i * CH + d + 1)
                    pool.tensor_tensor(inner(ZP, d), rows16(chunk(X1, d)), rows16(YB[d % 2]), ALU.add)\
                        .then_inc(x2_ready, 1)
                elif name in ("xc", "xc2"):
                    wait_read(pool, i, (name, d))
                    pool.tensor_tensor(chunk(LV, d), chunk(XC, d), chunk(XC, d), ALU.mult).then_inc(sq_ready, 1)
                elif name == "q":
                    k_rope(i, d)
                    pool.wait_ge(q_ready, i * CH + d + 1)
                    q_rope(i, d, 1)
                elif name == "dn":
                    wait_filled(pool, i, ("dn", d))
                    q_rope(i, d, 0)
                elif name == "am":
                    pool.wait_ge(am_ready, i * CH + d + 1)
                    pool.tensor_tensor(CT[d % 2][:, :], CT[d % 2][:, :], chunk(AR, d), ALU.mult)\
                        .then_inc(ym_ready, 1)

            for name, n in ATT:
                attention(0, name, n)
            with pool.Fori(0, PAIRS - 1) as i:
                for of_next, (name, n) in MERGED:
                    attention(i + 1, name, n) if of_next else main(i, name, n)
            for name, n in MAIN:
                main(PAIRS - 1, name, n)


def _block_diagonal(np_, a, b):
    z = np_.zeros_like(a)
    return np_.concatenate([np_.concatenate([a, z], 1), np_.concatenate([z, b], 1)], 0)


def layout(p):
    f = np.float32
    bd = lambda w: _block_diagonal(np, w.T, w.T)
    qkv = p["L0_conv_qkv_w"]
    w1 = p["L0_conv_w1_w"]
    lqk = p["L1_conv_qk_w"]
    vcols = np.zeros((R, R), f)
    for hh in range(2):
        for hp in range(2):
            for b in range(2):
                h = 2 * hp + hh
                col = ((hh * 2 + hp) * 2 + b) * D0
                vcols[b * C:(b + 1) * C, col:col + D0] = qkv[2 * C + h * D0:2 * C + (h + 1) * D0].T
    sq = {"q": bd(qkv[0:C]), "k": bd(qkv[C:2 * C]), "v": vcols, "w1a": bd(w1[0:C]), "w1b": bd(w1[C:2 * C]),
          "act": bd(p["L1_conv_act_proj_w"]), "inp": bd(p["L1_conv_in_proj_w"]), "lq": bd(lqk[0:C]),
          "lk": bd(lqk[C:2 * C]), "out": bd(p["L1_conv_out_proj_w"])}
    wsq = np.concatenate([sq[n] for n in SQ], 1)
    pw = p["L0_conv_proj_w"].T
    z = np.zeros_like(pw)
    zz = np.concatenate([z, z], 1)
    wproj = np.concatenate([np.concatenate([pw, z, z, pw, zz, zz], 1), np.concatenate([zz, zz, pw, z, z, pw], 1)], 0)
    w2 = np.concatenate([bd(p["L0_conv_w2_w"][:, :, t // 3, t % 3]) for t in range(9)], 1)
    f1, f2 = p["L1_conv_fc1_w"], p["L1_conv_fc2_w"]
    g = lambda m: slice(64 * m, 64 * m + 64)
    wfc1 = np.concatenate([_block_diagonal(np, f1[g(m)].T, f1[g(m)].T) for m in range(FG)], 1)
    wfc2 = np.concatenate([_block_diagonal(np, f2[:, g(m)].T, f2[:, g(m)].T) for m in range(FG)], 1)
    b0 = p["L0_conv_qkv_b"]
    vecs = {"bq": b0[0:C], "bk": b0[C:2 * C], "bv": b0[2 * C:], "bw1a": p["L0_conv_w1_b"][0:C],
            "bw1b": p["L0_conv_w1_b"][C:], "bw2": p["L0_conv_w2_b"], "proj_b": p["L0_conv_proj_b"],
            "cpe1_b": p["L1_conv_cpe1_b"], "n1w": p["L1_conv_norm1_w"], "n1b": p["L1_conv_norm1_b"],
            "act_b": p["L1_conv_act_proj_b"], "inp_b": p["L1_conv_in_proj_b"], "dwc_b": p["L1_conv_dwc_b"],
            "lq_b": p["L1_conv_qk_b"][0:C], "lepe_b": p["L1_conv_lepe_b"], "out_b": p["L1_conv_out_proj_b"],
            "cpe2_b": p["L1_conv_cpe2_b"], "n2w": p["L1_conv_norm2_w"], "n2b": p["L1_conv_norm2_b"],
            "fc2_b": p["L1_conv_fc2_b"]}
    for n in CONVS:
        w = p[f"L1_conv_{n}w"].reshape(C, 9)
        for t in range(9):
            vecs[f"{n}{t}"] = w[:, t]
    vec = np.stack([np.concatenate([vecs[n], vecs[n]]) for n in VEC], 1)
    fb = p["L1_conv_fc1_b"]
    fc1b = np.stack([np.concatenate([fb[g(m)], fb[g(m)]]) for m in range(FG)], 1)
    kb = p["L1_conv_qk_b"][C:]
    kbrow = np.broadcast_to(np.concatenate([kb, kb])[None], (TT, R))
    yy, xx = np.meshgrid(np.arange(WIN), np.arange(WIN), indexing="ij")
    co = np.stack([yy.reshape(-1), xx.reshape(-1)])
    rel = co[:, :, None] - co[:, None, :] + WIN - 1
    bias = p["L0_conv_bias_table"][rel[0] * (2 * WIN - 1) + rel[1]]
    bias = np.concatenate([bias, bias], 0)
    return {"wsq": wsq, "wproj": wproj, "w2": w2, "wfc1": wfc1, "wfc2": wfc2, "vec": vec, "fc1b": fc1b,
            "kbrow": kbrow, "bias": bias}


def constants():
    f = np.float32
    blk = np.kron(np.eye(2), np.ones((C, C)))
    swap = np.zeros((R, R))
    for j in range(0, R, 2):
        swap[j, j + 1], swap[j + 1, j] = -1, 1
    cn = {"center": np.eye(R) - blk / C, "mean": blk / C, "swap": swap, "swapT": swap.T,
          "headmask": np.kron(np.eye(R // D1), np.ones((D1, D1)))}
    const = np.concatenate([cn[n] for n in CN], 1).astype(f)
    masks = np.zeros((128, 2 + HEADS0 + 4), f)
    for b in range(2):
        masks[b * C:(b + 1) * C, b] = 1.0 / np.sqrt(D0)
    for h in range(HEADS0):
        masks[0:R, 2 + h] = (np.arange(R) % C) // D0 == h
    masks[:, 2 + HEADS0:4 + HEADS0] = 1.0
    masks[W:W + 2, 2 + HEADS0:4 + HEADS0] = 0.0
    masks[:, 4 + HEADS0] = 1e-5
    masks[:, 5 + HEADS0] = 1e-6
    kmax = C // 4
    theta = 1.0 / 10000.0 ** (np.arange(kmax) / kmax)
    hi = np.broadcast_to(np.arange(H)[:, None, None] * theta, (H, W, kmax))
    wi = np.broadcast_to(np.arange(W)[None, :, None] * theta, (H, W, kmax))
    ang = np.repeat(np.concatenate([hi, wi], -1).reshape(PX, C // 2), 2, axis=1)
    cs = np.stack([np.cos(ang), np.sin(ang)]).astype(f)
    two = lambda t: np.concatenate([t, t], 1)
    first = np.arange(C) < C // 2
    py, px = cs.reshape(2, H, W, C)[:, :, 0], cs.reshape(2, H, W, C)[:, 0]
    rope_y = np.concatenate([two(np.where(first, t, 1)).T for t in py], 1).astype(f)
    rope_x = np.concatenate([two(np.where(first, 1, t)).T for t in px], 1).astype(f)
    gap = lambda a: np.concatenate([a[:, :, 0:W], np.zeros_like(a[:, :, 0:2]), a[:, :, W:]], 2)
    tok = gap(cs.reshape(2, TILES, 2 * W, C)).transpose(2, 0, 1, 3)
    th = tok[:, :, :, 0:C // 2].reshape(TT, -1)
    tw = tok[:, :, 0, C // 2:].reshape(TT, -1)
    return {"const": const, "ident": np.eye(128, dtype=f), "masks": masks, "rope_y": rope_y,
            "rope_x": rope_x, "rope_th": th,
            "rope_tw": tw}


_INS = ["x", "wsq", "wproj", "w2", "wfc1", "wfc2", "vec", "fc1b", "kbrow", "bias", "const", "ident", "masks",
        "rope_y", "rope_x", "rope_th", "rope_tw"]


def kernel(**inputs):
    import numpy as _np
    import concourse.bacc as _bacc
    from concourse import mybir as _mybir
    from concourse.bass_utils import run_bass_kernel_spmd as _run

    data = {n: _np.asarray(a) for n, a in inputs.items()}
    placed = {"x": data["x"], **layout(data), **constants()}
    nc = _bacc.Bacc("TRN2", target_bir_lowering=False, num_devices=1)
    arrays, args = {}, []
    for name in _INS:
        a = _np.ascontiguousarray(placed[name])
        arrays[f"in_{name}_dram"] = a
        args.append(nc.dram_tensor(f"in_{name}_dram", a.shape, _mybir.dt.from_np(a.dtype), kind="ExternalInput").ap())
    out = nc.dram_tensor("out_0_dram", (B, C, H, W), _mybir.dt.float32, kind="ExternalOutput").ap()
    build(nc, *args, out)
    r = _run(nc, [arrays], core_ids=[0])
    return r.results[0]["out_0_dram"]
```

```python
from contextlib import ExitStack

import numpy as np

import concourse.bass as bass
from concourse import mybir

F32 = mybir.dt.float32
ALU = mybir.AluOpType
ACT = mybir.ActivationFunctionType
AX = mybir.AxisListType

B, C, H, W = 8, 48, 48, 48
PAIRS = B // 2
R = 2 * C
PX = H * W
WIN = 8
TOK = WIN * WIN
HEADS0, D0 = 4, C // 4
HEADS1, D1 = 6, C // 6
STRIPS = H // WIN
SPX = WIN * W
NW = W // WIN
CH = 3
CROWS = H // CH
CPX = CROWS * W
TT = 2 * W + 2
TILES = H // 2
CT_ = TILES // CH
HID = 4 * C
FG = HID // 64
PADW = W + 2
BANK = 512
NSLOT = 4
NSC = 3
N_LOADS_A, N_LOADS_B = 6, 10
VCOL = D0 + 1

SQ = ["q", "k", "v", "w1a", "w1b", "act", "inp", "lq", "lk", "out"]
CN = ["center", "mean", "swap", "swapT", "headmask"]
VEC = (["bq", "bk", "bw1a", "bw1b", "bw2", "cpe1_b", "n1w", "n1b", "act_b", "inp_b", "dwc_b", "lq_b",
        "lepe_b", "out_b", "cpe2_b", "n2w", "n2b", "fc2_b", "proj_b", "bv"]
       + [f"{n}{t}" for n in ("cpe1_", "dwc_", "lepe_", "cpe2_") for t in range(9)])
VI = {n: j for j, n in enumerate(VEC)}
CONVS = ["cpe1_", "dwc_", "lepe_", "cpe2_"]
TAPS = [4, 0, 1, 2, 3, 5, 6, 7, 8]
PARTS = 3


CV_PARTS = ["cva", "cvb", "cv"]

FIRST = """
    qk.0 qk.1 sc0.0 sc1.0 v.0 sc0.1 tr0.0 qk.2 v.1 tr1.0 sc1.1 sc0.2 av.0 v.2 tr0.1 ot.0 tr1.1 qk.3 sc1.2
    av.1 v.3 ot.1 tr0.2 tr1.2 pj.0 qk.4 sc0.3 sc1.3 sc0.4 av.2 pj.1 tr0.3 tr1.3 ot.2 w1.0 qk.5 sc1.4 sc0.5
    av.3 pj.2 tr0.4 tr1.4 ot.3 v.4 sc1.5 av.4 pj.3 v.5 tr0.5 tr1.5 w1.1 av.5 w1.2 w1.3 ot.4 ot.5 pj.4 pj.5
    w1.4 w1.5 edge.0 cva.0 cvb.0 cv.0 cva.1 cvb.1 cv.1 cva.2 cvb.2 cv.2
"""
LOOP = """
    zp.0 zp.1 c0_0.0 +qk.0 c0_1.0 zp.2 +qk.1 c0_2.0 +sc0.0 +sc1.0 c0_0.1 c0_1.1 c0_2.1 +v.0 xc.0 +v.1
    +tr0.0 c0_0.2 +qk.2 +tr1.0 xc.1 c0_1.2 va.0 va.1 +sc0.1 +sc1.1 yn.0 yn.1 +qk.3 c0_2.2 +av.0 ip.0 ip.1
    +tr0.1 xc.2 +ot.0 c1_0.0 c1_1.0 +tr1.1 va.2 +pj.0 +sc0.2 +sc1.2 yn.2 +av.1 +v.2 c1_2.0 ip.2 +tr0.2
    +ot.1 ts.0 c1_0.1 ac.0 +tr1.2 +sc0.3 kt.0 +sc1.3 +pj.1 c1_1.1 +av.2 q.0 +w1.0 ac.1 +ot.2 vt.0 c1_2.1
    c1_0.2 +tr0.3 ts.1 +qk.4 kv.0 c1_1.2 c1_2.2 +v.3 +v.4 ac.2 +tr1.3 +qk.5 ts.2 kt.1 +sc0.4 vt.1 +sc1.4
    +av.3 +pj.2 q.1 +tr0.4 +w1.1 kt.2 c2_0.0 q.2 +w1.2 +tr1.4 kv.1 vt.2 +ot.3 c2_1.0 +sc0.5 kv.2 +v.5 dn.0
    c2_2.0 +sc1.5 +av.4 kp.0 +pj.3 +tr0.5 c2_0.1 kk.0 +w1.3 +ot.4 c2_1.1 c2_2.1 dn.1 at.0 +tr1.5 am.0 dn.2
    +pj.4 +av.5 at.1 am.1 +ot.5 op.0 +pj.5 c2_0.2 +w1.4 +w1.5 c2_1.2 op.1 c2_2.2 at.2 am.2 c3_0.0 c3_1.0
    +edge.0 c3_2.0 +cva.0 +cvb.0 +cv.0 op.2 c3_0.1 +cva.1 c3_1.1 xc2.0 c3_2.1 +cvb.1 va2.0 c3_0.2 c3_1.2
    yn2.0 +cv.1 xc2.1 c3_2.2 +cva.2 va2.1 f1_2.0 +cvb.2 yn2.1 xc2.2 f1_0.0 f1_1.0 va2.2 f2.0 f1_0.1 yn2.2
    +cv.2 f1_2.1 f1_1.1 f2.1 f1_0.2 f1_1.2 f1_2.2 f2.2
"""
LAST = """
    zp.0 zp.1 c0_0.0 c0_1.0 c0_2.0 zp.2 c0_0.1 c0_1.1 c0_2.1 xc.0 c0_0.2 va.0 xc.1 yn.0 va.1 c0_1.2 ip.0
    c0_2.2 yn.1 xc.2 ip.1 va.2 c1_0.0 c1_1.0 yn.2 ip.2 ac.0 c1_2.0 c1_0.1 ac.1 c1_1.1 ts.0 ac.2 c1_2.1
    vt.0 ts.1 kt.0 vt.1 c1_0.2 c1_1.2 q.0 kt.1 c1_2.2 q.1 ts.2 kv.0 kt.2 c2_0.0 q.2 kv.1 c2_1.0 vt.2
    c2_2.0 kv.2 kp.0 c2_0.1 kk.0 dn.0 dn.1 c2_1.1 c2_2.1 at.0 am.0 dn.2 at.1 am.1 op.0 c2_0.2 c2_1.2 at.2
    op.1 c2_2.2 c3_0.0 am.2 c3_1.0 c3_2.0 op.2 c3_0.1 c3_1.1 xc2.0 va2.0 c3_2.1 c3_0.2 xc2.1 yn2.0 f1_2.0
    f1_0.0 c3_1.2 f1_1.0 c3_2.2 xc2.2 va2.1 va2.2 yn2.1 f2.0 f1_0.1 yn2.2 f1_2.1 f1_1.1 f2.1 f1_1.2 f1_0.2
    f1_2.2 f2.2
"""


def steps(text):
    return [(t.strip("+").split(".")[0], int(t.split(".")[1])) for t in text.split()]


ATT, MAIN = steps(FIRST), steps(LAST)
MERGED = [(t[0] == "+", step) for t, step in zip(LOOP.split(), steps(LOOP))]
NOT_PSUM = {"zp", "edge", "yn", "yn2", "ts", "am", "cvb", "cv"} | {f"c{n}_{k}" for n in range(4) for k in range(PARTS)}
SETUP_AFTER = ("sc0", 1)


def places(attention, main):
    rings = [[("cv", j[1]) if j[0] == "cva" else j for j in order if j[0] not in NOT_PSUM]
             for order in (attention, main)]
    return {j: (2 * r + n % 2, n // 2) for r, ring in enumerate(rings) for n, j in enumerate(ring)}


PLACES = {"first": places(ATT, []), "last": places([], MAIN),
          "loop": places([j for of_next, j in MERGED if of_next], [j for of_next, j in MERGED if not of_next])}
USES = [sum(1 for k, _ in PLACES["loop"].values() if k == slot) for slot in range(NSLOT)]


def build(nc, x, wsq, wproj, w2, wfc1, wfc2, vec, fc1b, kbrow, bias, const, ident, masks, rope_y, rope_x,
          rope_th, rope_tw, out):
    ctx = ExitStack()
    with ctx:
        def sb(name, shape):
            return ctx.enter_context(nc.sbuf_tensor(name, shape, F32))

        def sem(name):
            return ctx.enter_context(nc.semaphore(name))

        wsq_sb = sb("wsq_sb", [R, len(SQ) * R])
        wproj_sb = sb("wproj_sb", [R, 4 * R])
        w2_sb = sb("w2_sb", [R, 9 * R])
        wfc1_sb = sb("wfc1_sb", [R, FG * 128])
        wfc2_sb = sb("wfc2_sb", [128, FG * R])
        vec_sb = sb("vec_sb", [R, len(VEC)])
        fc1b_sb = sb("fc1b_sb", [128, FG])
        kbrow_sb = sb("kbrow_sb", [TT, R])
        bias_sb = sb("bias_sb", [128, TOK])
        const_sb = sb("const_sb", [R, len(CN) * R])
        ident_sb = sb("ident_sb", [128, 128])
        masks_sb = sb("masks_sb", [128, 2 + HEADS0 + 4])
        rope_y_sb = sb("rope_y_sb", [R, 2 * H])
        rope_x_sb = sb("rope_x_sb", [R, 2 * W])
        rope_th_sb = sb("rope_th_sb", [TT, 2 * TILES * (C // 2)])
        rope_tw_sb = sb("rope_tw_sb", [TT, 2 * (C // 2)])
        kbias = sb("kbias", [R, HEADS0])
        small = sb("small", [R, 8])
        fc1b2 = sb("fc1b2", [128, FG])

        def wq(n):
            j = SQ.index(n)
            return wsq_sb[:, j * R:(j + 1) * R]

        def cn(n):
            j = CN.index(n)
            return const_sb[:, j * R:(j + 1) * R]

        def v(n):
            return vec_sb[:, VI[n]:VI[n] + 1]

        img_mask = [masks_sb[0:R, j:j + 1] for j in range(2)]
        head_mask = [masks_sb[0:R, 2 + h:3 + h] for h in range(HEADS0)]
        ones2 = masks_sb[0:TT, 2 + HEADS0:4 + HEADS0]
        eps_ln = masks_sb[0:R, 4 + HEADS0:5 + HEADS0]
        eps_z = masks_sb[0:R, 5 + HEADS0:6 + HEADS0]
        half_bw1b, proj_b2, act_b2, inp_b2 = (small[:, j:j + 1] for j in range(4))

        XR = sb("XR", [R, PX])
        X1 = sb("X1", [R, PX])
        Gp = sb("G", [R, PADW, PADW])
        qbd = [sb(f"qbd{j}", [R, CPX])[:, :] for j in range(2)]
        kx = [sb(f"kx{j}", [R, 2 * CPX])[:, :] for j in range(2)]
        SC = [sb(f"SC{j}", [128, CPX])[:, :] for j in range(NSC)]
        PT = [sb(f"PT{j}", [128, CPX])[:, :] for j in range(2)]
        OT = [sb(f"OT{j}", [R, SPX])[:, :] for j in range(2)]
        SG = [sb(f"SG{j}", [R, SPX])[:, :] for j in range(2)]
        XW = [sb(f"XW{j}", [R, CPX]) for j in range(2)]
        vx = [sb(f"vx{j}", [128, NW * 8 * VCOL]) for j in range(2)]
        OB = [sb(f"OB{j}", [128, NW * C]) for j in range(2)]
        mx = sb("mx", [128, NSC * 12])
        rs = sb("rs", [128, 2 * NW * HEADS0])
        ZP = sb("ZP", [R, PADW, PADW])
        TP = sb("TP", [R, PADW, PADW])
        X3 = sb("X3", [R, PX])
        XC = sb("XC", [R, PX])
        LVt = sb("LV", [128, PX])
        LV = LVt[0:R, :]
        AR = sb("AR", [R, PX])
        CT = [sb(f"CT{j}", [R, CPX]) for j in range(2)]
        QH = sb("QH", [128, FG * CPX])
        Q = QH[0:R, 0:PX]
        HB = QH[:, :].rearrange("p (m n) -> p m n", m=FG)
        QS = sb("QS", [R, PX])
        T0 = [QS[:, d * CPX:(d + 1) * CPX] for d in range(CH)]
        KK, KC, KS, VT = ([sb(f"{n}{j}", [TT, CPX])[:, :] for j in range(2)] for n in ("KK", "KC", "KS", "VT"))
        YB = [t[:, :] for t in XW]
        QE = AZ = [XC[:, j * CPX:(j + 1) * CPX] for j in range(2)]
        KM = [LVt[0:TT, j * CPX:(j + 1) * CPX] for j in range(2)]
        kv_sum = sb("kv_sum", [R, 2 * R + 2])
        kv_sb = sb("kv_sb", [R, R])
        kv2_sb = sb("kv2_sb", [R, R])
        km_sb = sb("km_sb", [R, R])

        PS = [ctx.enter_context(nc.psum_tensor(f"ps{k}", [128, 2 * BANK], F32)) for k in range(NSLOT)]

        loaded_a = sem("loaded_a")
        loaded_b = sem("loaded_b")
        setup_pe = sem("setup_pe")
        setup_dve = sem("setup_dve")
        zeroed = sem("zeroed")
        x_loaded = [sem(f"x_loaded{s}") for s in range(STRIPS)]
        out_stored = sem("out_stored")
        filled = [sem(f"filled{k}") for k in range(NSLOT)]
        freed = [sem(f"freed{k}") for k in range(NSLOT)]
        windows_ready = sem("windows_ready")
        max_ready = sem("max_ready")
        sub_ready = sem("sub_ready")
        exp_ready = sem("exp_ready")
        rs_ready = sem("rs_ready")
        sig_ready = sem("sig_ready")
        g_padded = sem("g_padded")
        leaky_ready = sem("leaky_ready")
        x2_ready = sem("x2_ready")
        zp_ready = sem("zp_ready")
        conv_step = sem("conv_step")
        exp2_ready = sem("exp2_ready")
        yn_ready = sem("yn_ready")
        t_ready = sem("t_ready")
        q_ready = sem("q_ready")
        kexp_ready = sem("kexp_ready")
        k_ready = sem("k_ready")
        kcs_ready = sem("kcs_ready")
        km_ready = sem("km_ready")
        qhalf_ready = sem("qhalf_ready")
        qcs_ready = sem("qcs_ready")
        am_ready = sem("am_ready")
        ym_ready = sem("ym_ready")

        SLOT = {}

        def part_of_program(name):
            SLOT.clear()
            SLOT.update(PLACES[name])

        def slot(job):
            return PS[SLOT[job][0]]

        def wait_slot(pe, i, job):
            k, n = SLOT[job]
            pe.wait_ge(freed[k], i * (2 * USES[k]) + 2 * n + 2)

        def wait_filled(eng, i, job):
            k, n = SLOT[job]
            eng.wait_ge(filled[k], i * USES[k] + n + 1)

        def wait_read(eng, i, job):
            k, n = SLOT[job]
            eng.wait_ge(freed[k], i * (2 * USES[k]) + 2 * n + 4)

        def wait_reads(eng, i, jobs, job=None):
            need = {}
            for k, n in [(SLOT[j][0], 2 * SLOT[j][1] + 4) for j in jobs] \
                    + ([(SLOT[job][0], 2 * SLOT[job][1] + 2)] if job else []):
                need[k] = max(need.get(k, 0), n)
            for k, n in need.items():
                eng.wait_ge(freed[k], i * (2 * USES[k]) + n)

        def wait_first(eng, i, job):
            k, n = SLOT[job]
            eng.wait_ge(freed[k], i * (2 * USES[k]) + 2 * n + 3)

        def fill(job):
            return filled[SLOT[job][0]]

        def free(job):
            return freed[SLOT[job][0]]

        def two(job, rows=R, n=SPX):
            return slot(job)[0:rows, :].rearrange("p (b n) -> p b n", b=2)[:, :, 0:n]

        def chunk(t, d):
            return t[:, d * CPX:(d + 1) * CPX]

        def pairs(ap):
            return ap.rearrange("p (b n) -> p b n", b=2)

        def rows16(ap):
            return ap.rearrange("p (y x) -> p y x", x=W)

        def shifted(t, y0, rows, tap):
            dy, dx = tap // 3, tap % 3
            return t[:, y0 + dy:y0 + dy + rows, dx:dx + W]

        def inner(t, d):
            return t[:, 1 + d * CROWS:1 + (d + 1) * CROWS, 1:1 + W]

        def bc_mid(ap, n):
            return ap.unsqueeze(1).broadcast_to([ap.shape[0], n, ap.shape[1]])

        def bc_last(ap, n):
            return ap.unsqueeze(2).broadcast_to([ap.shape[0], ap.shape[1], n])

        def conv_at(i, conv, d, k):
            return i * (4 * CH * 9) + (conv * CH + d) * 9 + k + 2

        def wait_conv(eng, i, conv, d):
            eng.wait_ge(conv_step, conv_at(i, conv, d, 8))

        def halo_last(d):
            return min(d + 1, CH - 1)

        xp = x.rearrange("(n b) c h w -> n (b c) (h w)", b=2)
        op = out.rearrange("(n b) c h w -> n (b c) (h w)", b=2)

        block = ctx.enter_context(nc.Block())

        @block.sync
        def _(sp):
            def load(pair, s):
                px = slice(s * SPX, (s + 1) * SPX)
                sp.dma_start(XR[:, px], xp[pair][:, px]).then_inc(x_loaded[s], 16)

            def store(i):
                for d in range(CH):
                    wait_read(sp, i, ("f2", d))
                    sp.dma_start(op[i][:, d * CPX:(d + 1) * CPX], chunk(X3, d)).then_inc(out_stored, 16)

            sp.sem_inc(out_stored, 16)
            sp.sem_inc(conv_step, 1)
            sp.sem_inc(x2_ready, 1)
            load(0, 0)
            for dst, src in ((wsq_sb, wsq), (vec_sb, vec), (masks_sb, masks), (ident_sb, ident),
                             (wproj_sb, wproj), (bias_sb, bias)):
                sp.dma_start(dst[:, :], src).then_inc(loaded_a, 16)
            for s in range(1, STRIPS):
                load(0, s)
            for dst, src in ((w2_sb, w2), (const_sb, const), (wfc1_sb, wfc1), (wfc2_sb, wfc2), (fc1b_sb, fc1b),
                             (kbrow_sb, kbrow), (rope_y_sb, rope_y), (rope_x_sb, rope_x), (rope_th_sb, rope_th),
                             (rope_tw_sb, rope_tw)):
                sp.dma_start(dst[:, :], src).then_inc(loaded_b, 16)
            part_of_program("first")
            for s in range(STRIPS):
                wait_read(sp, 0, ("pj", s))
                load(1, s)
            part_of_program("loop")
            with sp.Fori(0, PAIRS - 2) as i:
                for s in range(STRIPS):
                    wait_read(sp, i + 1, ("pj", s))
                    load(i + 2, s)
                store(i)
            store(PAIRS - 2)
            part_of_program("last")
            store(PAIRS - 1)
            sp.wait_ge(out_stored, 16 * CH * PAIRS + 16)

        @block.tensor
        def _(pe):
            pe.wait_ge(loaded_a, N_LOADS_A * 16)
            for b in range(2):
                mm = pe.matmul(PS[0][0:R, 0:1], wproj_sb[0:C, b * R:(b + 1) * R], v("bv")[0:C, :],
                               start=(b == 0), stop=(b == 1))
                if b == 1:
                    mm.then_inc(setup_pe, 1)
            for k in range(NSLOT):
                pe.sem_inc(freed[k], 2)
            pe.wait_ge(setup_dve, 1)

            def setup_rest():
                pe.wait_ge(loaded_b, N_LOADS_B * 16)
                pe.matmul(PS[2][0:R, 0:1], wq("act"), v("n1b"), start=True, stop=True)
                pe.matmul(PS[2][0:R, 1:2], wq("inp"), v("n1b"), start=True, stop=True)
                for m in range(FG):
                    mm = pe.matmul(PS[3][0:128, m:m + 1], wfc1_sb[:, m * 128:(m + 1) * 128], v("n2b"),
                                   start=True, stop=True)
                mm.then_inc(setup_pe, 1)
                pe.wait_ge(setup_dve, 2)

            def product(i, job, lhsT, src, rows=R):
                wait_slot(pe, i, job)
                for b in range(2):
                    mm = pe.matmul(slot(job)[0:rows, b * BANK:b * BANK + SPX], lhsT,
                                   src[:, b * SPX:(b + 1) * SPX], start=True, stop=True)
                mm.then_inc(fill(job), 1)

            def two_rows(y):
                return TP[:, :, :].rearrange("p y x -> p (y x)")[:, y * PADW + 1:y * PADW + 1 + TT]

            def gate_conv(i, name, d):
                part, job = CV_PARTS.index(name), ("cv", d)
                if part == 0:
                    if d == 0:
                        pe.wait_ge(g_padded, i * (STRIPS + 1) + STRIPS + 1)
                    wait_slot(pe, i, job)
                for tap in range(3 * part, 3 * part + 3):
                    for b in range(2):
                        mm = pe.matmul(slot(job)[0:R, b * BANK:b * BANK + SPX], w2_sb[:, tap * R:(tap + 1) * R],
                                       shifted(Gp, d * CROWS + b * WIN, WIN, tap),
                                       start=(tap == 0), stop=(tap == 8))
                if part == 2:
                    mm.then_inc(fill(job), 1)

            def attention(i, name, s):
                if name == "edge":
                    return
                if name in CV_PARTS:
                    gate_conv(i, name, s)
                    return
                job = (name, s)
                xs = XR[:, s * SPX:(s + 1) * SPX]
                ps = slot(job)
                if name == "qk":
                    pe.wait_ge(x_loaded[s], i * 16 + 16)
                    wait_slot(pe, i, job)
                    pe.matmul(ps[0:R, 0:SPX], wq("q"), xs, start=True, stop=True)
                    mm = pe.matmul(ps[0:R, BANK:BANK + SPX], wq("k"), xs, start=True, stop=True)
                elif name == "v":
                    pe.wait_ge(windows_ready, i * (2 * STRIPS) + 2 * s + 2)
                    wait_slot(pe, i, job)
                    for w in range(NW):
                        mm = pe.matmul(ps[:, w * 128:w * 128 + R], XW[s % 2][:, w * 128:(w + 1) * 128],
                                       wq("v"), start=True, stop=True)
                elif name in ("sc0", "sc1"):
                    h = int(name[2])
                    wait_reads(pe, i, [("qk", s)], job)
                    for j in range(3):
                        w = 3 * h + j
                        mm = pe.matmul(ps[:, j * 256:(j + 1) * 256], qbd[s % 2][:, w * 128:(w + 1) * 128],
                                       kx[s % 2][:, w * 256:(w + 1) * 256], start=True, stop=True)
                elif name in ("tr0", "tr1"):
                    n = 2 * s + int(name[2])
                    pe.wait_ge(exp_ready, i * (2 * STRIPS) + n + 1)
                    wait_slot(pe, i, job)
                    for j in range(6):
                        mm = pe.transpose(ps[:, j * 128:(j + 1) * 128], SC[n % NSC][:, j * 128:(j + 1) * 128],
                                          ident_sb[:, :])
                elif name == "av":
                    wait_reads(pe, i, [("tr0", s), ("tr1", s), ("v", s)], job)
                    for w in range(NW):
                        for hp in range(2):
                            j = 2 * (w % 3) + hp
                            o = ps[:, w * 128:w * 128 + 8 * VCOL].rearrange("p (b e) -> p b e", b=2)
                            vb = vx[s % 2][:, (2 * w + hp) * 4 * VCOL:(2 * w + hp + 1) * 4 * VCOL]
                            mm = pe.matmul(o[:, :, hp * 2 * VCOL:(hp + 1) * 2 * VCOL],
                                           PT[w // 3][:, j * 128:(j + 1) * 128],
                                           vb.rearrange("p (b e) -> p b e", b=2), start=True, stop=True)
                elif name == "ot":
                    wait_reads(pe, i, [("av", s)], job)
                    for w in range(NW // 2):
                        mm = pe.transpose(ps[0:R, w * 128:(w + 1) * 128], OB[s % 2][:, w * R:(w + 1) * R],
                                          ident_sb[:, :])
                elif name == "pj":
                    wait_reads(pe, i, [("ot", s)], job)
                    for e in range(2):
                        dst = ps[0:R, 0:SPX].rearrange("p (y w e x) -> p e y w x", y=WIN, e=2, x=WIN)[:, e]
                        for b in range(2):
                            o = OT[s % 2].rearrange("p (w b y x) -> p b y w x", b=2, y=WIN, x=WIN)[:, b]
                            mm = pe.matmul(dst, wproj_sb[:, (2 * e + b) * R:(2 * e + b + 1) * R], o,
                                           start=(e == 0 and b == 0), stop=(e == 1 and b == 1),
                                           skip_group_check=True)
                else:
                    wait_reads(pe, i, [("pj", s)], job)
                    x1 = X1[:, s * SPX:(s + 1) * SPX]
                    pe.matmul(ps[0:R, 0:SPX], wq("w1a"), x1, start=True, stop=True)
                    mm = pe.matmul(ps[0:R, BANK:BANK + SPX], wq("w1b"), x1, start=True, stop=True)
                mm.then_inc(fill(job), 1)

            def main(i, name, d):
                job = (name, d)
                if name in ("xc", "xc2"):
                    wait_conv(pe, i, 0 if name == "xc" else 3, d)
                    product(i, job, cn("center"), chunk(X3, d))
                elif name in ("va", "va2"):
                    wait_reads(pe, i, [("xc" if name == "va" else "xc2", d)], job)
                    product(i, job, cn("mean"), chunk(LV, d))
                elif name in ("ip", "ac"):
                    pe.wait_ge(yn_ready, i * (2 * CH) + d + 1)
                    product(i, job, wq("inp" if name == "ip" else "act"), chunk(XC, d))
                elif name == "kt":
                    pe.wait_ge(t_ready, i * CH + d + 1)
                    wait_slot(pe, i, job)
                    for j in range(CT_):
                        mm = pe.matmul(slot(job)[0:TT, j * 128:j * 128 + R], two_rows(1 + d * CROWS + 2 * j),
                                       wq("lk"), start=True, stop=True)
                    mm.then_inc(fill(job), 1)
                elif name == "q":
                    pe.wait_ge(t_ready, i * CH + d + 1)
                    wait_slot(pe, i, job)
                    for b in range(2):
                        y = 1 + d * CROWS + b * WIN
                        mm = pe.matmul(slot(job)[0:R, b * BANK:b * BANK + SPX], wq("lq"),
                                       TP[:, y:y + WIN, 1:1 + W], start=True, stop=True)
                    mm.then_inc(fill(job), 1)
                elif name == "vt":
                    pe.wait_ge(t_ready, i * CH + d + 1)
                    wait_slot(pe, i, job)
                    for j in range(CT_):
                        mm = pe.transpose(slot(job)[0:TT, j * 128:j * 128 + R], two_rows(1 + d * CROWS + 2 * j),
                                          ident_sb[0:R, 0:R])
                    mm.then_inc(fill(job), 1)
                elif name == "kv":
                    pe.wait_ge(k_ready, i * CH + d + 1)
                    wait_slot(pe, i, job)
                    for t in range(CT_):
                        pe.matmul(slot(job)[0:R, R:R + 2], KK[d % 2][:, t * R:(t + 1) * R], ones2,
                                  start=(t == 0), stop=(t == CT_ - 1))
                    wait_read(pe, i, ("vt", d))
                    pe.wait_ge(kcs_ready, i * (4 * CH) + 4 * d + 4)
                    for src, at in ((KC, 0), (KS, BANK)):
                        for t in range(CT_):
                            mm = pe.matmul(slot(job)[0:R, at:at + R], src[d % 2][:, t * R:(t + 1) * R],
                                           VT[d % 2][:, t * R:(t + 1) * R], start=(t == 0), stop=(t == CT_ - 1))
                    mm.then_inc(fill(job), 1)
                elif name == "kp":
                    wait_reads(pe, i, [("kv", c) for c in range(CH)], job)
                    pe.matmul(slot(job)[0:R, 0:R], cn("swapT"), kv_sum[:, R + 2:2 * R + 2], start=True, stop=False)
                    pe.matmul(slot(job)[0:R, 0:R], ident_sb[0:R, 0:R], kv_sum[:, 0:R],
                              start=False, stop=True).then_inc(fill(job), 1)
                elif name == "kk":
                    wait_reads(pe, i, [("kp", 0)], job)
                    pe.matmul(slot(job)[0:R, 0:R], cn("swap"), kv_sb[:, :], start=True, stop=True)\
                        .then_inc(fill(job), 1)
                elif name == "dn":
                    if d == 0:
                        pe.wait_ge(km_ready, i + 1)
                    pe.wait_ge(q_ready, i * CH + d + 1)
                    product(i, job, km_sb[:, :], chunk(Q, d))
                elif name == "at":
                    pe.wait_ge(qcs_ready, i * (2 * CH) + CH + d + 1)
                    wait_reads(pe, i, [("kk", 0)], job)
                    for b in range(2):
                        o = slot(job)[0:R, b * BANK:b * BANK + SPX]
                        px = slice(d * CPX + b * SPX, d * CPX + (b + 1) * SPX)
                        pe.matmul(o, kv_sb[:, :], Q[:, px], start=True, stop=False)
                        mm = pe.matmul(o, kv2_sb[:, :], QS[:, px], start=False, stop=True)
                    mm.then_inc(fill(job), 1)
                elif name == "op":
                    pe.wait_ge(ym_ready, i * CH + d + 1)
                    product(i, job, wq("out"), CT[d % 2][:, :])
                elif name[:2] == "f1":
                    m = int(name[3])
                    pe.wait_ge(yn_ready, i * (2 * CH) + CH + d + 1)
                    product(i, job, wfc1_sb[:, m * 128:(m + 1) * 128], chunk(XC, d), 128)
                elif name == "f2":
                    for m in range(FG):
                        wait_reads(pe, i, [(f"f1_{m}", d)], job)
                        for b in range(2):
                            mm = pe.matmul(slot(job)[0:R, b * BANK:b * BANK + SPX], wfc2_sb[:, m * R:(m + 1) * R],
                                           HB[:, m, b * SPX:(b + 1) * SPX], start=(m == 0), stop=(m == FG - 1))
                    mm.then_inc(fill(job), 1)

            part_of_program("first")
            for name, n in ATT:
                attention(0, name, n)
                if (name, n) == SETUP_AFTER:
                    setup_rest()
            part_of_program("loop")
            with pe.Fori(0, PAIRS - 1) as i:
                for of_next, (name, n) in MERGED:
                    attention(i + 1, name, n) if of_next else main(i, name, n)
            part_of_program("last")
            for name, n in MAIN:
                main(PAIRS - 1, name, n)

        @block.scalar
        def _(act):
            act.wait_ge(setup_dve, 1)
            act.wait_ge(zeroed, 8)

            def edges(i, s):
                wait_read(act, i, ("w1", s))
                gs = Gp[:, 1 + s * WIN:1 + (s + 1) * WIN, :]
                act.activation(gs[:, :, 0:PADW:PADW - 1], gs[:, :, 1:PADW - 1:W - 1], ACT.Copy)\
                   .then_inc(g_padded, 1)

            def attention(i, name, s):
                if name == "edge":
                    edges(i, STRIPS - 1)
                    act.wait_ge(g_padded, i * (STRIPS + 1) + STRIPS)
                    act.activation(Gp[:, 0:PADW:PADW - 1, :], Gp[:, 1:PADW - 1:H - 1, :], ACT.Copy)\
                       .then_inc(g_padded, 1)
                    return
                if name in ("cva", "cvb"):
                    return
                job = (name, s)
                ps = slot(job)
                if name == "cv":
                    wait_filled(act, i, job)
                    if s >= 2:
                        act.wait_ge(x2_ready, i * CH + s)
                    act.activation(pairs(YB[s % 2]), two(job), ACT.Identity, bias=v("bw2")).then_inc(free(job), 2)
                if name == "qk":
                    dst = XW[s % 2][:, :].rearrange("p (w b y x) -> p b y w x", w=NW, b=2, y=WIN)
                    src = XR[:, s * SPX:(s + 1) * SPX].rearrange("p (y w x) -> p y w x", y=WIN, w=NW)
                    act.wait_ge(x_loaded[s], i * 16 + 16)
                    if s >= 2:
                        wait_filled(act, i, ("v", s - 2))
                    elif s == 0:
                        act.wait_ge(x2_ready, i * CH + 1)
                    for b in range(2):
                        act.activation(dst[:, b], src, ACT.Copy).then_inc(windows_ready, 1)
                    wait_filled(act, i, job)
                    src = ps[0:R, BANK:BANK + SPX].rearrange("p (y w x) -> p y w x", y=WIN, w=NW)
                    dst = kx[s % 2].rearrange("p (w h y x) -> p h y w x", w=NW, h=HEADS0, y=WIN)
                    for h in range(HEADS0):
                        op_ = act.activation(dst[:, h], src, ACT.Identity, bias=kbias[:, h:h + 1],
                                             scale=head_mask[h])
                    op_.then_inc(free(job), 1)
                elif name == "v":
                    wait_filled(act, i, job)
                    for hh in range(2):
                        p = slice(64 * hh, 64 * hh + 64)
                        dst = vx[s % 2][p, :].rearrange("p (w j u e) -> p w j u e", w=NW, j=4, u=2)
                        src = ps[p, 0:NW * 128].rearrange("p (w c) -> p w c", w=NW)[:, :, hh * C:(hh + 1) * C]
                        op_ = act.activation(dst[:, :, :, hh, 0:D0], src.rearrange("p w (j e) -> p w j e", j=4),
                                             ACT.Copy)
                    op_.then_inc(free(job), 2)
                elif name in ("sc0", "sc1"):
                    n = 2 * s + int(name[2])
                    act.wait_ge(sub_ready, i * (2 * STRIPS) + n + 1)
                    act.activation(SC[n % NSC], SC[n % NSC], ACT.Exp).then_inc(exp_ready, 1)
                elif name in ("tr0", "tr1"):
                    wait_filled(act, i, job)
                    act.activation(PT[int(name[2])], ps[:, 0:CPX], ACT.Copy).then_inc(free(job), 2)
                elif name == "ot":
                    wait_filled(act, i, job)
                    act.activation(OT[s % 2], ps[0:R, 0:SPX], ACT.Copy).then_inc(free(job), 2)
                elif name == "w1":
                    if s >= 2:
                        wait_read(act, i, ("w1", s - 2))
                    wait_filled(act, i, job)
                    act.activation(SG[s % 2], ps[0:R, BANK:BANK + SPX], ACT.Tanh, bias=half_bw1b,
                                   scale=0.5).then_inc(free(job), 1)
                    if s >= 1:
                        edges(i, s - 1)

            def main(i, name, d):
                job = (name, d)
                if name == "zp":
                    act.wait_ge(x2_ready, i * CH + d + 2)
                    act.wait_ge(conv_step, conv_at(i, 0, 0, 0) - 1)
                    act.activation(inner(ZP, d), rows16(chunk(X1, d)), ACT.Copy).then_inc(zp_ready, 1)
                elif name in ("xc", "xc2"):
                    wait_filled(act, i, job)
                    act.activation(pairs(chunk(XC, d)), two(job), ACT.Copy).then_inc(free(job), 1)
                    act.activation(pairs(chunk(LV, d)), two(job), ACT.Square).then_inc(free(job), 1)
                elif name == "ip":
                    wait_filled(act, i, job)
                    wait_conv(act, i, 0, halo_last(d))
                    for b in range(2):
                        y = 1 + d * CROWS + b * WIN
                        act.activation(ZP[:, y:y + WIN, 1:1 + W],
                                       rows16(slot(job)[0:R, b * BANK:b * BANK + SPX]), ACT.Identity,
                                       bias=inp_b2).then_inc(free(job), 1)
                elif name in ("va", "va2"):
                    wait_filled(act, i, job)
                    act.activation(pairs(chunk(LV, d)), two(job), ACT.Ln, bias=eps_ln).then_inc(free(job), 2)
                    wait_read(act, i, job)
                    act.activation(chunk(LV, d), chunk(LV, d), ACT.Exp, scale=-0.5).then_inc(exp2_ready, 1)
                elif name == "ac":
                    wait_filled(act, i, job)
                    act.activation(pairs(chunk(AR, d)), two(job), ACT.Silu, bias=act_b2).then_inc(free(job), 2)
                elif name == "ts":
                    wait_conv(act, i, 1, d)
                    act.activation(inner(TP, d), rows16(T0[d]), ACT.Silu).then_inc(t_ready, 1)
                elif name == "kt":
                    wait_read(act, i, job)
                    if d >= 2:
                        act.wait_ge(k_ready, i * CH + d - 1)
                    act.activation(KM[d % 2], KK[d % 2], ACT.Exp)
                    act.activation(KK[d % 2], KK[d % 2], ACT.Relu).then_inc(kexp_ready, 1)
                elif name == "q":
                    wait_filled(act, i, job)
                    act.activation(pairs(chunk(Q, d)), two(job), ACT.Relu, bias=v("lq_b")).then_inc(free(job), 1)
                    if d >= 2:
                        act.wait_ge(q_ready, i * CH + d - 1)
                    act.activation(pairs(QE[d % 2]), two(job), ACT.Exp, bias=v("lq_b")).then_inc(free(job), 1)
                elif name == "vt":
                    wait_filled(act, i, job)
                    act.activation(VT[d % 2].rearrange("p (t c) -> p t c", c=R),
                                   slot(job)[0:TT, :].rearrange("p (t c) -> p t c", c=128)[:, :, 0:R],
                                   ACT.Copy).then_inc(free(job), 2)
                elif name == "dn":
                    wait_filled(act, i, job)
                    act.activation(pairs(chunk(LV, d)), two(job), ACT.Ln, bias=eps_z).then_inc(free(job), 2)
                    wait_read(act, i, job)
                    act.activation(chunk(LV, d), chunk(LV, d), ACT.Exp, scale=-1.0).then_inc(exp2_ready, 1)
                elif name[:2] == "f1":
                    m = int(name[3])
                    wait_filled(act, i, job)
                    act.activation(pairs(HB[:, m, :]), two(job, 128), ACT.Gelu, bias=fc1b2[:, m:m + 1])\
                       .then_inc(free(job), 2)

            part_of_program("first")
            for name, n in ATT:
                attention(0, name, n)
            act.wait_ge(setup_dve, 2)
            part_of_program("loop")
            with act.Fori(0, PAIRS - 1) as i:
                for of_next, (name, n) in MERGED:
                    attention(i + 1, name, n) if of_next else main(i, name, n)
            part_of_program("last")
            for name, n in MAIN:
                main(PAIRS - 1, name, n)

        @block.vector
        def _(dve):
            dve.wait_ge(loaded_a, N_LOADS_A * 16)
            dve.tensor_scalar(kbias[:, :], masks_sb[0:R, 2:2 + HEADS0], v("bk"), None, ALU.mult)
            dve.tensor_scalar(half_bw1b, v("bw1b"), 0.5, None, ALU.mult)
            dve.wait_ge(setup_pe, 1)
            dve.tensor_tensor(proj_b2, PS[0][0:R, 0:1], v("proj_b"), ALU.add).then_inc(setup_dve, 1)

            def setup_rest():
                for n in ("cpe1_4", "cpe2_4"):
                    dve.tensor_scalar(v(n), v(n), 1.0, None, ALU.add)
                dve.wait_ge(loaded_b, N_LOADS_B * 16)
                dve.wait_ge(setup_pe, 2)
                dve.tensor_tensor(act_b2, PS[2][0:R, 0:1], v("act_b"), ALU.add)
                dve.tensor_tensor(inp_b2, PS[2][0:R, 1:2], v("inp_b"), ALU.add)
                dve.tensor_tensor(fc1b2[:, :], PS[3][:, 0:FG], fc1b_sb[:, :], ALU.add)
                dve.tensor_scalar(wq("act"), wq("act"), v("n1w"), None, ALU.mult)
                dve.tensor_scalar(wq("inp"), wq("inp"), v("n1w"), None, ALU.mult)
                dve.tensor_scalar(wfc1_sb[:, :], wfc1_sb[:, :], v("n2w"), None, ALU.mult).then_inc(setup_dve, 1)
                dve.wait_ge(setup_dve, 2)

            dve.wait_ge(zeroed, 8)

            def attention(i, name, s):
                job = (name, s)
                if name == "cv":
                    wait_read(dve, i, job)
                    dve.scalar_tensor_tensor(out=YB[s % 2], in0=YB[s % 2], scalar=0.2, in1=YB[s % 2],
                                             op0=ALU.mult, op1=ALU.max).then_inc(leaky_ready, 1)
                if name in CV_PARTS or name == "edge":
                    return
                ps = slot(job)
                if name == "qk":
                    wait_filled(dve, i, job)
                    src = ps[0:R, 0:SPX].rearrange("p (y w x) -> p y w x", y=WIN, w=NW)
                    dst = qbd[s % 2].rearrange("p (w b y x) -> p b y w x", w=NW, b=2, y=WIN)
                    for b in range(2):
                        op_ = dve.tensor_scalar(dst[:, b], src, v("bq"), img_mask[b], ALU.add, ALU.mult)
                    op_.then_inc(free(job), 1)
                elif name in ("sc0", "sc1"):
                    n = 2 * s + int(name[2])
                    sc = SC[n % NSC].rearrange("p (j m) -> p j m", m=TOK)
                    wait_filled(dve, i, job)
                    dve.tensor_tensor(sc, ps[:, 0:CPX].rearrange("p (j m) -> p j m", m=TOK),
                                      bc_mid(bias_sb[:, :], 12), ALU.add).then_inc(free(job), 2)
                    wait_read(dve, i, job)
                    dve.tensor_reduce(mx[:, (n % NSC) * 12:(n % NSC) * 12 + 12], sc, AX.X, ALU.max)\
                       .then_inc(max_ready, 1)
                elif name == "av":
                    wait_filled(dve, i, job)
                    for b in range(2):
                        p = slice(64 * b, 64 * b + 64)
                        o = ps[p, 0:NW * 128].rearrange("p (w c) -> p w c", w=NW)
                        o = o[:, :, b * 4 * VCOL:(b + 1) * 4 * VCOL].rearrange("p w (h e) -> p w h e", e=VCOL)
                        r = rs[p, (s % 2) * 24:(s % 2) * 24 + 24].rearrange("p (w h) -> p w h", w=NW)
                        dve.reciprocal(r, o[:, :, :, D0]).then_inc(rs_ready, 1)
                    dve.wait_ge(rs_ready, i * (2 * STRIPS) + 2 * s + 2)
                    for b in range(2):
                        p = slice(64 * b, 64 * b + 64)
                        o = ps[p, 0:NW * 128].rearrange("p (w c) -> p w c", w=NW)
                        o = o[:, :, b * 4 * VCOL:(b + 1) * 4 * VCOL].rearrange("p w (h e) -> p w h e", e=VCOL)
                        r = rs[p, (s % 2) * 24:(s % 2) * 24 + 24].rearrange("p (w h) -> p w h", w=NW)
                        op_ = dve.tensor_tensor(OB[s % 2][p, :].rearrange("p (w h e) -> p w h e", w=NW, h=HEADS0),
                                                o[:, :, :, 0:D0],
                                                r.unsqueeze(3).broadcast_to([64, NW, HEADS0, D0]), ALU.mult)
                    op_.then_inc(free(job), 2)
                elif name == "pj":
                    wait_filled(dve, i, job)
                    px = slice(s * SPX, (s + 1) * SPX)
                    dve.scalar_tensor_tensor(out=X1[:, px], in0=ps[0:R, 0:SPX], scalar=proj_b2, in1=XR[:, px],
                                             op0=ALU.add, op1=ALU.add).then_inc(free(job), 2)
                elif name == "w1":
                    wait_filled(dve, i, job)
                    wait_first(dve, i, job)
                    dve.tensor_scalar(SG[s % 2], SG[s % 2], 0.5, 0.5, ALU.mult, ALU.add).then_inc(sig_ready, 1)
                    dve.wait_ge(sig_ready, i * STRIPS + s + 1)
                    dve.scalar_tensor_tensor(out=Gp[:, 1 + s * WIN:1 + (s + 1) * WIN, 1:1 + W],
                                             in0=rows16(ps[0:R, 0:SPX]), scalar=v("bw1a"),
                                             in1=rows16(SG[s % 2]), op0=ALU.add, op1=ALU.mult)\
                       .then_inc(free(job), 1)

            def conv_part(i, no, d, part, src, dst, first):
                for k in range(3 * part, 3 * part + 3):
                    tap = TAPS[k]
                    win = shifted(src, d * CROWS, CROWS, tap)
                    wt = v(f"{CONVS[no]}{tap}")
                    if k == 0:
                        first(win, wt).then_inc(conv_step, 1)
                    else:
                        dve.wait_ge(conv_step, conv_at(i, no, d, k - 1))
                        dve.scalar_tensor_tensor(out=rows16(dst), in0=win, scalar=wt, in1=rows16(dst),
                                                 op0=ALU.mult, op1=ALU.add).then_inc(conv_step, 1)

            def with_bias(dst, b):
                return lambda win, wt: dve.tensor_scalar(rows16(dst), win, wt, v(b), ALU.mult, ALU.add)

            def main(i, name, d):
                job = (name, d)
                if name[:2] == "c0":
                    part = int(name[3])
                    if part == 0:
                        if d == 0:
                            dve.wait_ge(out_stored, i * (16 * CH) + 16)
                        dve.wait_ge(zp_ready, i * CH + halo_last(d) + 1)
                    conv_part(i, 0, d, part, ZP, chunk(X3, d), with_bias(chunk(X3, d), "cpe1_b"))
                elif name in ("yn", "yn2"):
                    dve.wait_ge(exp2_ready, i * (3 * CH) + (2 * CH if name == "yn2" else 0) + d + 1)
                    dve.tensor_tensor(chunk(XC, d), chunk(XC, d), chunk(LV, d), ALU.mult).then_inc(yn_ready, 1)
                elif name[:2] == "c1":
                    part = int(name[3])
                    if part == 0:
                        wait_read(dve, i, ("ip", halo_last(d)))
                    conv_part(i, 1, d, part, ZP, T0[d], with_bias(T0[d], "dwc_b"))
                elif name == "kt":
                    wait_filled(dve, i, job)
                    dve.tensor_tensor(KK[d % 2].rearrange("p (t c) -> p t c", c=R),
                                      slot(job)[0:TT, :].rearrange("p (t c) -> p t c", c=128)[:, :, 0:R],
                                      bc_mid(kbrow_sb[:, :], CT_), ALU.add).then_inc(free(job), 2)
                elif name == "q":
                    dve.wait_ge(kexp_ready, i * CH + d + 1)
                    dve.scalar_tensor_tensor(out=KK[d % 2], in0=KM[d % 2], scalar=1.0, in1=KK[d % 2],
                                             op0=ALU.min, op1=ALU.add).then_inc(k_ready, 1)
                    wait_read(dve, i, job)
                    dve.scalar_tensor_tensor(out=chunk(Q, d), in0=QE[d % 2], scalar=1.0, in1=chunk(Q, d),
                                             op0=ALU.min, op1=ALU.add).then_inc(q_ready, 1)
                elif name == "kv":
                    wait_filled(dve, i, job)
                    halves = ((kv_sum[:, 0:R + 2], slot(job)[0:R, 0:R + 2]),
                              (kv_sum[:, R + 2:2 * R + 2], slot(job)[0:R, BANK:BANK + R]))
                    if d > 0:
                        wait_read(dve, i, ("kv", d - 1))
                    for dst, src in halves:
                        if d == 0:
                            dve.tensor_copy(dst, src).then_inc(free(job), 1)
                        else:
                            dve.tensor_tensor(dst, src, dst, ALU.add).then_inc(free(job), 1)
                    if d == CH - 1:
                        wait_read(dve, i, job)
                        dve.tensor_scalar(km_sb[:, :], cn("headmask"), kv_sum[:, R:R + 1], 1.0 / PX,
                                          ALU.mult, ALU.mult).then_inc(km_ready, 1)
                elif name == "kp":
                    wait_filled(dve, i, job)
                    dve.scalar_tensor_tensor(out=kv_sb[:, :], in0=slot(job)[0:R, 0:R], scalar=1.0 / PX,
                                             in1=cn("headmask"), op0=ALU.mult, op1=ALU.mult).then_inc(free(job), 2)
                elif name == "kk":
                    wait_filled(dve, i, job)
                    dve.tensor_copy(kv2_sb[:, :], slot(job)[0:R, 0:R]).then_inc(free(job), 2)
                elif name == "at":
                    dve.wait_ge(exp2_ready, i * (3 * CH) + CH + d + 1)
                    wait_filled(dve, i, job)
                    dve.tensor_tensor(pairs(AZ[d % 2]), two(job), pairs(chunk(LV, d)), ALU.mult)\
                       .then_inc(free(job), 2)
                elif name == "am":
                    wait_read(dve, i, ("at", d))
                    wait_conv(dve, i, 2, d)
                    dve.tensor_tensor(CT[d % 2][:, :], CT[d % 2][:, :], AZ[d % 2], ALU.add).then_inc(am_ready, 1)
                elif name[:2] == "c2":
                    part = int(name[3])
                    ct = CT[d % 2][:, :]
                    if part == 0:
                        dve.wait_ge(t_ready, i * CH + halo_last(d) + 1)
                    conv_part(i, 2, d, part, TP, ct, with_bias(ct, "lepe_b"))
                elif name == "op":
                    wait_filled(dve, i, job)
                    for b in range(2):
                        y = 1 + d * CROWS + b * WIN
                        px = slice(d * CPX + b * SPX, d * CPX + (b + 1) * SPX)
                        dve.scalar_tensor_tensor(out=ZP[:, y:y + WIN, 1:1 + W],
                                                 in0=rows16(slot(job)[0:R, b * BANK:b * BANK + SPX]),
                                                 scalar=v("out_b"), in1=rows16(X3[:, px]),
                                                 op0=ALU.add, op1=ALU.add).then_inc(free(job), 1)
                elif name[:2] == "c3":
                    part = int(name[3])
                    if part == 0:
                        wait_read(dve, i, ("op", halo_last(d)))
                    conv_part(i, 3, d, part, ZP, chunk(X3, d), with_bias(chunk(X3, d), "cpe2_b"))
                elif name == "f2":
                    wait_filled(dve, i, job)
                    dve.scalar_tensor_tensor(out=pairs(chunk(X3, d)), in0=two(job), scalar=v("fc2_b"),
                                             in1=pairs(chunk(X3, d)), op0=ALU.add, op1=ALU.add)\
                       .then_inc(free(job), 2)

            part_of_program("first")
            for name, n in ATT:
                attention(0, name, n)
                if (name, n) == SETUP_AFTER:
                    setup_rest()
            part_of_program("loop")
            with dve.Fori(0, PAIRS - 1) as i:
                for of_next, (name, n) in MERGED:
                    attention(i + 1, name, n) if of_next else main(i, name, n)
            part_of_program("last")
            for name, n in MAIN:
                main(PAIRS - 1, name, n)

        @block.gpsimd
        def _(pool):
            pool.memset(ZP[:, :, :], 0.0).then_inc(zeroed, 1)
            pool.memset(TP[:, :, :], 0.0).then_inc(zeroed, 1)
            for j in range(2):
                pool.memset(vx[j][:, :], 0.0).then_inc(zeroed, 1)
            pool.wait_ge(zeroed, 4)
            for j in range(2):
                for hh in range(2):
                    dst = vx[j][64 * hh:64 * hh + 64, :].rearrange("p (w u e) -> p w u e", u=2, e=VCOL)
                    pool.memset(dst[:, :, hh, D0:VCOL], 1.0).then_inc(zeroed, 1)
            pool.wait_ge(zeroed, 8)

            def attention(i, name, s):
                if name in ("sc0", "sc1"):
                    n = 2 * s + int(name[2])
                    sc = SC[n % NSC].rearrange("p (j m) -> p j m", m=TOK)
                    pool.wait_ge(max_ready, i * (2 * STRIPS) + n + 1)
                    pool.tensor_tensor(sc, sc, bc_last(mx[:, (n % NSC) * 12:(n % NSC) * 12 + 12], TOK),
                                       ALU.subtract).then_inc(sub_ready, 1)

                elif name == "cv":
                    pool.wait_ge(leaky_ready, i * CH + s + 1)
                    pool.tensor_tensor(chunk(X1, s), chunk(X1, s), YB[s % 2], ALU.add).then_inc(x2_ready, 1)

            def k_rope(i, d):
                pool.wait_ge(k_ready, i * CH + d + 1)
                half = C // 2
                k4 = KK[d % 2].rearrange("p (t b u c) -> p t b u c", t=CT_, b=2, u=2)
                for n, dst in enumerate((KC, KS)):
                    o4 = dst[d % 2].rearrange("p (t b u c) -> p t b u c", t=CT_, b=2, u=2)
                    th = rope_th_sb[:, n * TILES * half:(n + 1) * TILES * half]
                    th = th.rearrange("p (t c) -> p t c", c=half)[:, d * CT_:(d + 1) * CT_, :]
                    tw = rope_tw_sb[:, n * half:(n + 1) * half]
                    pool.tensor_tensor(o4[:, :, :, 0, :], k4[:, :, :, 0, :],
                                       th.unsqueeze(2).broadcast_to([TT, CT_, 2, half]), ALU.mult)\
                        .then_inc(kcs_ready, 1)
                    pool.tensor_tensor(o4[:, :, :, 1, :], k4[:, :, :, 1, :],
                                       tw.unsqueeze(1).unsqueeze(1).broadcast_to([TT, CT_, 2, half]), ALU.mult)\
                        .then_inc(kcs_ready, 1)

            def q_rope(i, d, n):
                rows = rows16(chunk(Q, d))
                dst = rows16(chunk(QS, d)) if n == 1 else rows
                ty = rope_y_sb[:, n * H + d * CROWS:n * H + (d + 1) * CROWS]
                tx = rope_x_sb[:, n * W:(n + 1) * W]
                pool.tensor_tensor(dst, rows, bc_last(ty, W), ALU.mult).then_inc(qhalf_ready, 1)
                pool.wait_ge(qhalf_ready, i * (2 * CH) + (1 - n) * CH + d + 1)
                pool.tensor_tensor(dst, dst, bc_mid(tx, CROWS), ALU.mult).then_inc(qcs_ready, 1)

            def main(i, name, d):
                if name == "q":
                    k_rope(i, d)
                    pool.wait_ge(q_ready, i * CH + d + 1)
                    q_rope(i, d, 1)
                elif name == "dn":
                    wait_filled(pool, i, ("dn", d))
                    q_rope(i, d, 0)
                elif name == "am":
                    pool.wait_ge(am_ready, i * CH + d + 1)
                    pool.tensor_tensor(CT[d % 2][:, :], CT[d % 2][:, :], chunk(AR, d), ALU.mult)\
                        .then_inc(ym_ready, 1)

            part_of_program("first")
            for name, n in ATT:
                attention(0, name, n)
            pool.wait_ge(loaded_b, N_LOADS_B * 16)
            part_of_program("loop")
            with pool.Fori(0, PAIRS - 1) as i:
                for of_next, (name, n) in MERGED:
                    attention(i + 1, name, n) if of_next else main(i, name, n)
            part_of_program("last")
            for name, n in MAIN:
                main(PAIRS - 1, name, n)


def _block_diagonal(np_, a, b):
    z = np_.zeros_like(a)
    return np_.concatenate([np_.concatenate([a, z], 1), np_.concatenate([z, b], 1)], 0)


def layout(p):
    f = np.float32
    bd = lambda w: _block_diagonal(np, w.T, w.T)
    qkv = p["L0_conv_qkv_w"]
    w1 = p["L0_conv_w1_w"]
    lqk = p["L1_conv_qk_w"]
    vcols = np.zeros((R, R), f)
    for hh in range(2):
        for hp in range(2):
            for b in range(2):
                h = 2 * hp + hh
                col = ((hh * 2 + hp) * 2 + b) * D0
                vcols[b * C:(b + 1) * C, col:col + D0] = qkv[2 * C + h * D0:2 * C + (h + 1) * D0].T
    sq = {"q": bd(qkv[0:C]), "k": bd(qkv[C:2 * C]), "v": vcols, "w1a": bd(w1[0:C]), "w1b": bd(w1[C:2 * C]),
          "act": bd(p["L1_conv_act_proj_w"]), "inp": bd(p["L1_conv_in_proj_w"]), "lq": bd(lqk[0:C]),
          "lk": bd(lqk[C:2 * C]), "out": bd(p["L1_conv_out_proj_w"])}
    wsq = np.concatenate([sq[n] for n in SQ], 1)
    pw = p["L0_conv_proj_w"].T
    z = np.zeros_like(pw)
    zz = np.concatenate([z, z], 1)
    wproj = np.concatenate([np.concatenate([pw, z, z, pw, zz, zz], 1), np.concatenate([zz, zz, pw, z, z, pw], 1)], 0)
    w2 = np.concatenate([bd(p["L0_conv_w2_w"][:, :, t // 3, t % 3]) for t in range(9)], 1)
    f1, f2 = p["L1_conv_fc1_w"], p["L1_conv_fc2_w"]
    g = lambda m: slice(64 * m, 64 * m + 64)
    wfc1 = np.concatenate([_block_diagonal(np, f1[g(m)].T, f1[g(m)].T) for m in range(FG)], 1)
    wfc2 = np.concatenate([_block_diagonal(np, f2[:, g(m)].T, f2[:, g(m)].T) for m in range(FG)], 1)
    b0 = p["L0_conv_qkv_b"]
    vecs = {"bq": b0[0:C], "bk": b0[C:2 * C], "bv": b0[2 * C:], "bw1a": p["L0_conv_w1_b"][0:C],
            "bw1b": p["L0_conv_w1_b"][C:], "bw2": p["L0_conv_w2_b"], "proj_b": p["L0_conv_proj_b"],
            "cpe1_b": p["L1_conv_cpe1_b"], "n1w": p["L1_conv_norm1_w"], "n1b": p["L1_conv_norm1_b"],
            "act_b": p["L1_conv_act_proj_b"], "inp_b": p["L1_conv_in_proj_b"], "dwc_b": p["L1_conv_dwc_b"],
            "lq_b": p["L1_conv_qk_b"][0:C], "lepe_b": p["L1_conv_lepe_b"], "out_b": p["L1_conv_out_proj_b"],
            "cpe2_b": p["L1_conv_cpe2_b"], "n2w": p["L1_conv_norm2_w"], "n2b": p["L1_conv_norm2_b"],
            "fc2_b": p["L1_conv_fc2_b"]}
    for n in CONVS:
        w = p[f"L1_conv_{n}w"].reshape(C, 9)
        for t in range(9):
            vecs[f"{n}{t}"] = w[:, t]
    vec = np.stack([np.concatenate([vecs[n], vecs[n]]) for n in VEC], 1)
    fb = p["L1_conv_fc1_b"]
    fc1b = np.stack([np.concatenate([fb[g(m)], fb[g(m)]]) for m in range(FG)], 1)
    kb = p["L1_conv_qk_b"][C:]
    kbrow = np.broadcast_to(np.concatenate([kb, kb])[None], (TT, R))
    yy, xx = np.meshgrid(np.arange(WIN), np.arange(WIN), indexing="ij")
    co = np.stack([yy.reshape(-1), xx.reshape(-1)])
    rel = co[:, :, None] - co[:, None, :] + WIN - 1
    bias = p["L0_conv_bias_table"][rel[0] * (2 * WIN - 1) + rel[1]]
    bias = np.concatenate([bias, bias], 0)
    return {"wsq": wsq, "wproj": wproj, "w2": w2, "wfc1": wfc1, "wfc2": wfc2, "vec": vec, "fc1b": fc1b,
            "kbrow": kbrow, "bias": bias}


def constants():
    f = np.float32
    blk = np.kron(np.eye(2), np.ones((C, C)))
    swap = np.zeros((R, R))
    for j in range(0, R, 2):
        swap[j, j + 1], swap[j + 1, j] = -1, 1
    cn = {"center": np.eye(R) - blk / C, "mean": blk / C, "swap": swap, "swapT": swap.T,
          "headmask": np.kron(np.eye(R // D1), np.ones((D1, D1)))}
    const = np.concatenate([cn[n] for n in CN], 1).astype(f)
    masks = np.zeros((128, 2 + HEADS0 + 4), f)
    for b in range(2):
        masks[b * C:(b + 1) * C, b] = 1.0 / np.sqrt(D0)
    for h in range(HEADS0):
        masks[0:R, 2 + h] = (np.arange(R) % C) // D0 == h
    masks[:, 2 + HEADS0:4 + HEADS0] = 1.0
    masks[W:W + 2, 2 + HEADS0:4 + HEADS0] = 0.0
    masks[:, 4 + HEADS0] = 1e-5
    masks[:, 5 + HEADS0] = 1e-6
    kmax = C // 4
    theta = 1.0 / 10000.0 ** (np.arange(kmax) / kmax)
    hi = np.broadcast_to(np.arange(H)[:, None, None] * theta, (H, W, kmax))
    wi = np.broadcast_to(np.arange(W)[None, :, None] * theta, (H, W, kmax))
    ang = np.repeat(np.concatenate([hi, wi], -1).reshape(PX, C // 2), 2, axis=1)
    cs = np.stack([np.cos(ang), np.sin(ang)]).astype(f)
    two = lambda t: np.concatenate([t, t], 1)
    first = np.arange(C) < C // 2
    py, px = cs.reshape(2, H, W, C)[:, :, 0], cs.reshape(2, H, W, C)[:, 0]
    rope_y = np.concatenate([two(np.where(first, t, 1)).T for t in py], 1).astype(f)
    rope_x = np.concatenate([two(np.where(first, 1, t)).T for t in px], 1).astype(f)
    gap = lambda a: np.concatenate([a[:, :, 0:W], np.zeros_like(a[:, :, 0:2]), a[:, :, W:]], 2)
    tok = gap(cs.reshape(2, TILES, 2 * W, C)).transpose(2, 0, 1, 3)
    th = tok[:, :, :, 0:C // 2].reshape(TT, -1)
    tw = tok[:, :, 0, C // 2:].reshape(TT, -1)
    return {"const": const, "ident": np.eye(128, dtype=f), "masks": masks, "rope_y": rope_y,
            "rope_x": rope_x, "rope_th": th,
            "rope_tw": tw}


_INS = ["x", "wsq", "wproj", "w2", "wfc1", "wfc2", "vec", "fc1b", "kbrow", "bias", "const", "ident", "masks",
        "rope_y", "rope_x", "rope_th", "rope_tw"]


def kernel(**inputs):
    import numpy as _np
    import concourse.bacc as _bacc
    from concourse import mybir as _mybir
    from concourse.bass_utils import run_bass_kernel_spmd as _run

    data = {n: _np.asarray(a) for n, a in inputs.items()}
    placed = {"x": data["x"], **layout(data), **constants()}
    nc = _bacc.Bacc("TRN2", target_bir_lowering=False, num_devices=1)
    arrays, args = {}, []
    for name in _INS:
        a = _np.ascontiguousarray(placed[name])
        arrays[f"in_{name}_dram"] = a
        args.append(nc.dram_tensor(f"in_{name}_dram", a.shape, _mybir.dt.from_np(a.dtype), kind="ExternalInput").ap())
    out = nc.dram_tensor("out_0_dram", (B, C, H, W), _mybir.dt.float32, kind="ExternalOutput").ap()
    build(nc, *args, out)
    r = _run(nc, [arrays], core_ids=[0])
    return r.results[0]["out_0_dram"]
```
